# Optimizing a Trainium2 kernel written in Bass

```python
import numpy as np
import jax
import jax.numpy as jnp

def _softmax(x, axis=-1):
    return jax.nn.softmax(x, axis=axis)

def _gelu(x):
    return jax.nn.gelu(x, approximate=True)

def _silu(x):
    return jax.nn.silu(x)

def _sigmoid(x):
    return jax.nn.sigmoid(x)

def _layernorm(x, axis=-1, eps=1e-05):
    m = jnp.mean(x, axis=axis, keepdims=True)
    v = jnp.var(x, axis=axis, keepdims=True)
    return (x - m) / jnp.sqrt(v + eps)

def _scatter_add(tgt, idx, src, axis=0):
    return tgt.at[idx].add(src)

def _segment_sum(src, seg, n):
    return jax.ops.segment_sum(src, seg, n)
kernel_name = 'mk_decoder_postln_d1_seqx_r4_d2bd4b'

def setup_inputs(seed: int=0):
    np.random.seed(seed)
    _w = jnp.asarray

    def _rec_inputs():
        import jax
        import jax.numpy as jnp
        _rk = jax.random.key(seed)
        x = 7.22e-05 + 1 * jax.random.normal(jax.random.fold_in(_rk, 1), (4, 1024, 256), jnp.float32)
        _lenS = 1024 - jax.random.randint(jax.random.fold_in(_rk, 7), (4,), 0, max(1, 1024 // 4) + 1, jnp.int32)
        _lenS2 = 154 - jax.random.randint(jax.random.fold_in(_rk, 8), (4,), 0, max(1, 154 // 4) + 1, jnp.int32)
        _ctx_1024P = jax.random.normal(jax.random.fold_in(_rk, 11), (4, 16, 256), jnp.float32)
        _ctx_1024c = jax.random.dirichlet(jax.random.fold_in(_rk, 511), 0.3 * jnp.ones((16,), jnp.float32), (4, 154))
        _ctx_1024t = jnp.einsum('bsk,bkd->bsd', _ctx_1024c, _ctx_1024P)
        _ctx_1024t = _ctx_1024t * jax.lax.rsqrt(jnp.mean(jnp.square(_ctx_1024t)) + 1e-12) * 0.953939
        ctx_1024 = 4.13588e-05 + 0.999923 * (_ctx_1024t + 0.3 * jax.random.normal(jax.random.fold_in(_rk, 611), (4, 154, 256), jnp.float32))
        return (x, ctx_1024)
    x, ctx_1024 = _rec_inputs()

    def _L0_attn_setup():
        import jax, jax.numpy as jnp
        import numpy as np
        HIDDEN = 256
        NUM_HEADS = 16
        HEAD = HIDDEN // NUM_HEADS
        LEFT = 64
        RIGHT = 8
        NUM_POS = LEFT + RIGHT + 1
        key = jax.random.key(seed)
        ks = jax.random.split(key, 10)
        s = 1.0 / np.sqrt(HIDDEN)
        return {'hidden_states': jax.random.normal(ks[0], (4, 512, HIDDEN), jnp.float32), 'Wq': jax.random.normal(ks[1], (HIDDEN, HIDDEN), jnp.float32) * s, 'bq': jax.random.normal(ks[2], (HIDDEN,), jnp.float32) * 0.01, 'Wk': jax.random.normal(ks[3], (HIDDEN, HIDDEN), jnp.float32) * s, 'bk': jax.random.normal(ks[4], (HIDDEN,), jnp.float32) * 0.01, 'Wv': jax.random.normal(ks[5], (HIDDEN, HIDDEN), jnp.float32) * s, 'bv': jax.random.normal(ks[6], (HIDDEN,), jnp.float32) * 0.01, 'Wo': jax.random.normal(ks[7], (HIDDEN, HIDDEN), jnp.float32) * s, 'bo': jax.random.normal(ks[8], (HIDDEN,), jnp.float32) * 0.01, 'dist_emb': jax.random.normal(ks[9], (NUM_POS, HEAD), jnp.float32)}
    _L0_attn_all = _L0_attn_setup()
    _L0_attn_in = {k: v for k, v in _L0_attn_all.items() if k in ('Wq', 'bq', 'Wk', 'bk', 'Wv', 'bv', 'Wo', 'bo', 'dist_emb')}
    del _L0_attn_all

    def _L0_xattn_setup():
        import jax, jax.numpy as jnp
        import numpy as np
        B, SQ, SK, D = (4, 512, 512, 256)
        key = jax.random.key(seed)
        ks = jax.random.split(key, 8)
        s = 1.0 / np.sqrt(D)
        return {'input_seq': jax.random.normal(ks[0], (B, SQ, D), jnp.float32), 'condition_seq': jax.random.normal(ks[1], (B, SK, D), jnp.float32), 'Wq': jax.random.normal(ks[2], (D, D), jnp.float32) * s, 'bq': jnp.zeros((D,), jnp.float32), 'Wk': jax.random.normal(ks[3], (D, D), jnp.float32) * s, 'bk': jnp.zeros((D,), jnp.float32), 'Wv': jax.random.normal(ks[4], (D, D), jnp.float32) * s, 'bv': jnp.zeros((D,), jnp.float32)}
    _L0_xattn_all = _L0_xattn_setup()
    _L0_xattn_in = {k: v for k, v in _L0_xattn_all.items() if k in ('Wq', 'bq', 'Wk', 'bk', 'Wv', 'bv')}
    del _L0_xattn_all

    def _L0_ffn_setup():
        import jax, jax.numpy as jnp
        import numpy as np
        BLOCK = 32
        W_BITS = 4
        ACT_BITS = 16

        def act_qdq(x):
            qmax = 2.0 ** (ACT_BITS - 1) - 1.0
            scale = jnp.maximum(jnp.max(jnp.abs(x)) / qmax, 1e-12)
            return jnp.clip(jnp.round(x / scale), -qmax - 1.0, qmax) * scale

        def fixed_qdq_u16(x):
            scale = 1.0 / 65536.0
            return jnp.clip(jnp.round(x / scale), 0.0, 65535.0) * scale

        def lpbq_dequant(w):
            O, I = w.shape
            qmax = 2.0 ** (W_BITS - 1) - 1.0
            wb = w.reshape(O, I // BLOCK, BLOCK)
            s = jnp.maximum(jnp.max(jnp.abs(wb), axis=-1, keepdims=True) / qmax, 1e-12)
            wq = jnp.clip(jnp.round(wb / s), -qmax - 1.0, qmax) * s
            return wq.reshape(O, I)
        key = jax.random.key(seed)
        k1, k2, k3, k4 = jax.random.split(key, 4)
        B, S, H, I = (2, 1024, 256, 768)
        x = jax.random.normal(k1, (B, S, H), jnp.float32)
        w_gate = jax.random.normal(k2, (I, H), jnp.float32) * 0.02
        w_up = jax.random.normal(k3, (I, H), jnp.float32) * 0.02
        w_down = jax.random.normal(k4, (H, I), jnp.float32) * 0.02
        return {'x': x, 'w_gate': w_gate, 'w_up': w_up, 'w_down': w_down}
    _L0_ffn_all = _L0_ffn_setup()
    _L0_ffn_in = {k: v for k, v in _L0_ffn_all.items() if k in ('w_gate', 'w_up', 'w_down')}
    del _L0_ffn_all
    return {'x': x, 'ctx_1024': ctx_1024, 'L0_attn_Wq': _L0_attn_in['Wq'], 'L0_attn_bq': _L0_attn_in['bq'], 'L0_attn_Wk': _L0_attn_in['Wk'], 'L0_attn_bk': _L0_attn_in['bk'], 'L0_attn_Wv': _L0_attn_in['Wv'], 'L0_attn_bv': _L0_attn_in['bv'], 'L0_attn_Wo': _L0_attn_in['Wo'], 'L0_attn_bo': _L0_attn_in['bo'], 'L0_attn_dist_emb': _L0_attn_in['dist_emb'], 'L0_xattn_Wq': _L0_xattn_in['Wq'], 'L0_xattn_bq': _L0_xattn_in['bq'], 'L0_xattn_Wk': _L0_xattn_in['Wk'], 'L0_xattn_bk': _L0_xattn_in['bk'], 'L0_xattn_Wv': _L0_xattn_in['Wv'], 'L0_xattn_bv': _L0_xattn_in['bv'], 'L0_ffn_w_gate': _L0_ffn_in['w_gate'], 'L0_ffn_w_up': _L0_ffn_in['w_up'], 'L0_ffn_w_down': _L0_ffn_in['w_down']}

def reference(x, ctx_1024, L0_attn_Wq, L0_attn_bq, L0_attn_Wk, L0_attn_bk, L0_attn_Wv, L0_attn_bv, L0_attn_Wo, L0_attn_bo, L0_attn_dist_emb, L0_xattn_Wq, L0_xattn_bq, L0_xattn_Wk, L0_xattn_bk, L0_xattn_Wv, L0_xattn_bv, L0_ffn_w_gate, L0_ffn_w_up, L0_ffn_w_down):
    import jax
    import jax.numpy as jnp

    def _L0_attn_ref(hidden_states, Wq, bq, Wk, bk, Wv, bv, Wo, bo, dist_emb):
        import jax, jax.numpy as jnp
        import numpy as np
        HIDDEN = 256
        NUM_HEADS = 16
        HEAD = HIDDEN // NUM_HEADS
        LEFT = 64
        RIGHT = 8
        NUM_POS = LEFT + RIGHT + 1
        B, L, H = hidden_states.shape
        scale = 1.0 / np.sqrt(HEAD)

        def proj(W, b):
            return (hidden_states @ W.T + b).reshape(B, L, NUM_HEADS, HEAD).transpose(0, 2, 1, 3)
        q = proj(Wq, bq)
        k = proj(Wk, bk)
        v = proj(Wv, bv)
        attn = jnp.einsum('bhld,bhrd->bhlr', q, k) * scale
        dist = jnp.arange(L)[None, :] - jnp.arange(L)[:, None]
        dist = jnp.clip(dist, -LEFT, RIGHT) + LEFT
        pos_emb = dist_emb[dist]
        rel = jnp.einsum('bhld,lrd->bhlr', q, pos_emb) * scale
        attn = jax.nn.softmax(attn + rel, axis=-1)
        out = jnp.einsum('bhlr,bhrd->bhld', attn, v)
        out = out.transpose(0, 2, 1, 3).reshape(B, L, H)
        return out @ Wo.T + bo

    def _L0_xattn_ref(input_seq, condition_seq, Wq, bq, Wk, bk, Wv, bv):
        import jax, jax.numpy as jnp
        import numpy as np
        B, SQ, SK, D = (4, 512, 512, 256)
        q = jnp.einsum('bsd,ed->bse', input_seq, Wq) + bq
        k = jnp.einsum('btd,ed->bte', condition_seq, Wk) + bk
        v = jnp.einsum('btd,ed->bte', condition_seq, Wv) + bv
        scores = jnp.einsum('bse,bte->bst', q, k)
        attn = jax.nn.softmax(scores, axis=-1)
        attended = jnp.einsum('bst,bte->bse', attn, v)
        return attended

    def _L0_ffn_ref(x, w_gate, w_up, w_down):
        import jax, jax.numpy as jnp
        import numpy as np
        BLOCK = 32
        W_BITS = 4
        ACT_BITS = 16

        def act_qdq(x):
            qmax = 2.0 ** (ACT_BITS - 1) - 1.0
            scale = jnp.maximum(jnp.max(jnp.abs(x)) / qmax, 1e-12)
            return jnp.clip(jnp.round(x / scale), -qmax - 1.0, qmax) * scale

        def fixed_qdq_u16(x):
            scale = 1.0 / 65536.0
            return jnp.clip(jnp.round(x / scale), 0.0, 65535.0) * scale

        def lpbq_dequant(w):
            O, I = w.shape
            qmax = 2.0 ** (W_BITS - 1) - 1.0
            wb = w.reshape(O, I // BLOCK, BLOCK)
            s = jnp.maximum(jnp.max(jnp.abs(wb), axis=-1, keepdims=True) / qmax, 1e-12)
            wq = jnp.clip(jnp.round(wb / s), -qmax - 1.0, qmax) * s
            return wq.reshape(O, I)
        x = act_qdq(x)
        up = act_qdq(x @ lpbq_dequant(w_up).T)
        gate = act_qdq(x @ lpbq_dequant(w_gate).T)
        sig = fixed_qdq_u16(jax.nn.sigmoid(gate))
        gate = act_qdq(gate * sig)
        o = act_qdq(gate * up)
        return o @ lpbq_dequant(w_down).T
    x = _layernorm(x + _L0_attn_ref(x, L0_attn_Wq, L0_attn_bq, L0_attn_Wk, L0_attn_bk, L0_attn_Wv, L0_attn_bv, L0_attn_Wo, L0_attn_bo, L0_attn_dist_emb), axis=-1)
    x = _layernorm(x + _L0_xattn_ref(x, ctx_1024, L0_xattn_Wq, L0_xattn_bq, L0_xattn_Wk, L0_xattn_bk, L0_xattn_Wv, L0_xattn_bv), axis=-1)
    x = _layernorm(x + _L0_ffn_ref(x, L0_ffn_w_gate, L0_ffn_w_up, L0_ffn_w_down), axis=-1)
    return x

_drawn_inputs = setup_inputs


def setup_inputs(seed=0):
    import zlib

    import numpy as np

    out = dict(_drawn_inputs(seed))
    spreads = {'L0_xattn_bq': (0.0, 0.1), 'L0_xattn_bk': (0.0, 0.8), 'L0_xattn_bv': (0.0, 0.1)}
    factors = {'L0_attn_bq': 8.0, 'L0_attn_bk': 8.0, 'L0_attn_bo': 2.683}
    for name, (base, spread) in spreads.items():
        noise = np.random.default_rng([zlib.crc32(name.encode()), seed]).standard_normal(out[name].shape)
        drawn = base * np.exp(spread * noise) if base else spread * noise
        out[name] = jnp.asarray(drawn.astype(out[name].dtype))
    for name, factor in factors.items():
        out[name] = (out[name] * factor).astype(out[name].dtype)
    return out
```

```python
import concourse.bass as bass
from concourse import mybir
from contextlib import ExitStack

F32 = mybir.dt.float32
BF16 = mybir.dt.bfloat16
ALU = mybir.AluOpType
ACT = mybir.ActivationFunctionType
AX = mybir.AxisListType

P = 128
B, L, D = 4, 1024, 256
N = B * L
NH, HD = 16, 16
LEFT, RIGHT = 64, 8
NJ = LEFT + RIGHT
G = 4
NIT = B * NH // G
HALF = 512
TL = L // P
PADL = P
TW = PADL + NJ + P
WIN = LEFT + P + RIGHT
ZL = LEFT
STEPS = 32
KR = 6 * HD
NP_BUF = 4
LC = 154
FI = 768
FT = FI // P
NBLK = N // HALF
NSC = 5
EPS = 1e-5
QMAX = 32767.0
U16 = 65536.0
TINY = 1e-12
MAGIC = 1.5 * 2.0 ** 23
RMAX = bass.bass_isa.ReduceOp.max
NR = 4



def self_attention(nc, sem, ad, xT, wqT, wkT, wvT, bq, bk, bv, emb, part_of_row, e_lo, e_hi, ident):
    ctx = ExitStack()
    with ctx:
        def sb(name, shape, dt=F32):
            return ctx.enter_context(nc.sbuf_tensor(name, shape, dt))

        def dram(name, shape, dt=F32):
            return nc.dram_tensor(name, shape, dt, kind="Internal").ap()

        td = [dram(n, [NIT, G * 3 * HD, L], BF16) for n in ("q_parts", "k_lo_parts", "k_hi_parts", "k_mixed_parts")]
        vd = dram("v_all", [NIT, L, P])
        tab = dram("rel_table", [2, G, L, TW])

        psT = ctx.enter_context(nc.psum_tensor("scoresT", [P, 4, HALF], F32))
        psX = ctx.enter_context(nc.psum_tensor("scores_for_max", [P, 2, HALF], F32))
        psO = ctx.enter_context(nc.psum_tensor("attn_out", [P, HALF], F32))
        psM = ctx.enter_context(nc.psum_tensor("misc", [P, HALF], F32))

        idf = sb("idf", [P, P])
        idb = sb("idb", [P, P], BF16)
        embr = sb("embr", [KR, NJ + 1])
        prow = sb("prow", [KR, 3])
        embd = sb("embd", [KR, NJ])
        embt = sb("embt", [KR, 3, NJ])
        embp = sb("embp", [KR, 3, NJ], BF16)
        embS = sb("embS", [KR, NJ], BF16)
        colb = sb("colb", [P, 6])
        colc = sb("colc", [P, 6])

        s_const = sem("s_const")
        s_w = sem("s_w")
        s_pads = sem("s_pads")
        s_zero = sem("s_zero")
        s_prep = sem("s_prep")
        s_ones = sem("s_ones")
        s_bufs = sem("s_bufs")
        a_x = [sem(f"a_x{j}") for j in range(2)]
        a_full = sem("a_full")
        a_val = sem("a_val")
        a_hi_val = sem("a_hi_val")
        a_high = sem("a_high")
        a_rem = sem("a_rem")
        a_mid = sem("a_mid")
        a_low = sem("a_low")
        a_v = sem("a_v")
        a_mix = sem("a_mix")
        a_out = [sem(f"a_out{j}") for j in range(2)]
        ld_q = [sem(f"ld_q{i}") for i in range(2)]
        ld_k = [sem(f"ld_k{i}") for i in range(2)]
        ld_lo = [sem(f"ld_lo{i}") for i in range(2)]
        ld_hi = [sem(f"ld_hi{i}") for i in range(2)]
        ld_r = [sem(f"ld_r{i}") for i in range(2)]
        t_wr = [sem(f"t_wr{i}") for i in range(NR)]
        st_done = sem("st_done")
        exp_done = sem("exp_done")
        pv_done = sem("pv_done")
        mx_full = sem("mx_full")
        mx_free = sem("mx_free")
        m_ready = sem("m_ready")
        m_turned = sem("m_turned")
        qm_ready = sem("qm_ready")
        r_full = sem("r_full")
        r_rows = sem("r_rows")
        r_padded = sem("r_padded")
        wb_ready = sem("wb_ready")
        o_copied = sem("o_copied")
        o_turned = sem("o_turned")
        o_rec = sem("o_rec")
        m_small = sem("m_small")
        an_ready = sem("an_ready")
        an_out = sem("an_out")
        s_held = sem("s_held")
        s_dve = sem("s_dve")

        with ExitStack() as early:
            def sbe(name, shape, dt=F32):
                return early.enter_context(nc.sbuf_tensor(name, shape, dt))
            zero = sbe("zero", [P, TL * P])
            wq = sbe("wq", [P, 2, D])
            wk = sbe("wk", [P, 2, D])
            wv = sbe("wv", [P, 2, D])
            bvt = sbe("bvt", [P, D])
            xs = sbe("xs", [P, 2, 2, HALF])
            val = sbe("val", [P, 2, 6, HALF])
            rem = sbe("rem", [P, 2, 6, HALF])
            part = sbe("part", [P, 2, 8, 3, HALF], BF16)
            vs = sbe("vs", [P, 2, 4, NH, 32])

        qT = sb("qT", [P, 2, G, L], BF16)
        qR = sb("qR", [P, 2, G, L], BF16)
        kT = sb("kT", [P, 2, 3, G, L], BF16)
        vS = sb("vS", [P, 2, TL, P])
        win = sb("win", [P, 2, TL, G, ZL + WIN])
        winb = sb("winb", [P, 2, TL // 2, G, WIN], BF16)
        rows = sb("rows", [P, NR, G, PADL + NJ])
        pr = sb("pr", [P, NP_BUF, 2 * HALF])
        nmax = sb("nmax", [P, 2, 4, 2, G])
        mval = sb("mval", [P, G])
        mcol = sb("mcol", [P, G, 32], BF16)
        ot = sb("ot", [P, HALF])
        orec = sb("orec", [P, 16])
        an = sb("an", [P, 4, G * HD])

        block = ctx.enter_context(nc.Block())
        NCONST = 8
        NPADS = 2 * G
        A_DMAS = 16 + 4
        LQ, LK, LW = 3, 10, 4

        def row(t, i):
            return t[bass.ds(i, 1)].rearrange("a p n -> (a p) n")

        def pieces(cuts, hf):
            lo, hi = hf * HALF, (hf + 1) * HALF
            return [(max(a, lo), min(b, hi), v) for a, b, v in cuts if max(a, lo) < min(b, hi)]

        def by_query(kt, hf):
            return pieces([(0, (kt + 1) * P, 1), ((kt + 1) * P, (kt + 2) * P, 2), ((kt + 2) * P, L, 0)], hf)

        def by_key(qt, hf):
            return pieces([(0, (qt - 1) * P, 0), ((qt - 1) * P, qt * P, 2), (qt * P, L, 1)], hf)

        R_STEPS = {1: 0, 5: 1, 9: 2, 13: 3}
        M_STEPS = {2: 0, 6: 1, 10: 2, 14: 3}
        N_STEP = 4
        LEAD = 6
        T_CH = 32

        def chunks_at(t):
            return [((LEAD + 2 * t + e) // T_CH, (LEAD + 2 * t + e) % T_CH) for e in range(2)]

        def run_blocks(eng, block_of):
            block_of(0, 0, False, False)
            block_of(0, 1, True, False)
            with eng.Fori(1, B) as b:
                block_of(b, 0, True, True)
                block_of(b, 1, True, True)

        def hold(eng, s, value):
            eng.wait_ge(s, value)
            eng.sem_inc(s_held, 1)

        def run_groups(eng, group):
            group(0, 0, 0, first=True)
            with eng.Fori(0, 6) as j:
                group(1 + 2 * j, 1, j)
                group(2 + 2 * j, 0, j + 1)
            group(13, 1, 6, ahead=False)
            group(14, 0, 7, rel=False, ahead=False)
            group(15, 1, 7, rel=False, last=True, ahead=False)

        @block.sync
        def _(sp):
            def load_x(b, hf, again=True):
                k = 2 * b + hf
                if again:
                    hold(sp, a_full, 6 * (k - 1))
                sp.dma_start(xs[:, hf], xT[:, bass.ds(k * HALF, HALF)].rearrange("(c p) n -> p c n", p=P)).then_inc(a_x[hf], 16)

            load_x(0, 0, False)
            for dst, src in ((wq, wqT.rearrange("(c p) n -> p c n", p=P)),
                             (wk, wkT.rearrange("(c p) n -> p c n", p=P)),
                             (wv, wvT.rearrange("(c p) n -> p c n", p=P))):
                sp.dma_start(dst[:], src).then_inc(s_w, 16)
            for dst, src in ((idf, ident), (prow, part_of_row), (embr, emb), (colb[:, 0:2], bq), (colb[:, 2:4], bk),
                             (colb[:, 4:5], e_lo), (colb[:, 5:6], e_hi), (bvt, bv)):
                sp.dma_start(dst[:], src).then_inc(s_const, 16)
            sp.wait_ge(s_zero, 1)
            for p in range(2):
                for h in range(G):
                    sp.dma_start(tab[p, h].rearrange("(t p) n -> p t n", p=P)[:, :, PADL + NJ:TW],
                                 zero[:, :].rearrange("p (t n) -> p t n", n=P)).then_inc(s_pads, 16)

            def store_values(b, hf):
                k = 2 * b + hf
                hold(sp, a_v, 2 * k + 2)
                for g in range(4):
                    dst = vd[bass.ds(4 * b + g, 1), hf * HALF:(hf + 1) * HALF, :].rearrange("i (t p) n -> (i p) t n", p=P)
                    sp.dma_start(dst, vs[:, hf, :, 4 * g:4 * g + 4, :].rearrange("p t h r -> p t (h r)")).then_inc(a_out[hf], 16)

            def store_parts(b, hf):
                k = 2 * b + hf
                for n in range(8):
                    if n == 6:
                        store_values(b, hf)
                    if n < 6:
                        hold(sp, a_low, 6 * k + n + 1)
                    else:
                        hold(sp, a_mix, 4 * k + 2 * (n - 6) + 2)
                    for g in range(2):
                        dst = row(td[n // 2], 4 * b + 2 * (n % 2) + g)[:, hf * HALF:(hf + 1) * HALF]
                        sp.dma_start(dst.rearrange("(t r) n -> r t n", t=3),
                                     part[g * G * HD:(g + 1) * G * HD, hf, n, :, :]).then_inc(a_out[hf], 16)
            load_x(0, 1, False)
            store_parts(0, 0)
            with sp.Fori(1, B) as b:
                load_x(b, 0)
                store_parts(b - 1, 1)
                load_x(b, 1)
                store_parts(b, 0)
            store_parts(B - 1, 1)
            for hf in range(2):
                sp.wait_ge(a_out[hf], 16 * A_DMAS * B)
            sp.wait_ge(s_pads, 16 * NPADS)

            def load_q(dst, i, s):
                t = row(td[0], i).rearrange("(r h) n -> r (h n)", h=G)
                for r0, n in ((0, 3), (3, 2), (5, 1)):
                    sp.dma_start(dst[HD * r0:HD * (r0 + n)].rearrange("p h n -> p (h n)"), t[0:HD * n]).then_inc(s, 16)

            def load_k(dst, t, i, s):
                t = row(t, i)
                for p, r0, n in ((0, 0, 3), (1, 3, 2), (2, 5, 1)):
                    src = t[p * HD * G:(p + 1) * HD * G].rearrange("(r h) n -> r (h n)", h=G)
                    sp.dma_start(dst[HD * r0:HD * (r0 + n)].rearrange("p h n -> p (h n)"),
                                 src.unsqueeze(0).to_broadcast([n, HD, G * L])).then_inc(s, 16)

            def load_rel_q(i, par):
                load_q(qR[:, par], i, ld_r[par])

            def load_qk(i, par):
                load_q(qT[:, par], i, ld_q[par])
                for v in range(3):
                    load_k(kT[:, par, v], td[1 + v], i, ld_k[par])

            def load_v(i, par):
                sp.dma_start(vS[:, par, :, :], row(vd, i).rearrange("(t p) n -> p t n", p=P)).then_inc(ld_k[par], 16)

            def load_windows(par, part):
                for h in range(G):
                    first = ((par * G + h) * L + part * HALF) * TW + P
                    src = bass.AP(tab.tensor, first, [[TW - 1, P], [P * TW, 4], [1, WIN]])
                    sp.dma_start(win[:, par, 4 * part:4 * part + 4, h, ZL:], src).then_inc((ld_lo, ld_hi)[part][par], 16)

            def store_rows(n, par, qt):
                hold(sp, r_padded, n + 1)
                dst = tab[par].rearrange("h (t p) n -> t p h n", p=P)[qt, :, :, 0:PADL + NJ]
                sp.dma_start(dst, rows[:, qt % NR, :, :]).then_inc(t_wr[qt % NR], 16)

            def store_attn(i, hf, m):
                hold(sp, an_ready, m + 1)
                dst = row(ad, i)[hf * HALF:(hf + 1) * HALF, :].rearrange("(t p) n -> p t n", p=P)
                sp.dma_start(dst, an[:]).then_inc(an_out, 16)

            load_rel_q(0, 0)
            load_rel_q(1, 1)
            sp.wait_ge(s_bufs, 5)
            load_q(qT[:, 0], 0, ld_q[0])
            for i in range(2):
                for qt in range(TL):
                    store_rows(TL * i + qt, i, qt)
                    if i == 0 and qt in (1, 3, 5):
                        load_k(kT[:, 0, qt // 2], td[1 + qt // 2], 0, ld_k[0])
                if i == 0:
                    for p in range(NR):
                        sp.wait_ge(t_wr[p], 16 * (TL // NR))
                    load_windows(0, 0)
                    load_windows(0, 1)
            load_v(0, 0)
            load_rel_q(2, 0)

            def group(i, par, k, first=False, rel=True, last=False, ahead=True):
                if not last:
                    if not first:
                        hold(sp, pv_done, STEPS * i)
                    for p in range(NR):
                        hold(sp, t_wr[p], 16 * (TL // NR) * (i + 2))
                    load_windows(1 - par, 0)
                    load_qk(i + 1, 1 - par)
                if rel:
                    hold(sp, ld_lo[par], 16 * LW * (k + 1))
                    hold(sp, ld_hi[par], 16 * LW * (k + 1))
                for hf in range(2):
                    for t in range(16):
                        if t == N_STEP + 1 and not (first and hf == 0):
                            store_attn(i if hf else i - 1, 1 - hf, 2 * i + hf - 1)
                        if t in R_STEPS and rel:
                            qt = 4 * hf + R_STEPS[t]
                            store_rows(TL * (i + 2) + qt, par, qt)
                        if hf == 0 and not last:
                            if t == 6:
                                load_windows(1 - par, 1)
                            if t == 10:
                                load_v(i + 1, 1 - par)
                        if hf == 0 and t == 12 and ahead:
                            hold(sp, r_full, TL * (i + 2))
                            load_rel_q(i + 3, 1 - par)

            run_groups(sp, group)
            store_attn(NIT - 1, 1, 2 * NIT - 1)
            sp.wait_ge(an_out, 16 * 2 * NIT)

        @block.gpsimd
        def _(pool):
            nc.gpsimd.memset(zero[:], 0.0).then_inc(s_zero, 1)
            nc.gpsimd.memset(vs[:], 0.0).then_inc(s_ones, 1)
            pool.wait_ge(s_ones, 1)
            nc.gpsimd.memset(vs[:, :, :, :, HD:HD + 1], 1.0).then_inc(s_ones, 1)

            def mix_keys(b, hf, before, again):
                k = 2 * b + hf
                if again:
                    hold(pool, a_out[hf], 16 * A_DMAS * b)
                for m in range(2):
                    for v in range(2):
                        hold(pool, a_low, 6 * k + 3 + 2 * v + m)
                        halves = [part[:, hf, n, :, :].rearrange("p t (q n) -> p (t q) n", n=P)[:, :, v * ZL:(v + 1) * ZL]
                                  for n in (6 + m, 2 + 2 * v + m)]
                        nc.gpsimd.tensor_copy(halves[0], halves[1]).then_inc(a_mix, 1)

            run_blocks(pool, mix_keys)

            def pad_rows(n, qt):
                hold(pool, r_rows, n + 1)
                nc.gpsimd.tensor_copy(rows[:, qt % NR, :, 0:PADL],
                                      rows[:, qt % NR, :, PADL:PADL + 1].to_broadcast([P, G, PADL])).then_inc(r_padded, 1)

            def cast_window(T, par, k, part, q4, wait_use=True):
                hold(pool, (ld_lo, ld_hi)[part][par], 16 * LW * (k + 1))
                if wait_use:
                    hold(pool, mx_full, T_CH * (T - 2) + 8 * (q4 + 1))
                nc.gpsimd.tensor_copy(winb[:, part, q4, :, :], win[:, par, 4 * part + q4, :, ZL:]).then_inc(wb_ready, 1)

            for i in range(2):
                for qt in range(TL):
                    pad_rows(TL * i + qt, qt)
            for q4 in range(4):
                cast_window(0, 0, 0, 0, q4, False)
            cast_window(1, 0, 0, 1, 0, False)

            def group(i, par, k, first=False, rel=True, last=False, ahead=True):
                for hf in range(2):
                    T = 2 * i + hf
                    for t in range(16):
                        if t in (0, 3, 6) and not (last and hf):
                            tp, tk = (par, k) if hf == 0 else (1 - par, k + par)
                            cast_window(T + 1, tp, tk, 1 - hf, 1 + t // 3, not first or hf == 1)
                        if t == 12 and not last:
                            cast_window(T + 2, 1 - par, k + par, hf, 0)
                        if t in R_STEPS and rel:
                            qt = 4 * hf + R_STEPS[t]
                            pad_rows(TL * (i + 2) + qt, qt)

            run_groups(pool, group)

        @block.scalar
        def _(act):
            act.wait_ge(s_prep, 3)

            def project(b, hf, before, again):
                k = 2 * b + hf
                if again:
                    act.wait_ge(a_out[hf], 16 * A_DMAS * b)
                    act.wait_ge(a_low, 6 * (k - 1))

                def value(n):
                    act.wait_ge(a_full, 6 * k + 1 + n)
                    nc.scalar.activation(val[:, hf, n, :], psT[:, n, :], ACT.Identity, bias=colc[:, n:n + 1],
                                         scale=0.25 if n < 2 else 1.0).then_inc(a_val, 1)

                def high(n):
                    if n < 4:
                        act.wait_ge(a_val, 4 * k + 1 + n)
                    else:
                        act.wait_ge(a_hi_val, 2 * k + n - 3)
                    nc.scalar.activation(part[:, hf, n, 0, :], val[:, hf, n, :], ACT.Copy).then_inc(a_high, 1)

                def middle(n):
                    act.wait_ge(a_rem, 6 * k + 1 + n)
                    nc.scalar.activation(part[:, hf, n, 1, :], rem[:, hf, n, :], ACT.Copy).then_inc(a_mid, 1)

                value(0)
                value(1)
                high(0)
                high(1)
                value(2)
                value(3)
                for n in range(2, 6):
                    middle(n - 2)
                    high(n)
                middle(4)
                middle(5)

            run_blocks(act, project)
            act.wait_ge(s_bufs, 1)

            def copy_rows(n, qt, tw):
                act.wait_ge(r_full, n + 1)
                act.wait_ge(t_wr[qt % NR], 16 * tw)
                nc.scalar.activation(rows[:, qt % NR, :, PADL:PADL + NJ],
                                     psM[:, 0:G * NJ].rearrange("p (h n) -> p h n", h=G), ACT.Copy).then_inc(r_rows, 1)

            def exps(i, s, first):
                act.wait_ge(st_done, STEPS * i + s + 1)
                if not (first and s < NP_BUF):
                    act.wait_ge(pv_done, STEPS * i + s + 1 - NP_BUF)
                hp = s % 2
                nc.scalar.activation(pr[:, s % NP_BUF, :], psT[:, 2 * hp:2 * hp + 2, :].rearrange("p a n -> p (a n)"),
                                     ACT.Exp).then_inc(exp_done, 1)

            def copy_out(T):
                act.wait_ge(pv_done, 16 * (T + 1))
                if not (isinstance(T, int) and T == 0):
                    act.wait_ge(o_turned, T)
                nc.scalar.activation(ot[:], psO[:], ACT.Copy).then_inc(o_copied, 1)

            for i in range(2):
                for qt in range(TL):
                    copy_rows(TL * i + qt, qt, TL // NR * i + qt // NR)

            def group(i, par, k, first=False, rel=True, last=False, ahead=True):
                for hf in range(2):
                    for t in range(16):
                        exps(i, 16 * hf + t, first)
                        if t == 2 and not (first and hf == 0):
                            copy_out(2 * i + hf - 1)
                        if t in R_STEPS and rel:
                            qt = 4 * hf + R_STEPS[t]
                            copy_rows(TL * (i + 2) + qt, qt, TL // NR * (i + 2) + qt // NR)

            run_groups(act, group)
            copy_out(2 * NIT - 1)

        @block.vector
        def _(dve):
            small = [0]

            def link(ins):
                small[0] += 1
                ins.then_inc(s_dve, 1)
                dve.wait_ge(s_dve, small[0])

            dve.wait_ge(s_const, 16 * NCONST)
            nc.vector.tensor_scalar(colc[:, 0:2], colb[:, 0:2], 0.25, None, ALU.mult).then_inc(s_prep, 1)
            nc.vector.tensor_scalar(colc[:, 2:4], colb[:, 2:4], colb[:, 4:5], None, ALU.add).then_inc(s_prep, 1)
            nc.vector.tensor_scalar(colc[:, 4:6], colb[:, 2:4], colb[:, 5:6], None, ALU.add).then_inc(s_prep, 1)
            link(nc.vector.tensor_tensor(embd[:], embr[:, 0:NJ], embr[:, NJ:NJ + 1].to_broadcast([KR, NJ]), ALU.subtract))
            left = embd[:]
            for p in range(3):
                link(nc.vector.tensor_copy(embp[:, p, :], left))
                if p < 2:
                    link(nc.vector.tensor_tensor(embt[:, p, :], left, embp[:, p, :], ALU.subtract))
                    left = embt[:, p, :]
            link(nc.vector.tensor_scalar(embt[:, 2, :], embp[:, 0, :], prow[:, 0:1], None, ALU.mult))
            link(nc.vector.scalar_tensor_tensor(embt[:, 0, :], embp[:, 1, :], prow[:, 1:2], embt[:, 2, :], ALU.mult, ALU.add))
            link(nc.vector.scalar_tensor_tensor(embS[:], embp[:, 2, :], prow[:, 2:3], embt[:, 0, :], ALU.mult, ALU.add))
            nc.vector.tensor_copy(idb[:], idf[:]).then_inc(s_prep, 1)
            dve.wait_ge(s_ones, 2)

            def project(b, hf, before, again):
                k = 2 * b + hf
                if again:
                    dve.wait_ge(a_out[hf], 16 * A_DMAS * b)
                    dve.wait_ge(a_mid, 6 * (k - 1))

                def k_hi(m):
                    dve.wait_ge(a_val, 4 * k + 3 + m)
                    nc.vector.tensor_scalar(val[:, hf, 4 + m, :], psT[:, 2 + m, :], colc[:, 4 + m:5 + m], None,
                                            ALU.add).then_inc(a_hi_val, 1)

                def remainder(n):
                    dve.wait_ge(a_high, 6 * k + 1 + n)
                    nc.vector.tensor_tensor(rem[:, hf, n, :], val[:, hf, n, :], part[:, hf, n, 0, :], ALU.subtract).then_inc(a_rem, 1)

                def low(n):
                    dve.wait_ge(a_mid, 6 * k + 1 + n)
                    nc.vector.tensor_tensor(part[:, hf, n, 2, :], rem[:, hf, n, :], part[:, hf, n, 1, :], ALU.subtract).then_inc(a_low, 1)

                remainder(0)
                remainder(1)
                k_hi(0)
                k_hi(1)
                for v in range(2):
                    dve.wait_ge(a_full, 6 * k + 5 + v)
                    for e in range(2):
                        last = nc.vector.tensor_tensor(
                            vs[:, hf, 2 * v + e, :, 0:HD],
                            psX[:, v, e * D:(e + 1) * D].rearrange("p (h d) -> p h d", d=HD),
                            bvt[:].rearrange("p (h d) -> p h d", d=HD), ALU.add)
                    last.then_inc(a_v, 1)
                for n in range(2, 6):
                    low(n - 2)
                    remainder(n)
                low(4)
                low(5)

            run_blocks(dve, project)
            for hf in range(2):
                dve.wait_ge(a_out[hf], 16 * A_DMAS * B)
            dve.wait_ge(s_pads, 16 * NPADS)
            nc.vector.memset(kT[KR:KR + 2, 0], 1.0).then_inc(s_bufs, 1)
            for par in range(2):
                nc.vector.memset(win[:, par, :, :, 0:ZL], 0.0).then_inc(s_bufs, 1)
            nc.vector.memset(mcol[:], 0.0).then_inc(s_bufs, 1)
            nc.vector.memset(kT[KR:KR + 2, 1], 1.0).then_inc(s_bufs, 1)

            def reduce(T, part, c, q4, kh, h):
                n = T_CH * T + c
                dve.wait_ge(mx_full, n + 1)
                nc.vector.tensor_reduce(nmax[:, part, q4, kh, h:h + 1], psX[:, c % 2, :], AX.X, ALU.max,
                                        negate=True).then_inc(mx_free, 1)
                if c % 8 == 7:
                    m = 4 * T + q4
                    dve.wait_ge(mx_free, n + 1)
                    nc.vector.tensor_tensor(mval[:], nmax[:, part, q4, 0, :], nmax[:, part, q4, 1, :],
                                            ALU.min).then_inc(m_small, 1)
                    if not (isinstance(T, int) and m == 0):
                        dve.wait_ge(m_turned, m)
                    dve.wait_ge(m_small, 2 * m + 1)
                    nc.vector.tensor_copy(mcol[:, :, 0], mval[:]).then_inc(m_small, 1)
                    dve.wait_ge(m_small, 2 * m + 2)
                    nc.vector.tensor_tensor(mcol[:, :, 1], mval[:], mcol[:, :, 0], ALU.subtract).then_inc(m_ready, 1)

            def chunk(T, part, c):
                reduce(T, part, c, c // 8, c // 4 % 2, c % 4)

            def place_max(T, par, part, q4, i):
                dve.wait_ge(m_turned, 4 * T + q4 + 1)
                if i is not None:
                    dve.wait_ge(st_done, 16 * (T - 1))
                to = qT[96:98, par, :, part * HALF + q4 * P:part * HALF + (q4 + 1) * P]
                nc.vector.tensor_copy(to, psM[96:98, :].rearrange("p (h n) -> p h n", h=G)).then_inc(qm_ready, 1)

            def normalise(T):
                dve.wait_ge(o_turned, T + 1)
                o = psM[:].rearrange("p (g r) -> p g r", r=32)
                nc.vector.reciprocal(orec[:], o[:, :, HD]).then_inc(o_rec, 1)
                dve.wait_ge(o_rec, T + 1)
                if not (isinstance(T, int) and T == 0):
                    dve.wait_ge(an_out, 16 * T)
                nc.vector.tensor_tensor(an[:].rearrange("p q (h d) -> p (q h) d", d=HD), o[:, :, 0:HD],
                                        orec[:].unsqueeze(2).to_broadcast([P, 16, HD]), ALU.mult).then_inc(an_ready, 1)

            for c in range(T_CH):
                chunk(0, 0, c)
                if c % 8 == 7:
                    place_max(0, 0, 0, c // 8, None)
            for c in range(LEAD):
                chunk(1, 1, c)

            def group(i, par, k, first=False, rel=True, last=False, ahead=True):
                for hf in range(2):
                    T = 2 * i + hf
                    for t in range(16):
                        if t == N_STEP + 1 and not (first and hf == 0):
                            normalise(T - 1)
                        for ahead, c in chunks_at(t):
                            if not (last and hf + ahead >= 1):
                                chunk(T + 1 + ahead, (hf + 1 + ahead) % 2, c)
                        if t in M_STEPS and not (last and hf):
                            place_max(T + 1, par if hf == 0 else 1 - par, 1 - hf, M_STEPS[t], None if first and hf == 0 else i)

            run_groups(dve, group)
            normalise(2 * NIT - 1)

        @block.tensor
        def _(pe):
            mm = nc.tensor.matmul
            pe.wait_ge(s_w, 16 * 3)

            def project(b, hf, before, again):
                k = 2 * b + hf
                pe.wait_ge(a_x[hf], 16 * (b + 1))
                if before:
                    pe.wait_ge(a_val, 4 * k)
                for w, bank in ((wq, 0), (wk, 2)):
                    if bank and before:
                        pe.wait_ge(a_hi_val, 2 * k)
                    for m in range(2):
                        for c in range(2):
                            last = mm(psT[:, bank + m, :], w[:, c, m * P:(m + 1) * P], xs[:, hf, c, :],
                                      start=(c == 0), stop=(c == 1))
                        last.then_inc(a_full, 1)
                if before:
                    pe.wait_ge(a_v, 2 * k)
                for v in range(2):
                    for e in range(2):
                        t = 2 * v + e
                        for c in range(2):
                            last = mm(psX[:, v, e * D:(e + 1) * D], xs[:, hf, c, t * P:(t + 1) * P], wv[:, c, :],
                                      start=(c == 0), stop=(c == 1))
                    last.then_inc(a_full, 1)

            run_blocks(pe, project)
            pe.wait_ge(a_val, 8 * B)
            pe.wait_ge(a_hi_val, 4 * B)
            pe.wait_ge(a_v, 4 * B)

            def misc_bank(R, M, O):
                pe.wait_ge(r_rows, R)
                if M is not None:
                    pe.wait_ge(qm_ready, M)
                if O is not None:
                    pe.wait_ge(an_ready, O)

            def make_rows(n, par, k, qt, M, O=None):
                if qt == 0:
                    pe.wait_ge(ld_r[par], 16 * LQ * (k + 1))
                misc_bank(n, M, O)
                for h in range(G):
                    last = mm(psM[:, h * NJ:(h + 1) * NJ], qR[0:KR, par, h, qt * P:(qt + 1) * P], embS[:],
                              start=True, stop=True)
                last.then_inc(r_full, 1)

            def max_chunk(T, part, par, k, c, begun=True):
                q4, kh, h = c // 8, c // 4 % 2, c % 4
                qt = 4 * part + q4
                if c == 0:
                    pe.wait_ge(ld_q[par], 16 * LQ * (k + 1))
                    pe.wait_ge(ld_k[par], 16 * LK * (k + 1))
                if c % 8 == 0:
                    pe.wait_ge(wb_ready, 4 * T + q4 + 1)
                if begun:
                    pe.wait_ge(mx_free, T_CH * T + c - 1)
                lo = kh * HALF
                bank = psX[:, c % 2, :]
                ps = by_key(qt, kh)
                w0, w1 = max(qt * P - LEFT, lo), min(qt * P + P + RIGHT, lo + HALF)
                near = w0 < w1
                for n, (a, e, v) in enumerate(ps):
                    last = mm(bank[:, a - lo:e - lo], qT[0:KR, par, h, qt * P:(qt + 1) * P], kT[0:KR, par, v, h, a:e],
                              start=(n == 0), stop=not near and n == len(ps) - 1, skip_group_check=True)
                if near:
                    u = w0 - (qt * P - LEFT)
                    last = mm(bank[:, w0 - lo:w1 - lo], idb[:], winb[:, part, q4, h, u:u + w1 - w0],
                              start=False, stop=True, skip_group_check=True)
                last.then_inc(mx_full, 1)

            def turn_max(m, R, O=None):
                pe.wait_ge(m_ready, m + 1)
                misc_bank(R, m, O)
                for h in range(G):
                    last = mm(psM[96:P, h * P:(h + 1) * P], mcol[:, h, :], idb[:], start=True, stop=True)
                last.then_inc(m_turned, 1)

            def scores(i, par, s, first):
                hf, kt, hp = s // 16, s % 16 // 2, s % 2
                if s % 16 == 0:
                    pe.wait_ge(qm_ready, 4 * (2 * i + hf + 1))
                if not (first and s < 2):
                    pe.wait_ge(exp_done, STEPS * i + s - 1)
                lo = hf * HALF
                ps = by_query(kt, hf)
                near = [(qt, c0, w) for qt, c0, w in ((kt + 1, 0, P), (kt, P, P), (kt - 1, 2 * P, RIGHT))
                        if 4 * hf <= qt < 4 * hf + 4]
                for n, (a, e, v) in enumerate(ps):
                    for h in (2 * hp, 2 * hp + 1):
                        last = mm(psT[:, h, a - lo:e - lo], kT[0:KR + 2, par, v, h, kt * P:(kt + 1) * P], qT[0:KR + 2, par, h, a:e],
                                  start=(n == 0), stop=not near and n == len(ps) - 1, skip_group_check=True)
                for n, (qt, c0, w) in enumerate(near):
                    for h in (2 * hp, 2 * hp + 1):
                        if w == P:
                            last = mm(psT[:, h, qt * P - lo:(qt + 1) * P - lo], win[:, par, qt, h, c0:c0 + w], idf[:],
                                      is_transpose=True, start=False, stop=n == len(near) - 1, skip_group_check=True)
                        else:
                            last = mm(psT[0:w, h, (qt + 1) * P - w - lo:(qt + 1) * P - lo], win[:, par, qt, h, c0:c0 + w],
                                      idf[:, P - w:P], start=False, stop=n == len(near) - 1, skip_group_check=True)
                last.then_inc(st_done, 1)

            def weigh(i, par, s, first):
                hf, kt, hp = s // 16, s % 16 // 2, s % 2
                pe.wait_ge(exp_done, STEPS * i + s + 1)
                if s % 16 == 0 and not (first and hf == 0):
                    pe.wait_ge(o_copied, 2 * i + hf)
                for e in range(2):
                    h = 2 * hp + e
                    last = mm(psO[32 * h:32 * h + 32, :], vS[:, par, kt, 32 * h:32 * h + 32],
                              pr[:, s % NP_BUF, e * HALF:(e + 1) * HALF], start=(kt == 0), stop=(kt == TL - 1))
                last.then_inc(pv_done, 1)

            def turn_out(T, R, M, O=None):
                pe.wait_ge(o_copied, T + 1)
                misc_bank(R, M, O)
                for q in range(4):
                    last = nc.tensor.transpose(psM[:, q * P:(q + 1) * P], ot[:, q * P:(q + 1) * P], idf[:])
                last.then_inc(o_turned, 1)

            pe.wait_ge(s_prep, 4)
            pe.wait_ge(s_bufs, 5)
            for i in range(2):
                for qt in range(TL):
                    make_rows(TL * i + qt, i, 0, qt, None)
            for c in range(T_CH):
                max_chunk(0, 0, 0, 0, c, c >= 2)
                if c % 8 == 7:
                    turn_max(c // 8, 2 * TL)
            for c in range(LEAD):
                max_chunk(1, 1, 0, 0, c)

            def group(i, par, k, first=False, rel=True, last=False, ahead=True):
                for hf in range(2):
                    T = 2 * i + hf
                    for t in range(16):
                        s = 16 * hf + t
                        scores(i, par, s, first)
                        for ahead, c in chunks_at(t):
                            if not (last and hf + ahead >= 1):
                                same = hf + 1 + ahead < 2
                                max_chunk(T + 1 + ahead, (hf + 1 + ahead) % 2, par if same else 1 - par,
                                          k if same else k + par, c)
                        if s >= 2:
                            weigh(i, par, s - 2, first)
                        elif not first:
                            weigh(i - 1, 1 - par, STEPS + s - 2, False)
                        outs = None if first and hf == 0 or first and t <= N_STEP else T if t > N_STEP else T - 1
                        tabs = TL * (i + 2) + 4 * hf + sum(u < t for u in R_STEPS) if rel else TL * NIT
                        turns = 4 * (T + 1) + sum(u < t for u in M_STEPS) if not (last and hf) else 8 * NIT
                        if t in R_STEPS and rel:
                            qt = 4 * hf + R_STEPS[t]
                            make_rows(tabs, par, k + 1, qt, turns, outs)
                        if t in M_STEPS and not (last and hf):
                            turn_max(turns, tabs, outs)
                        if t == N_STEP and not (first and hf == 0):
                            turn_out(T - 1, tabs, turns, outs)

            run_groups(pe, group)
            weigh(NIT - 1, 1, STEPS - 2, False)
            weigh(NIT - 1, 1, STEPS - 1, False)
            turn_out(2 * NIT - 1, TL * NIT, 8 * NIT, 2 * NIT - 1)



def decoder_rest(nc, sem, ad, x, ident, woT, bo, ctxT, xwqT, xwkT, xwvT, xbq, xbk, xbv, w_up, w_gate, w_down, out):
    h2d = nc.dram_tensor("second_norm", [NBLK, HALF, D], F32, kind="Internal").ap()
    s_held = sem("f_held")

    def hold(eng, s, value):
        eng.wait_ge(s, value)
        eng.sem_inc(s_held, 1)

    def tokens(t, n):
        return t[bass.ds(n, 1)].rearrange("a (q p) d -> p (a q) d", p=P)

    with ExitStack() as ctx:
        def sb(name, shape, dt=F32):
            return ctx.enter_context(nc.sbuf_tensor(name, shape, dt))

        idf = sb("ident_f", [P, P])
        wuT = sb("w_upT", [P, 2, FI])
        wgT = sb("w_gateT", [P, 2, FI])
        wdT = sb("w_downT", [P, FT, D])
        neg_half = sb("neg_half", [P, 1])
        amax = sb("amax", [P, NSC, NBLK])
        top = sb("top", [P, NSC])
        top_all = sb("top_all", [P, NSC])
        step = sb("step", [P, NSC])
        inv = sb("inv", [P, NSC])
        stats = sb("stats", [P, 2, 4, 6])
        mv = sb("mean_var", [P, 2, 4, 2])
        rstd = sb("rstd", [P, 2, 4])
        magic = sb("magic", [P, 1])
        ps = ctx.enter_context(nc.psum_tensor("banks", [P, 8, HALF], F32))

        l_sum = sem("l_sum")
        l_stat = sem("l_stat")
        l_aggr = sem("l_aggr")
        l_eps = sem("l_eps")
        l_rstd = sem("l_rstd")
        s_half = sem("s_half")
        t_top = sem("t_top")
        t_all = sem("t_all")
        t_step = sem("t_step")
        t_inv = sem("t_inv")

        def norm_stats(dve, i, hf, h):
            hold(dve, l_sum, i + 1)
            for q in range(4):
                last = nc.vector.bn_stats(stats[:, hf, q, :], h[:, q, :])
            last.then_inc(l_stat, 1)
            hold(dve, l_stat, i + 1)
            for q in range(4):
                last = nc.vector.bn_aggr(mv[:, hf, q, :], stats[:, hf, q, :])
            last.then_inc(l_aggr, 1)

        def norm_rstd(pool, i, hf):
            hold(pool, l_aggr, i + 1)
            nc.gpsimd.tensor_scalar(rstd[:, hf, :], mv[:, hf, :, 1], EPS, None, ALU.add).then_inc(l_eps, 1)
            hold(pool, l_eps, i + 1)
            nc.gpsimd.tensor_tensor(rstd[:, hf, :], rstd[:, hf, :], neg_half[:].to_broadcast([P, 4]),
                                    ALU.pow).then_inc(l_rstd, 1)

        def norm_apply(dve, i, hf, h, to):
            hold(dve, l_rstd, i + 1)
            for q in range(4):
                last = nc.vector.tensor_scalar(to[:, q, :], h[:, q, :], mv[:, hf, q, 0:1], rstd[:, hf, q:q + 1],
                                               ALU.subtract, ALU.mult)
            return last

        def scale_dve(dve, k):
            nc.vector.tensor_reduce(top[:, k:k + 1], amax[:, k, :], AX.X, ALU.max).then_inc(t_top, 1)
            dve.wait_ge(t_all, k + 1)
            nc.vector.tensor_scalar(step[:, k:k + 1], top_all[:, k:k + 1], 1.0 / QMAX, TINY, ALU.mult, ALU.max).then_inc(t_step, 1)
            dve.wait_ge(t_step, k + 1)
            nc.vector.reciprocal(inv[:, k:k + 1], step[:, k:k + 1]).then_inc(t_inv, 1)

        def scale_pool(pool, k):
            pool.wait_ge(t_top, k + 1)
            nc.gpsimd.partition_all_reduce(top_all[:, k:k + 1], top[:, k:k + 1], P, RMAX).then_inc(t_all, 1)

        cross_attention(nc, sem, hold, tokens, ad, x, ident, woT, bo, ctxT, xwqT, xwkT, xwvT, xbq, xbk, xbv,
                        w_up, w_gate, w_down, h2d, idf, wuT, wgT, wdT, neg_half, magic, s_half, amax, ps,
                        l_sum, norm_stats, norm_rstd, norm_apply)

        with ExitStack() as feed:
            raw = feed.enter_context(nc.sbuf_tensor("raw", [P, NBLK, FT * HALF], F32))
            up = feed.enter_context(nc.sbuf_tensor("up_steps", [P, NBLK, FT * HALF], mybir.dt.int16))
            project_up_gate(nc, sem, hold, tokens, h2d, idf, wuT, wgT, magic, amax, step, inv, t_inv, ps, raw, up,
                            scale_dve, scale_pool)
            gate_and_down(nc, sem, hold, tokens, h2d, wdT, magic, amax, step, inv, t_inv, ps, raw, up,
                          scale_dve, scale_pool, l_sum, norm_stats, norm_rstd, norm_apply, out)


def cross_attention(nc, sem, hold, tokens, ad, x, ident, woT, bo, ctxT, xwqT, xwkT, xwvT, xbq, xbk, xbv,
                    w_up, w_gate, w_down, h2d, idf, wuT, wgT, wdT, neg_half, magic, s_half, amax, ps,
                    l_sum, norm_stats, norm_rstd, norm_apply):
    with ExitStack() as ctx:
        def sb(name, shape, dt=F32):
            return ctx.enter_context(nc.sbuf_tensor(name, shape, dt))

        wo = sb("wo", [P, 2, D])
        xq_w = sb("xq_w", [P, 2, D])
        xk_w = sb("xk_w", [P, 2, D])
        xv_w = sb("xv_w", [P, 2, D])
        bot = sb("bot", [P, D])
        bvt = sb("xbvt", [P, D])
        bqk = sb("bqk", [P, 4])
        cT = sb("cT", [P, 2, B, LC])
        kx = sb("kx", [P, 2, B, LC])
        vx = sb("vx", [P, 2, B, D])
        at = sb("at", [P, 2, 4, D])
        xt = sb("xt", [P, 2, 4, D])
        atT = sb("atT", [P, 2, 2, HALF])
        h = sb("h", [P, 2, 4, D])
        h1 = sb("h1", [P, 2, 4, D])
        h1T = sb("h1T", [P, 2, 2, HALF])
        qx = sb("qx", [P, 2, 2, HALF])
        nm = sb("nm", [P, 2, 4])
        e = sb("e", [P, 2, 4, LC])
        esum = sb("esum", [P, 2, 4])
        erec = sb("erec", [P, 2, 4])
        eT = sb("eT", [P, 2, 2, HALF])
        g = sb("g", [P, 2, 4, D])
        h2 = sb("h2", [P, 2, 4, D])
        wn = [sb(f"wn{j}", [P, FT * D]) for j in range(3)]
        ws = [sb(f"ws{j}", [P, FT * D // 32]) for j in range(3)]
        wi = [sb(f"wi{j}", [P, FT * D // 32]) for j in range(3)]

        c_in = sem("c_in")
        ld = [sem(f"d_ld{j}") for j in range(2)]
        d_st = [sem(f"d_st{j}") for j in range(2)]
        d_t1 = sem("d_t1")
        d_atT = sem("d_atT")
        d_y = sem("d_y")
        d_bo = sem("d_bo")
        d_h1 = sem("d_h1")
        d_t2 = sem("d_t2")
        d_h1T = sem("d_h1T")
        d_q = sem("d_q")
        d_qx = sem("d_qx")
        d_s = sem("d_s")
        d_nm = sem("d_nm")
        d_e = sem("d_e")
        d_t3 = sem("d_t3")
        d_eT = sem("d_eT")
        d_a = sem("d_a")
        d_rec = sem("d_rec")
        d_h2 = sem("d_h2")
        d_am = sem("d_am")
        c_kv = sem("c_kv")
        c_k = sem("c_k")
        c_v = sem("c_v")
        w_in = sem("w_in")
        w_top = sem("w_top")
        w_inv = sem("w_inv")
        w_s = sem("w_s")
        w_over = sem("w_over")
        w_round = sem("w_round")
        w_deq = sem("w_deq")
        w_turn = sem("w_turn")
        w_copy = sem("w_copy")

        block = ctx.enter_context(nc.Block())
        NC_IN = 10
        TAIL = LC - P

        def run_batches(eng, batch):
            batch(0, False)
            with eng.Fori(1, B) as b:
                batch(b, True)

        @block.sync
        def _(sp):
            for j, w in enumerate((w_up, w_gate)):
                sp.dma_start(wn[j][:].rearrange("p (t d) -> p t d", d=D), w.rearrange("(t p) d -> p t d", p=P)).then_inc(w_in, 16)
            sp.dma_start(wn[2][:].rearrange("p (t d) -> p t d", d=FI), w_down.rearrange("(t p) d -> p t d", p=P)).then_inc(w_in, 16)
            sp.dma_start(idf[:], ident).then_inc(c_in, 16)
            for to, w in ((wo, woT), (xq_w, xwqT), (xk_w, xwkT), (xv_w, xwvT)):
                sp.dma_start(to[:], w.rearrange("(c p) n -> p c n", p=P)).then_inc(c_in, 16)
            sp.dma_start(cT[:].rearrange("p c b t -> p c (b t)"), ctxT.rearrange("(c p) n -> p c n", p=P)).then_inc(c_in, 16)
            sp.dma_start(bot[:], bo).then_inc(c_in, 16)
            sp.dma_start(bvt[:], xbv).then_inc(c_in, 16)
            sp.dma_start(bqk[:, 0:2], xbq).then_inc(c_in, 16)
            sp.dma_start(bqk[:, 2:4], xbk).then_inc(c_in, 16)

            def batch(b, before):
                for hf in range(2):
                    n = 2 * b + hf
                    if before:
                        hold(sp, d_t1, n - 1)
                        hold(sp, l_sum, 4 * b - 3 + hf)
                    for gr in range(4):
                        sp.dma_start(at[:, hf, :, gr * G * HD:(gr + 1) * G * HD],
                                     ad[bass.ds(4 * b + gr, 1), hf * HALF:(hf + 1) * HALF, :].rearrange(
                                         "a (q p) d -> p (a q) d", p=P)).then_inc(ld[hf], 16)
                    sp.dma_start(xt[:, hf], tokens(x, n)).then_inc(ld[hf], 16)
                if before:
                    for hf in range(2):
                        hold(sp, d_h2, 2 * b + hf - 1)
                        sp.dma_start(tokens(h2d, 2 * b + hf - 2), h2[:, hf]).then_inc(d_st[hf], 16)

            run_batches(sp, batch)
            for hf in range(2):
                sp.wait_ge(d_h2, NBLK - 1 + hf)
                sp.dma_start(tokens(h2d, NBLK - 2 + hf), h2[:, hf]).then_inc(d_st[hf], 16)
            for hf in range(2):
                sp.wait_ge(d_st[hf], 16 * B)

        @block.gpsimd
        def _(pool):
            nc.gpsimd.memset(magic[:], MAGIC)
            nc.gpsimd.memset(neg_half[:], -0.5).then_inc(s_half, 1)
            pool.wait_ge(s_half, 1)
            def batch(b, before):
                for ln in range(2):
                    for hf in range(2):
                        norm_rstd(pool, 4 * b + 2 * ln + hf, hf)

            run_batches(pool, batch)

        @block.scalar
        def _(act):
            act.wait_ge(c_in, 16 * NC_IN)
            for m in range(2):
                for j in range(2):
                    act.wait_ge(c_kv, 2 * m + j + 1)
                    last = nc.scalar.activation(kx[:, m, 2 * j:2 * j + 2, :].rearrange("p b t -> p (b t)"),
                                                ps[:, 2 * m + j, 0:2 * LC], ACT.Identity, bias=bqk[:, 2 + m:3 + m])
                    last.then_inc(c_k, 1)
            for j, to in enumerate((wuT, wgT, wdT)):
                flat = to[:].rearrange("p a b -> p (a b)")
                for k in range(3):
                    act.wait_ge(w_turn, 3 * j + k + 1)
                    nc.scalar.activation(flat[:, k * HALF:(k + 1) * HALF], ps[:, (3 * j + k) % 8, :], ACT.Copy).then_inc(w_copy, 1)

            def batch(b, before):
                for hf in range(2):
                    hold(act, d_t1, 2 * b + hf + 1)
                    nc.scalar.activation(atT[:, hf], ps[:, 2 * hf:2 * hf + 2, :], ACT.Copy).then_inc(d_atT, 1)
                for hf in range(2):
                    hold(act, d_t2, 2 * b + hf + 1)
                    nc.scalar.activation(h1T[:, hf], ps[:, 2 * hf:2 * hf + 2, :], ACT.Copy).then_inc(d_h1T, 1)
                for hf in range(2):
                    hold(act, d_q, 2 * b + hf + 1)
                    for m in range(2):
                        last = nc.scalar.activation(qx[:, hf, m, :], ps[:, 4 + 2 * hf + m, :], ACT.Identity, bias=bqk[:, m:m + 1])
                    last.then_inc(d_qx, 1)
                for hf in range(2):
                    hold(act, d_nm, 2 * b + hf + 1)
                    for q in range(4):
                        o = (q % 2) * D
                        last = nc.scalar.activation(e[:, hf, q, :], ps[:, 2 * hf + q // 2, o:o + LC], ACT.Exp,
                                                    bias=nm[:, hf, q:q + 1], accum_out=esum[:, hf, q:q + 1])
                    last.then_inc(d_e, 1)
                for hf in range(2):
                    hold(act, d_t3, 2 * b + hf + 1)
                    nc.scalar.activation(eT[:, hf, 0, :], ps[:, 4 + 2 * hf, :], ACT.Copy)
                    nc.scalar.activation(eT[0:TAIL, hf, 1, :], ps[0:TAIL, 5 + 2 * hf, :], ACT.Copy).then_inc(d_eT, 1)

            run_batches(act, batch)

        @block.vector
        def _(dve):
            dve.wait_ge(w_in, 16 * 3)
            for j in range(3):
                v = wn[j][:].rearrange("p (n k) -> p n k", k=32)
                nc.vector.tensor_reduce(ws[j][:], v, AX.X, ALU.max, apply_absolute_value=True).then_inc(w_top, 1)
                dve.wait_ge(w_top, j + 1)
                nc.vector.tensor_scalar(ws[j][:], ws[j][:], 1.0 / 7.0, TINY, ALU.mult, ALU.max).then_inc(w_s, 1)
                dve.wait_ge(w_s, j + 1)
                nc.vector.reciprocal(wi[j][:], ws[j][:]).then_inc(w_inv, 1)
                dve.wait_ge(w_inv, j + 1)
                nc.vector.tensor_tensor(v, v, wi[j][:].unsqueeze(2).to_broadcast([P, FT * D // 32, 32]),
                                        ALU.mult).then_inc(w_over, 1)
            dve.wait_ge(c_in, 16 * NC_IN)
            dve.wait_ge(c_kv, 5)
            for b in range(B):
                nc.vector.tensor_tensor(vx[:, 0, b, :], ps[:, 4 + b // 2, (b % 2) * D:(b % 2 + 1) * D], bvt[:], ALU.add)
                last = nc.vector.tensor_tensor(vx[0:TAIL, 1, b, :], ps[0:TAIL, 6 + b // 2, (b % 2) * D:(b % 2 + 1) * D],
                                               bvt[0:TAIL, :], ALU.add)
            last.then_inc(c_v, 1)
            for j in range(3):
                v = wn[j][:].rearrange("p (n k) -> p n k", k=32)
                dve.wait_ge(w_over, j + 1)
                nc.vector.tensor_scalar(wn[j][:], wn[j][:], MAGIC, MAGIC, ALU.add, ALU.subtract).then_inc(w_round, 1)
                dve.wait_ge(w_round, j + 1)
                nc.vector.tensor_tensor(v, v, ws[j][:].unsqueeze(2).to_broadcast([P, FT * D // 32, 32]),
                                        ALU.mult).then_inc(w_deq, 1)

            def batch(b, before):
                for hf in range(2):
                    n = 2 * b + hf
                    hold(dve, ld[hf], 16 * 5 * (b + 1))
                    nc.vector.tensor_tensor(xt[:, hf], xt[:, hf], bot[:].unsqueeze(1).to_broadcast([P, 4, D]), ALU.add).then_inc(d_bo, 1)
                for hf in range(2):
                    n = 2 * b + hf
                    hold(dve, d_bo, n + 1)
                    hold(dve, d_y, n + 1)
                    nc.vector.tensor_tensor(h[:, hf].rearrange("p q d -> p (q d)"),
                                            ps[:, 4 + 2 * hf:6 + 2 * hf, :].rearrange("p a n -> p (a n)"),
                                            xt[:, hf].rearrange("p q d -> p (q d)"), ALU.add).then_inc(l_sum, 1)
                    norm_stats(dve, 4 * b + hf, hf, h[:, hf])
                for hf in range(2):
                    norm_apply(dve, 4 * b + hf, hf, h[:, hf], h1[:, hf]).then_inc(d_h1, 1)
                for hf in range(2):
                    hold(dve, d_s, 2 * b + hf + 1)
                    v = ps[:, 2 * hf:2 * hf + 2, :].rearrange("p a (c n) -> p (a c) n", n=D)
                    nc.vector.tensor_reduce(nm[:, hf, :], v[:, :, 0:LC], AX.X, ALU.max, negate=True).then_inc(d_nm, 1)
                for hf in range(2):
                    n = 2 * b + hf
                    hold(dve, d_e, n + 1)
                    nc.vector.reciprocal(erec[:, hf, :], esum[:, hf, :]).then_inc(d_rec, 1)
                    hold(dve, d_rec, n + 1)
                    hold(dve, d_a, n + 1)
                    for q in range(4):
                        o = (q % 2) * D
                        last = nc.vector.scalar_tensor_tensor(g[:, hf, q, :], ps[:, 2 * hf + q // 2, o:o + D],
                                                              erec[:, hf, q:q + 1], h1[:, hf, q, :], ALU.mult, ALU.add)
                    last.then_inc(l_sum, 1)
                    norm_stats(dve, 4 * b + 2 + hf, hf, g[:, hf])
                for hf in range(2):
                    n = 2 * b + hf
                    if before:
                        hold(dve, d_st[hf], 16 * b)
                    norm_apply(dve, 4 * b + 2 + hf, hf, g[:, hf], h2[:, hf]).then_inc(d_h2, 1)
                    hold(dve, d_h2, n + 1)
                    nc.vector.tensor_reduce(amax[:, 0, bass.ds(n, 1)], h2[:, hf].rearrange("p q d -> p (q d)"), AX.X, ALU.max,
                                            apply_absolute_value=True).then_inc(d_am, 1)

            run_batches(dve, batch)

        @block.tensor
        def _(pe):
            mm = nc.tensor.matmul
            tr = nc.tensor.transpose
            pe.wait_ge(c_in, 16 * NC_IN)
            for m in range(2):
                for j in range(2):
                    for c in range(2):
                        last = mm(ps[:, 2 * m + j, 0:2 * LC], xk_w[:, c, m * P:(m + 1) * P],
                                  cT[:, c, 2 * j:2 * j + 2, :].rearrange("p b t -> p (b t)"), start=(c == 0), stop=(c == 1))
                    last.then_inc(c_kv, 1)
            for b in range(B):
                for w, lo, hi in ((0, 0, P), (1, P, LC)):
                    for c in range(2):
                        last = mm(ps[0:hi - lo, 4 + 2 * w + b // 2, (b % 2) * D:(b % 2 + 1) * D], cT[:, c, b, lo:hi], xv_w[:, c, :],
                                  start=(c == 0), stop=(c == 1))
            last.then_inc(c_kv, 1)
            pe.wait_ge(c_k, 4)
            pe.wait_ge(c_v, 1)
            for j in range(3):
                pe.wait_ge(w_deq, j + 1)
                for k in range(3):
                    bank = 3 * j + k
                    if bank >= 8:
                        pe.wait_ge(w_copy, bank - 7)
                    for u in range(4):
                        v = 4 * k + u
                        if j < 2:
                            c, t = v // FT, v % FT
                            src = wn[j][:, t * D + c * P:t * D + (c + 1) * P]
                        else:
                            t, c = v // 2, v % 2
                            src = wn[j][:, c * FI + t * P:c * FI + (t + 1) * P]
                        last = tr(ps[:, bank % 8, u * P:(u + 1) * P], src, idf[:])
                    last.then_inc(w_turn, 1)
            pe.wait_ge(w_copy, 9)

            def batch(b, before):
                for hf in range(2):
                    hold(pe, ld[hf], 16 * 5 * (b + 1))
                    if before:
                        hold(pe, l_sum, 4 * b - 1 + hf)
                    for c in range(2):
                        for q in range(4):
                            last = tr(ps[:, 2 * hf + c, q * P:(q + 1) * P], at[:, hf, q, c * P:(c + 1) * P], idf[:])
                    last.then_inc(d_t1, 1)
                for hf in range(2):
                    hold(pe, d_atT, 2 * b + hf + 1)
                    for q in range(4):
                        for c in range(2):
                            last = mm(ps[:, 4 + 2 * hf + q // 2, (q % 2) * D:(q % 2 + 1) * D], atT[:, hf, c, q * P:(q + 1) * P],
                                      wo[:, c, :], start=(c == 0), stop=(c == 1))
                    last.then_inc(d_y, 1)
                for hf in range(2):
                    hold(pe, d_h1, 2 * b + hf + 1)
                    for c in range(2):
                        for q in range(4):
                            last = tr(ps[:, 2 * hf + c, q * P:(q + 1) * P], h1[:, hf, q, c * P:(c + 1) * P], idf[:])
                    last.then_inc(d_t2, 1)
                for hf in range(2):
                    hold(pe, d_h1T, 2 * b + hf + 1)
                    for m in range(2):
                        for c in range(2):
                            last = mm(ps[:, 4 + 2 * hf + m, :], xq_w[:, c, m * P:(m + 1) * P], h1T[:, hf, c, :],
                                      start=(c == 0), stop=(c == 1))
                    last.then_inc(d_q, 1)
                for hf in range(2):
                    hold(pe, d_qx, 2 * b + hf + 1)
                    for q in range(4):
                        for m in range(2):
                            o = (q % 2) * D
                            last = mm(ps[:, 2 * hf + q // 2, o:o + LC], qx[:, hf, m, q * P:(q + 1) * P],
                                      kx[:, m, bass.ds(b, 1), :].rearrange("p a t -> p (a t)"), start=(m == 0), stop=(m == 1))
                    last.then_inc(d_s, 1)
                for hf in range(2):
                    hold(pe, d_e, 2 * b + hf + 1)
                    for q in range(4):
                        tr(ps[:, 4 + 2 * hf, q * P:(q + 1) * P], e[:, hf, q, 0:P], idf[:])
                        last = tr(ps[0:TAIL, 5 + 2 * hf, q * P:(q + 1) * P], e[:, hf, q, P:LC], idf[:])
                    last.then_inc(d_t3, 1)
                for hf in range(2):
                    hold(pe, d_eT, 2 * b + hf + 1)
                    for q in range(4):
                        to = ps[:, 2 * hf + q // 2, (q % 2) * D:(q % 2 + 1) * D]
                        mm(to, eT[:, hf, 0, q * P:(q + 1) * P], vx[:, 0, bass.ds(b, 1), :].rearrange("p a d -> p (a d)"),
                           start=True, stop=False)
                        last = mm(to, eT[0:TAIL, hf, 1, q * P:(q + 1) * P],
                                  vx[0:TAIL, 1, bass.ds(b, 1), :].rearrange("p a d -> p (a d)"), start=False, stop=True)
                    last.then_inc(d_a, 1)

            run_batches(pe, batch)


def project_up_gate(nc, sem, hold, tokens, h2d, idf, wuT, wgT, magic, amax, step, inv, t_inv, ps, raw, up,
                    scale_dve, scale_pool):
    with ExitStack() as ctx:
        xqT = ctx.enter_context(nc.sbuf_tensor("xqT", [P, 2, NBLK, HALF], F32))
        hb = ctx.enter_context(nc.sbuf_tensor("hb", [P, 2, 4, D], F32))
        f_ld = [sem(f"f_ld{j}") for j in range(2)]
        f_x = sem("f_x")
        f_xq = sem("f_xq")
        f_t = sem("f_t")
        f_xqT = sem("f_xqT")
        f_u = sem("f_u")
        f_uc = sem("f_uc")
        f_ua = sem("f_ua")
        f_ur = sem("f_ur")
        f_ui = sem("f_ui")
        f_g = sem("f_g")
        f_gc = sem("f_gc")
        f_ga = sem("f_ga")
        block = ctx.enter_context(nc.Block())

        def run_pairs(eng, body):
            body(0, 0, False)
            body(1, 1, False)
            with eng.Fori(1, NBLK // 2) as j:
                body(2 * j, 0, True)
                body(2 * j + 1, 1, True)

        @block.sync
        def _(sp):
            def load(n, par, before):
                if before:
                    hold(sp, f_t, n - 1)
                sp.dma_start(hb[:, par], tokens(h2d, n)).then_inc(f_ld[par], 16)

            run_pairs(sp, load)

        @block.gpsimd
        def _(pool):
            for k in range(3):
                scale_pool(pool, k)

        @block.scalar
        def _(act):
            act.wait_ge(t_inv, 1)

            def turned(n, par):
                hold(act, f_t, n + 1)
                nc.scalar.activation(xqT[:, :, bass.ds(n, 1), :].rearrange("p c a n -> p c (a n)"),
                                     ps[:, 2 * par:2 * par + 2, :], ACT.Copy).then_inc(f_xqT, 1)

            def quantise(n, par, before):
                hold(act, f_ld[par], 16 * (n // 2 + 1))
                nc.scalar.activation(hb[:, par], hb[:, par], ACT.Identity, bias=magic[:], scale=inv[:, 0:1]).then_inc(f_x, 1)
                turned(n, par)

            run_pairs(act, quantise)
            with act.Fori(0, NBLK) as n:
                for m in range(FT):
                    hold(act, f_u, FT * n + m + 1)
                    nc.scalar.activation(raw[:, bass.ds(n, 1), m * HALF:(m + 1) * HALF].rearrange("p a n -> p (a n)"),
                                         ps[:, m, :], ACT.Copy).then_inc(f_uc, 1)
            act.wait_ge(t_inv, 2)

            def round_up(n):
                hold(act, f_ua, NBLK)
                v = raw[:, bass.ds(n, 1), :].rearrange("p a n -> p (a n)")
                nc.scalar.activation(v, v, ACT.Identity, bias=magic[:], scale=inv[:, 1:2]).then_inc(f_ur, 1)

            def copy_gate(n):
                hold(act, f_ui, n + 1)
                for m in range(FT):
                    hold(act, f_g, FT * n + m + 1)
                    nc.scalar.activation(raw[:, bass.ds(n, 1), m * HALF:(m + 1) * HALF].rearrange("p a n -> p (a n)"),
                                         ps[:, m, :], ACT.Copy).then_inc(f_gc, 1)

            round_up(0)
            with act.Fori(0, NBLK - 1) as n:
                round_up(n + 1)
                copy_gate(n)
            copy_gate(NBLK - 1)

        @block.vector
        def _(dve):
            scale_dve(dve, 0)

            def quantise(n, par, before):
                hold(dve, f_x, n + 1)
                nc.vector.tensor_scalar(hb[:, par], hb[:, par], MAGIC, step[:, 0:1], ALU.subtract, ALU.mult).then_inc(f_xq, 1)

            run_pairs(dve, quantise)
            with dve.Fori(0, NBLK) as n:
                hold(dve, f_uc, FT * n + FT)
                nc.vector.tensor_reduce(amax[:, 1, bass.ds(n, 1)], raw[:, bass.ds(n, 1), :].rearrange("p a n -> p (a n)"), AX.X, ALU.max,
                                        apply_absolute_value=True).then_inc(f_ua, 1)
            dve.wait_ge(f_ua, NBLK)
            scale_dve(dve, 1)
            with dve.Fori(0, NBLK) as n:
                hold(dve, f_ur, n + 1)
                nc.vector.tensor_scalar(up[:, bass.ds(n, 1), :].rearrange("p a n -> p (a n)"),
                                        raw[:, bass.ds(n, 1), :].rearrange("p a n -> p (a n)"), MAGIC, None,
                                        ALU.subtract).then_inc(f_ui, 1)
                hold(dve, f_gc, FT * n + FT)
                nc.vector.tensor_reduce(amax[:, 2, bass.ds(n, 1)], raw[:, bass.ds(n, 1), :].rearrange("p a n -> p (a n)"), AX.X, ALU.max,
                                        apply_absolute_value=True).then_inc(f_ga, 1)
            dve.wait_ge(f_ga, NBLK)
            scale_dve(dve, 2)

        @block.tensor
        def _(pe):
            mm = nc.tensor.matmul

            def turn(n, par, before):
                hold(pe, f_xq, n + 1)
                if before:
                    hold(pe, f_xqT, n - 1)
                for c in range(2):
                    for q in range(4):
                        last = nc.tensor.transpose(ps[:, 2 * par + c, q * P:(q + 1) * P], hb[:, par, q, c * P:(c + 1) * P], idf[:])
                last.then_inc(f_t, 1)

            run_pairs(pe, turn)
            pe.wait_ge(f_xqT, NBLK)

            def products(w, n, full, copied, before):
                for m in range(FT):
                    if before:
                        hold(pe, copied, FT * (n - 1) + m + 1)
                    for c in range(2):
                        last = mm(ps[:, m, :], w[:, c, m * P:(m + 1) * P],
                                  xqT[:, c, bass.ds(n, 1), :].rearrange("p a n -> p (a n)"), start=(c == 0), stop=(c == 1))
                    last.then_inc(full, 1)

            products(wuT, 0, f_u, None, False)
            with pe.Fori(1, NBLK) as n:
                products(wuT, n, f_u, f_uc, True)
            pe.wait_ge(f_uc, FT * NBLK)
            products(wgT, 0, f_g, None, False)
            with pe.Fori(1, NBLK) as n:
                products(wgT, n, f_g, f_gc, True)


def gate_and_down(nc, sem, hold, tokens, h2d, wdT, magic, amax, step, inv, t_inv, ps, raw, up,
                  scale_dve, scale_pool, l_sum, norm_stats, norm_rstd, norm_apply, out):
    with ExitStack() as ctx:
        work = ctx.enter_context(nc.sbuf_tensor("work", [P, 2, FT * HALF], F32))
        res = ctx.enter_context(nc.sbuf_tensor("res", [P, 2, 4, D], F32))
        g_r = sem("g_r")
        g_q = sem("g_q")
        g_sig = sem("g_sig")
        g_sr = sem("g_sr")
        g_sq = sem("g_sq")
        g_g2 = sem("g_g2")
        g_a2 = sem("g_a2")
        p_r = sem("p_r")
        p_q = sem("p_q")
        p_o = sem("p_o")
        p_a = sem("p_a")
        o_r = sem("o_r")
        o_q = sem("o_q")
        o_ps = sem("o_ps")
        o_fin = sem("o_fin")
        o_ld = [sem(f"o_ld{j}") for j in range(2)]
        o_st = [sem(f"o_st{j}") for j in range(2)]
        block = ctx.enter_context(nc.Block())

        def flat(t, n):
            return t[:, bass.ds(n, 1), :].rearrange("p a n -> p (a n)")

        def run_pairs(eng, body):
            body(0, 0, False)
            body(1, 1, False)
            with eng.Fori(1, NBLK // 2) as j:
                body(2 * j, 0, True)
                body(2 * j + 1, 1, True)

        @block.sync
        def _(sp):
            def load(n, par, before):
                if before:
                    hold(sp, o_fin, n - 1)
                    sp.dma_start(tokens(out, n - 2), res[:, par]).then_inc(o_st[par], 16)
                    hold(sp, o_st[par], 16 * (n // 2))
                sp.dma_start(res[:, par], tokens(h2d, n)).then_inc(o_ld[par], 16)

            run_pairs(sp, load)
            for par in range(2):
                sp.wait_ge(o_fin, NBLK - 1 + par)
                sp.dma_start(tokens(out, NBLK - 2 + par), res[:, par]).then_inc(o_st[par], 16)
            for par in range(2):
                sp.wait_ge(o_st[par], 8 * NBLK)

        @block.gpsimd
        def _(pool):
            scale_pool(pool, 3)
            scale_pool(pool, 4)
            run_pairs(pool, lambda n, par, before: norm_rstd(pool, 2 * NBLK + n, par))

        @block.scalar
        def _(act):
            def round_(n, k, done):
                nc.scalar.activation(flat(raw, n), flat(raw, n), ACT.Identity, bias=magic[:], scale=inv[:, k:k + 1]).then_inc(done, 1)

            def sigmoid(n, par, before):
                round_(n, 2, g_r)
                hold(act, g_q, n + 1)
                if before:
                    hold(act, g_g2, n - 1)
                nc.scalar.activation(work[:, par], flat(raw, n), ACT.Sigmoid).then_inc(g_sig, 1)

            run_pairs(act, sigmoid)
            act.wait_ge(t_inv, 4)
            with act.Fori(0, NBLK) as n:
                round_(n, 3, p_r)
            act.wait_ge(t_inv, 5)
            with act.Fori(0, NBLK) as n:
                round_(n, 4, o_r)

        @block.vector
        def _(dve):
            def gate(n, par, before):
                hold(dve, g_r, n + 1)
                nc.vector.tensor_scalar(flat(raw, n), flat(raw, n), MAGIC, step[:, 2:3], ALU.subtract, ALU.mult).then_inc(g_q, 1)
                hold(dve, g_sig, n + 1)
                w = work[:, par]
                nc.vector.tensor_scalar(w, w, U16, MAGIC, ALU.mult, ALU.add).then_inc(g_sr, 1)
                hold(dve, g_sr, n + 1)
                nc.vector.tensor_scalar(w, w, MAGIC, U16 - 1.0, ALU.subtract, ALU.min).then_inc(g_sq, 1)
                hold(dve, g_sq, n + 1)
                nc.vector.scalar_tensor_tensor(flat(raw, n), w, 1.0 / U16, flat(raw, n), ALU.mult, ALU.mult).then_inc(g_g2, 1)
                hold(dve, g_g2, n + 1)
                nc.vector.tensor_reduce(amax[:, 3, bass.ds(n, 1)], flat(raw, n), AX.X, ALU.max, apply_absolute_value=True).then_inc(g_a2, 1)

            run_pairs(dve, gate)
            dve.wait_ge(g_a2, NBLK)
            scale_dve(dve, 3)
            with dve.Fori(0, NBLK) as n:
                hold(dve, p_r, n + 1)
                nc.vector.tensor_scalar(flat(raw, n), flat(raw, n), MAGIC, step[:, 3:4], ALU.subtract, ALU.mult).then_inc(p_q, 1)
                hold(dve, p_q, n + 1)
                nc.vector.scalar_tensor_tensor(flat(raw, n), flat(up, n), step[:, 1:2], flat(raw, n), ALU.mult, ALU.mult).then_inc(p_o, 1)
                hold(dve, p_o, n + 1)
                nc.vector.tensor_reduce(amax[:, 4, bass.ds(n, 1)], flat(raw, n), AX.X, ALU.max, apply_absolute_value=True).then_inc(p_a, 1)
            dve.wait_ge(p_a, NBLK)
            scale_dve(dve, 4)

            def down_in(n, par, before):
                hold(dve, o_r, n + 1)
                if before:
                    hold(dve, o_ps, n - 1)
                nc.vector.tensor_scalar(work[:, par], flat(raw, n), MAGIC, step[:, 4:5], ALU.subtract, ALU.mult).then_inc(o_q, 1)

            def finish(n, par, before):
                hold(dve, o_ps, n + 1)
                hold(dve, o_ld[par], 16 * (n // 2 + 1))
                r = res[:, par]
                nc.vector.tensor_tensor(r.rearrange("p q d -> p (q d)"), ps[:, 2 * par:2 * par + 2, :].rearrange("p a n -> p (a n)"),
                                        r.rearrange("p q d -> p (q d)"), ALU.add).then_inc(l_sum, 1)
                norm_stats(dve, 2 * NBLK + n, par, r)
                norm_apply(dve, 2 * NBLK + n, par, r, r).then_inc(o_fin, 1)

            down_in(0, 0, False)
            down_in(1, 1, False)
            finish(0, 0, False)
            with dve.Fori(1, NBLK // 2) as j:
                down_in(2 * j, 0, True)
                finish(2 * j - 1, 1, True)
                down_in(2 * j + 1, 1, True)
                finish(2 * j, 0, True)
            finish(NBLK - 1, 1, True)

        @block.tensor
        def _(pe):
            def down(n, par, before):
                hold(pe, o_q, n + 1)
                if before:
                    hold(pe, l_sum, 2 * NBLK + n - 1)
                for q in range(4):
                    for m in range(FT):
                        last = nc.tensor.matmul(ps[:, 2 * par + q // 2, (q % 2) * D:(q % 2 + 1) * D],
                                                work[:, par, m * HALF + q * P:m * HALF + (q + 1) * P], wdT[:, m, :],
                                                start=(m == 0), stop=(m == FT - 1))
                last.then_inc(o_ps, 1)

            run_pairs(pe, down)


def build(nc, xT, wqT, wkT, wvT, bq, bk, bv, emb, part_of_row, e_lo, e_hi, ident,
          x, woT, bo, ctxT, xwqT, xwkT, xwvT, xbq, xbk, xbv, w_up, w_gate, w_down, out):
    with ExitStack() as sems:
        def sem(name):
            return sems.enter_context(nc.semaphore(name))

        ad = nc.dram_tensor("attn_all", [NIT, L, G * HD], F32, kind="Internal").ap()
        self_attention(nc, sem, ad, xT, wqT, wkT, wvT, bq, bk, bv, emb, part_of_row, e_lo, e_hi, ident)
        decoder_rest(nc, sem, ad, x, ident, woT, bo, ctxT, xwqT, xwkT, xwvT, xbq, xbk, xbv, w_up, w_gate, w_down, out)


def kernel(**inputs):
    import numpy as np
    import concourse.bacc as bacc
    from concourse.bass_utils import run_bass_kernel_spmd

    a = {k: np.asarray(v) for k, v in inputs.items()}
    e = a["L0_attn_dist_emb"]
    part_of_row = np.zeros((KR, 3), np.float32)
    for slot, p in enumerate((0, 0, 0, 1, 1, 2)):
        part_of_row[HD * slot:HD * (slot + 1), p] = 1.0
    ident = np.eye(P, dtype=np.float32)

    def by_dim(w):
        return w.reshape(-1, 2, 2, G, HD).transpose(0, 1, 2, 4, 3).reshape(-1, D)

    arrays = {
        "xT": a["x"].reshape(N, D).T, "wqT": by_dim(a["L0_attn_Wq"].T), "wkT": by_dim(a["L0_attn_Wk"].T), "wvT": a["L0_attn_Wv"].T,
        "bq": by_dim(a["L0_attn_bq"]).reshape(2, P).T, "bk": by_dim(a["L0_attn_bk"]).reshape(2, P).T,
        "bv": np.broadcast_to(a["L0_attn_bv"], (P, D)), "emb": np.tile(e.T, (6, 1)), "part_of_row": part_of_row,
        "e_lo": np.tile(np.repeat(e[0], G), 2).reshape(P, 1), "e_hi": np.tile(np.repeat(e[NJ], G), 2).reshape(P, 1),
        "ident": ident,
        "x": a["x"].reshape(NBLK, HALF, D), "woT": a["L0_attn_Wo"].T, "bo": np.broadcast_to(a["L0_attn_bo"], (P, D)),
        "ctxT": a["ctx_1024"].reshape(B * LC, D).T, "xwqT": a["L0_xattn_Wq"].T, "xwkT": a["L0_xattn_Wk"].T,
        "xwvT": a["L0_xattn_Wv"].T, "xbq": a["L0_xattn_bq"].reshape(2, P).T, "xbk": a["L0_xattn_bk"].reshape(2, P).T,
        "xbv": np.broadcast_to(a["L0_xattn_bv"], (P, D)),
        "w_up": a["L0_ffn_w_up"], "w_gate": a["L0_ffn_w_gate"], "w_down": a["L0_ffn_w_down"],
    }
    nc = bacc.Bacc("TRN2", target_bir_lowering=False, num_devices=1)
    args = []
    for name in arrays:
        arrays[name] = np.ascontiguousarray(arrays[name])
        args.append(nc.dram_tensor(name, arrays[name].shape, mybir.dt.from_np(arrays[name].dtype), kind="ExternalInput").ap())
    args.append(nc.dram_tensor("result", [NBLK, HALF, D], F32, kind="ExternalOutput").ap())
    build(nc, *args)
    r = run_bass_kernel_spmd(nc, [arrays], core_ids=[0])
    return r.results[0]["result"].reshape(B, L, D)
```

```python
import concourse.bass as bass
from concourse import mybir
from contextlib import ExitStack

F32 = mybir.dt.float32
BF16 = mybir.dt.bfloat16
ALU = mybir.AluOpType
ACT = mybir.ActivationFunctionType
AX = mybir.AxisListType

P = 128
B, L, D = 4, 1024, 256
N = B * L
NH, HD = 16, 16
LEFT, RIGHT = 64, 8
NJ = LEFT + RIGHT
G = 4
NIT = B * NH // G
HALF = 512
TL = L // P
PADL = P
TW = PADL + NJ + P
WIN = LEFT + P + RIGHT
ZL = LEFT
STEPS = 32
KR = 6 * HD
NP_BUF = 4
LC = 154
FI = 768
FT = FI // P
NBLK = N // HALF
NSC = 5
EPS = 1e-5
QMAX = 32767.0
U16 = 65536.0
TINY = 1e-12
MAGIC = 1.5 * 2.0 ** 23
RMAX = bass.bass_isa.ReduceOp.max
NR = 4



def self_attention(nc, sem, ad, xT, wqT, wkT, wvT, bq, bk, bv, emb, part_of_row, e_lo, e_hi, ident):
    ctx = ExitStack()
    with ctx:
        def sb(name, shape, dt=F32):
            return ctx.enter_context(nc.sbuf_tensor(name, shape, dt))

        def dram(name, shape, dt=F32):
            return nc.dram_tensor(name, shape, dt, kind="Internal").ap()

        td = [dram(n, [NIT, G * 3 * HD, L], BF16) for n in ("q_parts", "k_lo_parts", "k_hi_parts", "k_mixed_parts")]
        vd = dram("v_all", [NIT, L, P])
        tab = dram("rel_table", [2, G, L, TW])

        psT = ctx.enter_context(nc.psum_tensor("scoresT", [P, 4, HALF], F32))
        psX = ctx.enter_context(nc.psum_tensor("scores_for_max", [P, 2, HALF], F32))
        psO = ctx.enter_context(nc.psum_tensor("attn_out", [P, HALF], F32))
        psM = ctx.enter_context(nc.psum_tensor("misc", [P, HALF], F32))

        idf = sb("idf", [P, P])
        idb = sb("idb", [P, P], BF16)
        embr = sb("embr", [KR, NJ + 1])
        prow = sb("prow", [KR, 3])
        embd = sb("embd", [KR, NJ])
        embt = sb("embt", [KR, 3, NJ])
        embp = sb("embp", [KR, 3, NJ], BF16)
        embS = sb("embS", [KR, NJ], BF16)
        colb = sb("colb", [P, 6])
        colc = sb("colc", [P, 6])

        s_const = sem("s_const")
        s_w = sem("s_w")
        s_pads = sem("s_pads")
        s_zero = sem("s_zero")
        s_prep = sem("s_prep")
        s_ones = sem("s_ones")
        s_bufs = sem("s_bufs")
        a_x = [sem(f"a_x{j}") for j in range(2)]
        a_full = sem("a_full")
        a_val = sem("a_val")
        a_hi_val = sem("a_hi_val")
        a_high = sem("a_high")
        a_rem = sem("a_rem")
        a_mid = sem("a_mid")
        a_low = sem("a_low")
        a_v = sem("a_v")
        a_mix = sem("a_mix")
        a_out = [sem(f"a_out{j}") for j in range(2)]
        ld_q = [sem(f"ld_q{i}") for i in range(2)]
        ld_k = [sem(f"ld_k{i}") for i in range(2)]
        ld_lo = [sem(f"ld_lo{i}") for i in range(2)]
        ld_hi = [sem(f"ld_hi{i}") for i in range(2)]
        ld_r = [sem(f"ld_r{i}") for i in range(2)]
        t_wr = [sem(f"t_wr{i}") for i in range(NR)]
        st_done = sem("st_done")
        exp_done = sem("exp_done")
        pv_done = sem("pv_done")
        mx_full = sem("mx_full")
        mx_free = sem("mx_free")
        m_ready = sem("m_ready")
        m_turned = sem("m_turned")
        qm_ready = sem("qm_ready")
        r_full = sem("r_full")
        r_rows = sem("r_rows")
        r_padded = sem("r_padded")
        wb_ready = sem("wb_ready")
        o_copied = sem("o_copied")
        o_turned = sem("o_turned")
        o_rec = sem("o_rec")
        m_small = sem("m_small")
        an_ready = sem("an_ready")
        an_out = sem("an_out")
        s_held = sem("s_held")
        s_dve = sem("s_dve")

        with ExitStack() as early:
            def sbe(name, shape, dt=F32):
                return early.enter_context(nc.sbuf_tensor(name, shape, dt))
            zero = sbe("zero", [P, TL * P])
            wq = sbe("wq", [P, 2, D])
            wk = sbe("wk", [P, 2, D])
            wv = sbe("wv", [P, 2, D])
            bvt = sbe("bvt", [P, D])
            xs = sbe("xs", [P, 2, 2, HALF])
            val = sbe("val", [P, 2, 6, HALF])
            rem = sbe("rem", [P, 2, 6, HALF])
            part = sbe("part", [P, 2, 8, 3, HALF], BF16)
            vs = sbe("vs", [P, 2, 4, NH, 32])

        qT = sb("qT", [P, 2, G, L], BF16)
        qR = sb("qR", [P, 2, G, L], BF16)
        kT = sb("kT", [P, 2, 3, G, L], BF16)
        vS = sb("vS", [P, 2, TL, P])
        win = sb("win", [P, 2, TL, G, ZL + WIN])
        winb = sb("winb", [P, 2, TL // 2, G, WIN], BF16)
        rows = sb("rows", [P, NR, G, PADL + NJ])
        pr = sb("pr", [P, NP_BUF, 2 * HALF])
        nmax = sb("nmax", [P, 2, 4, 2, G])
        mval = sb("mval", [P, G])
        mcol = sb("mcol", [P, G, 32], BF16)
        ot = sb("ot", [P, HALF])
        orec = sb("orec", [P, 16])
        an = sb("an", [P, 4, G * HD])

        block = ctx.enter_context(nc.Block())
        NCONST = 8
        NPADS = 2 * G
        A_DMAS = 16 + 4
        LQ, LK, LW = 3, 10, 4

        def row(t, i):
            return t[bass.ds(i, 1)].rearrange("a p n -> (a p) n")

        def pieces(cuts, hf):
            lo, hi = hf * HALF, (hf + 1) * HALF
            return [(max(a, lo), min(b, hi), v) for a, b, v in cuts if max(a, lo) < min(b, hi)]

        def by_query(kt, hf):
            return pieces([(0, (kt + 1) * P, 1), ((kt + 1) * P, (kt + 2) * P, 2), ((kt + 2) * P, L, 0)], hf)

        def by_key(qt, hf):
            return pieces([(0, (qt - 1) * P, 0), ((qt - 1) * P, qt * P, 2), (qt * P, L, 1)], hf)

        R_STEPS = {1: 0, 5: 1, 9: 2, 13: 3}
        M_STEPS = {2: 0, 6: 1, 10: 2, 14: 3}
        N_STEP = 4
        LEAD = 6
        T_CH = 32

        def chunks_at(t):
            return [((LEAD + 2 * t + e) // T_CH, (LEAD + 2 * t + e) % T_CH) for e in range(2)]

        def run_blocks(eng, block_of):
            block_of(0, 0, False, False)
            block_of(0, 1, True, False)
            with eng.Fori(1, B) as b:
                block_of(b, 0, True, True)
                block_of(b, 1, True, True)

        def hold(eng, s, value):
            eng.wait_ge(s, value)
            eng.sem_inc(s_held, 1)

        def run_groups(eng, group):
            group(0, 0, 0, first=True)
            with eng.Fori(0, 6) as j:
                group(1 + 2 * j, 1, j)
                group(2 + 2 * j, 0, j + 1)
            group(13, 1, 6, ahead=False)
            group(14, 0, 7, rel=False, ahead=False)
            group(15, 1, 7, rel=False, last=True, ahead=False)

        @block.sync
        def _(sp):
            def load_x(b, hf, again=True):
                k = 2 * b + hf
                if again:
                    hold(sp, a_full, 6 * (k - 1))
                sp.dma_start(xs[:, hf], xT[:, bass.ds(k * HALF, HALF)].rearrange("(c p) n -> p c n", p=P)).then_inc(a_x[hf], 16)

            load_x(0, 0, False)
            for dst, src in ((wq, wqT.rearrange("(c p) n -> p c n", p=P)),
                             (wk, wkT.rearrange("(c p) n -> p c n", p=P)),
                             (wv, wvT.rearrange("(c p) n -> p c n", p=P))):
                sp.dma_start(dst[:], src).then_inc(s_w, 16)
            for dst, src in ((idf, ident), (prow, part_of_row), (embr, emb), (colb[:, 0:2], bq), (colb[:, 2:4], bk),
                             (colb[:, 4:5], e_lo), (colb[:, 5:6], e_hi), (bvt, bv)):
                sp.dma_start(dst[:], src).then_inc(s_const, 16)
            sp.wait_ge(s_zero, 1)
            for p in range(2):
                for h in range(G):
                    sp.dma_start(tab[p, h].rearrange("(t p) n -> p t n", p=P)[:, :, PADL + NJ:TW],
                                 zero[:, :].rearrange("p (t n) -> p t n", n=P)).then_inc(s_pads, 16)

            def store_values(b, hf):
                k = 2 * b + hf
                hold(sp, a_v, 2 * k + 2)
                for g in range(4):
                    dst = vd[bass.ds(4 * b + g, 1), hf * HALF:(hf + 1) * HALF, :].rearrange("i (t p) n -> (i p) t n", p=P)
                    sp.dma_start(dst, vs[:, hf, :, 4 * g:4 * g + 4, :].rearrange("p t h r -> p t (h r)")).then_inc(a_out[hf], 16)

            def store_parts(b, hf):
                k = 2 * b + hf
                for n in range(8):
                    if n == 6:
                        store_values(b, hf)
                    if n < 6:
                        hold(sp, a_low, 6 * k + n + 1)
                    else:
                        hold(sp, a_mix, 4 * k + 2 * (n - 6) + 2)
                    for g in range(2):
                        dst = row(td[n // 2], 4 * b + 2 * (n % 2) + g)[:, hf * HALF:(hf + 1) * HALF]
                        sp.dma_start(dst.rearrange("(t r) n -> r t n", t=3),
                                     part[g * G * HD:(g + 1) * G * HD, hf, n, :, :]).then_inc(a_out[hf], 16)
            load_x(0, 1, False)
            store_parts(0, 0)
            with sp.Fori(1, B) as b:
                load_x(b, 0)
                store_parts(b - 1, 1)
                load_x(b, 1)
                store_parts(b, 0)
            store_parts(B - 1, 1)
            for hf in range(2):
                sp.wait_ge(a_out[hf], 16 * A_DMAS * B)
            sp.wait_ge(s_pads, 16 * NPADS)

            def load_q(dst, i, s):
                t = row(td[0], i).rearrange("(r h) n -> r (h n)", h=G)
                for r0, n in ((0, 3), (3, 2), (5, 1)):
                    sp.dma_start(dst[HD * r0:HD * (r0 + n)].rearrange("p h n -> p (h n)"), t[0:HD * n]).then_inc(s, 16)

            def load_k(dst, t, i, s):
                t = row(t, i)
                for p, r0, n in ((0, 0, 3), (1, 3, 2), (2, 5, 1)):
                    src = t[p * HD * G:(p + 1) * HD * G].rearrange("(r h) n -> r (h n)", h=G)
                    sp.dma_start(dst[HD * r0:HD * (r0 + n)].rearrange("p h n -> p (h n)"),
                                 src.unsqueeze(0).to_broadcast([n, HD, G * L])).then_inc(s, 16)

            def load_rel_q(i, par):
                load_q(qR[:, par], i, ld_r[par])

            def load_qk(i, par):
                load_q(qT[:, par], i, ld_q[par])
                for v in range(3):
                    load_k(kT[:, par, v], td[1 + v], i, ld_k[par])

            def load_v(i, par):
                sp.dma_start(vS[:, par, :, :], row(vd, i).rearrange("(t p) n -> p t n", p=P)).then_inc(ld_k[par], 16)

            def load_windows(par, part):
                for h in range(G):
                    first = ((par * G + h) * L + part * HALF) * TW + P
                    src = bass.AP(tab.tensor, first, [[TW - 1, P], [P * TW, 4], [1, WIN]])
                    sp.dma_start(win[:, par, 4 * part:4 * part + 4, h, ZL:], src).then_inc((ld_lo, ld_hi)[part][par], 16)

            def store_rows(n, par, qt):
                hold(sp, r_padded, n + 1)
                dst = tab[par].rearrange("h (t p) n -> t p h n", p=P)[qt, :, :, 0:PADL + NJ]
                sp.dma_start(dst, rows[:, qt % NR, :, :]).then_inc(t_wr[qt % NR], 16)

            def store_attn(i, hf, m):
                hold(sp, an_ready, m + 1)
                dst = row(ad, i)[hf * HALF:(hf + 1) * HALF, :].rearrange("(t p) n -> p t n", p=P)
                sp.dma_start(dst, an[:]).then_inc(an_out, 16)

            load_rel_q(0, 0)
            load_rel_q(1, 1)
            load_q(qT[:, 0], 0, ld_q[0])
            for i in range(2):
                for qt in range(TL):
                    store_rows(TL * i + qt, i, qt)
                    if i == 0 and qt in (1, 3, 5):
                        load_k(kT[:, 0, qt // 2], td[1 + qt // 2], 0, ld_k[0])
                if i == 0:
                    for p in range(NR):
                        sp.wait_ge(t_wr[p], 16 * (TL // NR))
                    load_windows(0, 0)
                    load_windows(0, 1)
            load_v(0, 0)
            load_rel_q(2, 0)

            def group(i, par, k, first=False, rel=True, last=False, ahead=True):
                if not last:
                    if not first:
                        hold(sp, pv_done, STEPS * i)
                    for p in range(NR):
                        hold(sp, t_wr[p], 16 * (TL // NR) * (i + 2))
                    load_windows(1 - par, 0)
                    load_qk(i + 1, 1 - par)
                if rel:
                    hold(sp, ld_lo[par], 16 * LW * (k + 1))
                    hold(sp, ld_hi[par], 16 * LW * (k + 1))
                for hf in range(2):
                    for t in range(16):
                        if t == N_STEP + 1 and not (first and hf == 0):
                            store_attn(i if hf else i - 1, 1 - hf, 2 * i + hf - 1)
                        if t in R_STEPS and rel:
                            qt = 4 * hf + R_STEPS[t]
                            store_rows(TL * (i + 2) + qt, par, qt)
                        if hf == 0 and not last:
                            if t == 6:
                                load_windows(1 - par, 1)
                            if t == 10:
                                load_v(i + 1, 1 - par)
                        if hf == 0 and t == 12 and ahead:
                            hold(sp, r_full, TL * (i + 2))
                            load_rel_q(i + 3, 1 - par)

            run_groups(sp, group)
            store_attn(NIT - 1, 1, 2 * NIT - 1)
            sp.wait_ge(an_out, 16 * 2 * NIT)

        @block.gpsimd
        def _(pool):
            nc.gpsimd.memset(zero[:], 0.0).then_inc(s_zero, 1)
            nc.gpsimd.memset(vs[:], 0.0).then_inc(s_ones, 1)
            pool.wait_ge(s_ones, 1)
            nc.gpsimd.memset(vs[:, :, :, :, HD:HD + 1], 1.0).then_inc(s_ones, 1)

            def mix_keys(b, hf, before, again):
                k = 2 * b + hf
                if again:
                    hold(pool, a_out[hf], 16 * A_DMAS * b)
                for m in range(2):
                    for v in range(2):
                        hold(pool, a_low, 6 * k + 3 + 2 * v + m)
                        halves = [part[:, hf, n, :, :].rearrange("p t (q n) -> p (t q) n", n=P)[:, :, v * ZL:(v + 1) * ZL]
                                  for n in (6 + m, 2 + 2 * v + m)]
                        nc.gpsimd.tensor_copy(halves[0], halves[1]).then_inc(a_mix, 1)

            run_blocks(pool, mix_keys)

            def pad_rows(n, qt):
                hold(pool, r_rows, n + 1)
                nc.gpsimd.tensor_copy(rows[:, qt % NR, :, 0:PADL],
                                      rows[:, qt % NR, :, PADL:PADL + 1].to_broadcast([P, G, PADL])).then_inc(r_padded, 1)

            def cast_window(T, par, k, part, q4, wait_use=True):
                hold(pool, (ld_lo, ld_hi)[part][par], 16 * LW * (k + 1))
                if wait_use:
                    hold(pool, mx_full, T_CH * (T - 2) + 8 * (q4 + 1))
                nc.gpsimd.tensor_copy(winb[:, part, q4, :, :], win[:, par, 4 * part + q4, :, ZL:]).then_inc(wb_ready, 1)

            for i in range(2):
                for qt in range(TL):
                    pad_rows(TL * i + qt, qt)
            for q4 in range(4):
                cast_window(0, 0, 0, 0, q4, False)
            cast_window(1, 0, 0, 1, 0, False)

            def group(i, par, k, first=False, rel=True, last=False, ahead=True):
                for hf in range(2):
                    T = 2 * i + hf
                    for t in range(16):
                        if t in (0, 3, 6) and not (last and hf):
                            tp, tk = (par, k) if hf == 0 else (1 - par, k + par)
                            cast_window(T + 1, tp, tk, 1 - hf, 1 + t // 3, not first or hf == 1)
                        if t == 12 and not last:
                            cast_window(T + 2, 1 - par, k + par, hf, 0)
                        if t in R_STEPS and rel:
                            qt = 4 * hf + R_STEPS[t]
                            pad_rows(TL * (i + 2) + qt, qt)

            run_groups(pool, group)

        @block.scalar
        def _(act):
            act.wait_ge(s_prep, 3)

            def project(b, hf, before, again):
                k = 2 * b + hf
                if again:
                    act.wait_ge(a_out[hf], 16 * A_DMAS * b)
                    act.wait_ge(a_low, 6 * (k - 1))

                def value(n):
                    act.wait_ge(a_full, 6 * k + 1 + n)
                    nc.scalar.activation(val[:, hf, n, :], psT[:, n, :], ACT.Identity, bias=colc[:, n:n + 1],
                                         scale=0.25 if n < 2 else 1.0).then_inc(a_val, 1)

                def high(n):
                    if n < 4:
                        act.wait_ge(a_val, 4 * k + 1 + n)
                    else:
                        act.wait_ge(a_hi_val, 2 * k + n - 3)
                    nc.scalar.activation(part[:, hf, n, 0, :], val[:, hf, n, :], ACT.Copy).then_inc(a_high, 1)

                def middle(n):
                    act.wait_ge(a_rem, 6 * k + 1 + n)
                    nc.scalar.activation(part[:, hf, n, 1, :], rem[:, hf, n, :], ACT.Copy).then_inc(a_mid, 1)

                value(0)
                value(1)
                high(0)
                high(1)
                value(2)
                value(3)
                for n in range(2, 6):
                    middle(n - 2)
                    high(n)
                middle(4)
                middle(5)

            run_blocks(act, project)
            for hf in range(2):
                act.wait_ge(a_out[hf], 16 * A_DMAS * B)
            act.wait_ge(s_pads, 16 * NPADS)

            def copy_rows(n, qt, tw):
                act.wait_ge(r_full, n + 1)
                act.wait_ge(t_wr[qt % NR], 16 * tw)
                nc.scalar.activation(rows[:, qt % NR, :, PADL:PADL + NJ],
                                     psM[:, 0:G * NJ].rearrange("p (h n) -> p h n", h=G), ACT.Copy).then_inc(r_rows, 1)

            def exps(i, s, first):
                act.wait_ge(st_done, STEPS * i + s + 1)
                if not (first and s < NP_BUF):
                    act.wait_ge(pv_done, STEPS * i + s + 1 - NP_BUF)
                hp = s % 2
                nc.scalar.activation(pr[:, s % NP_BUF, :], psT[:, 2 * hp:2 * hp + 2, :].rearrange("p a n -> p (a n)"),
                                     ACT.Exp).then_inc(exp_done, 1)

            def copy_out(T):
                act.wait_ge(pv_done, 16 * (T + 1))
                if not (isinstance(T, int) and T == 0):
                    act.wait_ge(o_turned, T)
                nc.scalar.activation(ot[:], psO[:], ACT.Copy).then_inc(o_copied, 1)

            for i in range(2):
                for qt in range(TL):
                    copy_rows(TL * i + qt, qt, TL // NR * i + qt // NR)

            def group(i, par, k, first=False, rel=True, last=False, ahead=True):
                for hf in range(2):
                    for t in range(16):
                        exps(i, 16 * hf + t, first)
                        if t == 2 and not (first and hf == 0):
                            copy_out(2 * i + hf - 1)
                        if t in R_STEPS and rel:
                            qt = 4 * hf + R_STEPS[t]
                            copy_rows(TL * (i + 2) + qt, qt, TL // NR * (i + 2) + qt // NR)

            run_groups(act, group)
            copy_out(2 * NIT - 1)

        @block.vector
        def _(dve):
            small = [0]

            def link(ins):
                small[0] += 1
                ins.then_inc(s_dve, 1)
                dve.wait_ge(s_dve, small[0])

            dve.wait_ge(s_const, 16 * NCONST)
            nc.vector.tensor_scalar(colc[:, 0:2], colb[:, 0:2], 0.25, None, ALU.mult).then_inc(s_prep, 1)
            nc.vector.tensor_scalar(colc[:, 2:4], colb[:, 2:4], colb[:, 4:5], None, ALU.add).then_inc(s_prep, 1)
            nc.vector.tensor_scalar(colc[:, 4:6], colb[:, 2:4], colb[:, 5:6], None, ALU.add).then_inc(s_prep, 1)
            link(nc.vector.tensor_tensor(embd[:], embr[:, 0:NJ], embr[:, NJ:NJ + 1].to_broadcast([KR, NJ]), ALU.subtract))
            left = embd[:]
            for p in range(3):
                link(nc.vector.tensor_copy(embp[:, p, :], left))
                if p < 2:
                    link(nc.vector.tensor_tensor(embt[:, p, :], left, embp[:, p, :], ALU.subtract))
                    left = embt[:, p, :]
            link(nc.vector.tensor_scalar(embt[:, 2, :], embp[:, 0, :], prow[:, 0:1], None, ALU.mult))
            link(nc.vector.scalar_tensor_tensor(embt[:, 0, :], embp[:, 1, :], prow[:, 1:2], embt[:, 2, :], ALU.mult, ALU.add))
            link(nc.vector.scalar_tensor_tensor(embS[:], embp[:, 2, :], prow[:, 2:3], embt[:, 0, :], ALU.mult, ALU.add))
            nc.vector.tensor_copy(idb[:], idf[:]).then_inc(s_prep, 1)
            dve.wait_ge(s_ones, 2)

            def project(b, hf, before, again):
                k = 2 * b + hf
                if again:
                    dve.wait_ge(a_out[hf], 16 * A_DMAS * b)
                    dve.wait_ge(a_mid, 6 * (k - 1))

                def k_hi(m):
                    dve.wait_ge(a_val, 4 * k + 3 + m)
                    nc.vector.tensor_scalar(val[:, hf, 4 + m, :], psT[:, 2 + m, :], colc[:, 4 + m:5 + m], None,
                                            ALU.add).then_inc(a_hi_val, 1)

                def remainder(n):
                    dve.wait_ge(a_high, 6 * k + 1 + n)
                    nc.vector.tensor_tensor(rem[:, hf, n, :], val[:, hf, n, :], part[:, hf, n, 0, :], ALU.subtract).then_inc(a_rem, 1)

                def low(n):
                    dve.wait_ge(a_mid, 6 * k + 1 + n)
                    nc.vector.tensor_tensor(part[:, hf, n, 2, :], rem[:, hf, n, :], part[:, hf, n, 1, :], ALU.subtract).then_inc(a_low, 1)

                remainder(0)
                remainder(1)
                k_hi(0)
                k_hi(1)
                for v in range(2):
                    dve.wait_ge(a_full, 6 * k + 5 + v)
                    for e in range(2):
                        last = nc.vector.tensor_tensor(
                            vs[:, hf, 2 * v + e, :, 0:HD],
                            psX[:, v, e * D:(e + 1) * D].rearrange("p (h d) -> p h d", d=HD),
                            bvt[:].rearrange("p (h d) -> p h d", d=HD), ALU.add)
                    last.then_inc(a_v, 1)
                for n in range(2, 6):
                    low(n - 2)
                    remainder(n)
                low(4)
                low(5)

            run_blocks(dve, project)
            for hf in range(2):
                dve.wait_ge(a_out[hf], 16 * A_DMAS * B)
            dve.wait_ge(s_pads, 16 * NPADS)
            for par in range(2):
                nc.vector.memset(win[:, par, :, :, 0:ZL], 0.0).then_inc(s_bufs, 1)
            nc.vector.memset(mcol[:], 0.0).then_inc(s_bufs, 1)
            for par in range(2):
                nc.vector.memset(kT[KR:KR + 2, par], 1.0).then_inc(s_bufs, 1)

            def reduce(T, part, c, q4, kh, h):
                n = T_CH * T + c
                dve.wait_ge(mx_full, n + 1)
                nc.vector.tensor_reduce(nmax[:, part, q4, kh, h:h + 1], psX[:, c % 2, :], AX.X, ALU.max,
                                        negate=True).then_inc(mx_free, 1)
                if c % 8 == 7:
                    m = 4 * T + q4
                    dve.wait_ge(mx_free, n + 1)
                    nc.vector.tensor_tensor(mval[:], nmax[:, part, q4, 0, :], nmax[:, part, q4, 1, :],
                                            ALU.min).then_inc(m_small, 1)
                    if not (isinstance(T, int) and m == 0):
                        dve.wait_ge(m_turned, m)
                    dve.wait_ge(m_small, 2 * m + 1)
                    nc.vector.tensor_copy(mcol[:, :, 0], mval[:]).then_inc(m_small, 1)
                    dve.wait_ge(m_small, 2 * m + 2)
                    nc.vector.tensor_tensor(mcol[:, :, 1], mval[:], mcol[:, :, 0], ALU.subtract).then_inc(m_ready, 1)

            def chunk(T, part, c):
                reduce(T, part, c, c // 8, c // 4 % 2, c % 4)

            def place_max(T, par, part, q4, i):
                dve.wait_ge(m_turned, 4 * T + q4 + 1)
                if i is not None:
                    dve.wait_ge(st_done, 16 * (T - 1))
                to = qT[96:98, par, :, part * HALF + q4 * P:part * HALF + (q4 + 1) * P]
                nc.vector.tensor_copy(to, psM[96:98, :].rearrange("p (h n) -> p h n", h=G)).then_inc(qm_ready, 1)

            def normalise(T):
                dve.wait_ge(o_turned, T + 1)
                o = psM[:].rearrange("p (g r) -> p g r", r=32)
                nc.vector.reciprocal(orec[:], o[:, :, HD]).then_inc(o_rec, 1)
                dve.wait_ge(o_rec, T + 1)
                if not (isinstance(T, int) and T == 0):
                    dve.wait_ge(an_out, 16 * T)
                nc.vector.tensor_tensor(an[:].rearrange("p q (h d) -> p (q h) d", d=HD), o[:, :, 0:HD],
                                        orec[:].unsqueeze(2).to_broadcast([P, 16, HD]), ALU.mult).then_inc(an_ready, 1)

            for c in range(T_CH):
                chunk(0, 0, c)
                if c % 8 == 7:
                    place_max(0, 0, 0, c // 8, None)
            for c in range(LEAD):
                chunk(1, 1, c)

            def group(i, par, k, first=False, rel=True, last=False, ahead=True):
                for hf in range(2):
                    T = 2 * i + hf
                    for t in range(16):
                        if t == N_STEP + 1 and not (first and hf == 0):
                            normalise(T - 1)
                        for ahead, c in chunks_at(t):
                            if not (last and hf + ahead >= 1):
                                chunk(T + 1 + ahead, (hf + 1 + ahead) % 2, c)
                        if t in M_STEPS and not (last and hf):
                            place_max(T + 1, par if hf == 0 else 1 - par, 1 - hf, M_STEPS[t], None if first and hf == 0 else i)

            run_groups(dve, group)
            normalise(2 * NIT - 1)

        @block.tensor
        def _(pe):
            mm = nc.tensor.matmul
            pe.wait_ge(s_w, 16 * 3)

            def project(b, hf, before, again):
                k = 2 * b + hf
                pe.wait_ge(a_x[hf], 16 * (b + 1))
                if before:
                    pe.wait_ge(a_val, 4 * k)
                for w, bank in ((wq, 0), (wk, 2)):
                    if bank and before:
                        pe.wait_ge(a_hi_val, 2 * k)
                    for m in range(2):
                        for c in range(2):
                            last = mm(psT[:, bank + m, :], w[:, c, m * P:(m + 1) * P], xs[:, hf, c, :],
                                      start=(c == 0), stop=(c == 1))
                        last.then_inc(a_full, 1)
                if before:
                    pe.wait_ge(a_v, 2 * k)
                for v in range(2):
                    for e in range(2):
                        t = 2 * v + e
                        for c in range(2):
                            last = mm(psX[:, v, e * D:(e + 1) * D], xs[:, hf, c, t * P:(t + 1) * P], wv[:, c, :],
                                      start=(c == 0), stop=(c == 1))
                    last.then_inc(a_full, 1)

            run_blocks(pe, project)
            pe.wait_ge(a_val, 8 * B)
            pe.wait_ge(a_hi_val, 4 * B)
            pe.wait_ge(a_v, 4 * B)

            def misc_bank(R, M, O):
                pe.wait_ge(r_rows, R)
                if M is not None:
                    pe.wait_ge(qm_ready, M)
                if O is not None:
                    pe.wait_ge(an_ready, O)

            def make_rows(n, par, k, qt, M, O=None):
                if qt == 0:
                    pe.wait_ge(ld_r[par], 16 * LQ * (k + 1))
                misc_bank(n, M, O)
                for h in range(G):
                    last = mm(psM[:, h * NJ:(h + 1) * NJ], qR[0:KR, par, h, qt * P:(qt + 1) * P], embS[:],
                              start=True, stop=True)
                last.then_inc(r_full, 1)

            def max_chunk(T, part, par, k, c, begun=True):
                q4, kh, h = c // 8, c // 4 % 2, c % 4
                qt = 4 * part + q4
                if c == 0:
                    pe.wait_ge(ld_q[par], 16 * LQ * (k + 1))
                    pe.wait_ge(ld_k[par], 16 * LK * (k + 1))
                if c % 8 == 0:
                    pe.wait_ge(wb_ready, 4 * T + q4 + 1)
                if begun:
                    pe.wait_ge(mx_free, T_CH * T + c - 1)
                lo = kh * HALF
                bank = psX[:, c % 2, :]
                ps = by_key(qt, kh)
                w0, w1 = max(qt * P - LEFT, lo), min(qt * P + P + RIGHT, lo + HALF)
                near = w0 < w1
                for n, (a, e, v) in enumerate(ps):
                    last = mm(bank[:, a - lo:e - lo], qT[0:KR, par, h, qt * P:(qt + 1) * P], kT[0:KR, par, v, h, a:e],
                              start=(n == 0), stop=not near and n == len(ps) - 1, skip_group_check=True)
                if near:
                    u = w0 - (qt * P - LEFT)
                    last = mm(bank[:, w0 - lo:w1 - lo], idb[:], winb[:, part, q4, h, u:u + w1 - w0],
                              start=False, stop=True, skip_group_check=True)
                last.then_inc(mx_full, 1)

            def turn_max(m, R, O=None):
                pe.wait_ge(m_ready, m + 1)
                misc_bank(R, m, O)
                for h in range(G):
                    last = mm(psM[96:P, h * P:(h + 1) * P], mcol[:, h, :], idb[:], start=True, stop=True)
                last.then_inc(m_turned, 1)

            def scores(i, par, s, first):
                hf, kt, hp = s // 16, s % 16 // 2, s % 2
                if s % 16 == 0:
                    pe.wait_ge(qm_ready, 4 * (2 * i + hf + 1))
                if not (first and s < 2):
                    pe.wait_ge(exp_done, STEPS * i + s - 1)
                lo = hf * HALF
                ps = by_query(kt, hf)
                near = [(qt, c0, w) for qt, c0, w in ((kt + 1, 0, P), (kt, P, P), (kt - 1, 2 * P, RIGHT))
                        if 4 * hf <= qt < 4 * hf + 4]
                for n, (a, e, v) in enumerate(ps):
                    for h in (2 * hp, 2 * hp + 1):
                        last = mm(psT[:, h, a - lo:e - lo], kT[0:KR + 2, par, v, h, kt * P:(kt + 1) * P], qT[0:KR + 2, par, h, a:e],
                                  start=(n == 0), stop=not near and n == len(ps) - 1, skip_group_check=True)
                for n, (qt, c0, w) in enumerate(near):
                    for h in (2 * hp, 2 * hp + 1):
                        if w == P:
                            last = mm(psT[:, h, qt * P - lo:(qt + 1) * P - lo], win[:, par, qt, h, c0:c0 + w], idf[:],
                                      is_transpose=True, start=False, stop=n == len(near) - 1, skip_group_check=True)
                        else:
                            last = mm(psT[0:w, h, (qt + 1) * P - w - lo:(qt + 1) * P - lo], win[:, par, qt, h, c0:c0 + w],
                                      idf[:, P - w:P], start=False, stop=n == len(near) - 1, skip_group_check=True)
                last.then_inc(st_done, 1)

            def weigh(i, par, s, first):
                hf, kt, hp = s // 16, s % 16 // 2, s % 2
                pe.wait_ge(exp_done, STEPS * i + s + 1)
                if s % 16 == 0 and not (first and hf == 0):
                    pe.wait_ge(o_copied, 2 * i + hf)
                for e in range(2):
                    h = 2 * hp + e
                    last = mm(psO[32 * h:32 * h + 32, :], vS[:, par, kt, 32 * h:32 * h + 32],
                              pr[:, s % NP_BUF, e * HALF:(e + 1) * HALF], start=(kt == 0), stop=(kt == TL - 1))
                last.then_inc(pv_done, 1)

            def turn_out(T, R, M, O=None):
                pe.wait_ge(o_copied, T + 1)
                misc_bank(R, M, O)
                for q in range(4):
                    last = nc.tensor.transpose(psM[:, q * P:(q + 1) * P], ot[:, q * P:(q + 1) * P], idf[:])
                last.then_inc(o_turned, 1)

            pe.wait_ge(s_prep, 4)
            for i in range(2):
                for qt in range(TL):
                    make_rows(TL * i + qt, i, 0, qt, None)
            pe.wait_ge(s_bufs, 3)
            for c in range(T_CH):
                max_chunk(0, 0, 0, 0, c, c >= 2)
                if c % 8 == 7:
                    turn_max(c // 8, 2 * TL)
            for c in range(LEAD):
                max_chunk(1, 1, 0, 0, c)
            pe.wait_ge(s_bufs, 5)

            def group(i, par, k, first=False, rel=True, last=False, ahead=True):
                for hf in range(2):
                    T = 2 * i + hf
                    for t in range(16):
                        s = 16 * hf + t
                        scores(i, par, s, first)
                        for ahead, c in chunks_at(t):
                            if not (last and hf + ahead >= 1):
                                same = hf + 1 + ahead < 2
                                max_chunk(T + 1 + ahead, (hf + 1 + ahead) % 2, par if same else 1 - par,
                                          k if same else k + par, c)
                        if s >= 2:
                            weigh(i, par, s - 2, first)
                        elif not first:
                            weigh(i - 1, 1 - par, STEPS + s - 2, False)
                        outs = None if first and hf == 0 or first and t <= N_STEP else T if t > N_STEP else T - 1
                        tabs = TL * (i + 2) + 4 * hf + sum(u < t for u in R_STEPS) if rel else TL * NIT
                        turns = 4 * (T + 1) + sum(u < t for u in M_STEPS) if not (last and hf) else 8 * NIT
                        if t in R_STEPS and rel:
                            qt = 4 * hf + R_STEPS[t]
                            make_rows(tabs, par, k + 1, qt, turns, outs)
                        if t in M_STEPS and not (last and hf):
                            turn_max(turns, tabs, outs)
                        if t == N_STEP and not (first and hf == 0):
                            turn_out(T - 1, tabs, turns, outs)

            run_groups(pe, group)
            weigh(NIT - 1, 1, STEPS - 2, False)
            weigh(NIT - 1, 1, STEPS - 1, False)
            turn_out(2 * NIT - 1, TL * NIT, 8 * NIT, 2 * NIT - 1)



def decoder_rest(nc, sem, ad, x, ident, woT, bo, ctxT, xwqT, xwkT, xwvT, xbq, xbk, xbv, w_up, w_gate, w_down, out):
    h2d = nc.dram_tensor("second_norm", [NBLK, HALF, D], F32, kind="Internal").ap()
    ud = nc.dram_tensor("up_raw", [NBLK, P, FT * HALF], F32, kind="Internal").ap()
    s_held = sem("f_held")

    def hold(eng, s, value):
        eng.wait_ge(s, value)
        eng.sem_inc(s_held, 1)

    def tokens(t, n):
        return t[bass.ds(n, 1)].rearrange("a (q p) d -> p (a q) d", p=P)

    with ExitStack() as ctx:
        def sb(name, shape, dt=F32):
            return ctx.enter_context(nc.sbuf_tensor(name, shape, dt))

        idf = sb("ident_f", [P, P])
        wuT = sb("w_upT", [P, 2, FI])
        wgT = sb("w_gateT", [P, 2, FI])
        wdT = sb("w_downT", [P, FT, D])
        neg_half = sb("neg_half", [P, 1])
        amax = sb("amax", [P, NSC, NBLK])
        top = sb("top", [P, NSC])
        top_all = sb("top_all", [P, NSC])
        step = sb("step", [P, NSC])
        inv = sb("inv", [P, NSC])
        stats = sb("stats", [P, 2, 4, 6])
        mv = sb("mean_var", [P, 2, 4, 2])
        rstd = sb("rstd", [P, 2, 4])
        magic = sb("magic", [P, 2])
        coarse = sb("coarse", [P, 1])
        ps = ctx.enter_context(nc.psum_tensor("banks", [P, 8, HALF], F32))

        l_sum = sem("l_sum")
        l_stat = sem("l_stat")
        l_aggr = sem("l_aggr")
        l_eps = sem("l_eps")
        l_rstd = sem("l_rstd")
        s_half = sem("s_half")
        t_top = sem("t_top")
        t_all = sem("t_all")
        t_step = sem("t_step")
        t_coarse = sem("t_coarse")
        t_inv = sem("t_inv")

        def norm_stats(dve, i, hf, h):
            hold(dve, l_sum, i + 1)
            for q in range(4):
                last = nc.vector.bn_stats(stats[:, hf, q, :], h[:, q, :])
            last.then_inc(l_stat, 1)
            hold(dve, l_stat, i + 1)
            for q in range(4):
                last = nc.vector.bn_aggr(mv[:, hf, q, :], stats[:, hf, q, :])
            last.then_inc(l_aggr, 1)

        def norm_rstd(pool, i, hf):
            hold(pool, l_aggr, i + 1)
            nc.gpsimd.tensor_scalar(rstd[:, hf, :], mv[:, hf, :, 1], EPS, None, ALU.add).then_inc(l_eps, 1)
            hold(pool, l_eps, i + 1)
            nc.gpsimd.tensor_tensor(rstd[:, hf, :], rstd[:, hf, :], neg_half[:].to_broadcast([P, 4]),
                                    ALU.pow).then_inc(l_rstd, 1)

        def norm_apply(dve, i, hf, h, to):
            hold(dve, l_rstd, i + 1)
            for q in range(4):
                last = nc.vector.tensor_scalar(to[:, q, :], h[:, q, :], mv[:, hf, q, 0:1], rstd[:, hf, q:q + 1],
                                               ALU.subtract, ALU.mult)
            return last

        def scale_of(dve, k, unit=1.0, coarse=None):
            nc.vector.tensor_reduce(top[:, k:k + 1], amax[:, k, :], AX.X, ALU.max).then_inc(t_top, 1)
            dve.wait_ge(t_all, k + 1)
            largest = top_all[:, k:k + 1]
            if coarse is not None:
                nc.vector.tensor_tensor(largest, largest, coarse, ALU.mult).then_inc(t_coarse, 1)
                dve.wait_ge(t_coarse, 2)
            nc.vector.tensor_scalar(step[:, k:k + 1], largest, 1.0 / QMAX, TINY * unit, ALU.mult, ALU.max).then_inc(t_step, 1)
            dve.wait_ge(t_step, k + 1)
            nc.vector.reciprocal(inv[:, k:k + 1], step[:, k:k + 1]).then_inc(t_inv, 1)
            if coarse is not None:
                dve.wait_ge(t_inv, k + 1)
                nc.vector.tensor_tensor(inv[:, k:k + 1], inv[:, k:k + 1], coarse, ALU.mult).then_inc(t_inv, 1)

        def scale_pool(pool, k):
            pool.wait_ge(t_top, k + 1)
            nc.gpsimd.partition_all_reduce(top_all[:, k:k + 1], top[:, k:k + 1], P, RMAX).then_inc(t_all, 1)

        cross_attention(nc, sem, hold, tokens, ad, x, ident, woT, bo, ctxT, xwqT, xwkT, xwvT, xbq, xbk, xbv,
                        w_up, w_gate, w_down, h2d, idf, wuT, wgT, wdT, neg_half, magic, s_half, amax, ps,
                        l_sum, norm_stats, norm_rstd, norm_apply)

        with ExitStack() as feed:
            raw = feed.enter_context(nc.sbuf_tensor("raw", [P, NBLK, FT * HALF], F32))
            with ExitStack() as first:
                xqT = first.enter_context(nc.sbuf_tensor("xqT", [P, 2, NBLK, HALF], F32))
                project_gate(nc, sem, hold, tokens, h2d, idf, wgT, magic, step, inv, t_inv, ps, xqT, raw, amax, scale_of, scale_pool)
                project_up(nc, sem, hold, wuT, ud, magic, step, inv, t_inv, ps, xqT, raw, amax, scale_of, scale_pool)
            down(nc, sem, hold, tokens, h2d, ud, wdT, magic, coarse, t_coarse, step, inv, t_inv, ps, raw, amax,
                 scale_of, scale_pool, l_sum, norm_stats, norm_rstd, norm_apply, out)


def cross_attention(nc, sem, hold, tokens, ad, x, ident, woT, bo, ctxT, xwqT, xwkT, xwvT, xbq, xbk, xbv,
                    w_up, w_gate, w_down, h2d, idf, wuT, wgT, wdT, neg_half, magic, s_half, amax, ps,
                    l_sum, norm_stats, norm_rstd, norm_apply):
    with ExitStack() as ctx:
        def sb(name, shape, dt=F32):
            return ctx.enter_context(nc.sbuf_tensor(name, shape, dt))

        wo = sb("wo", [P, 2, D])
        xq_w = sb("xq_w", [P, 2, D])
        xk_w = sb("xk_w", [P, 2, D])
        xv_w = sb("xv_w", [P, 2, D])
        bot = sb("bot", [P, D])
        bvt = sb("xbvt", [P, D])
        bqk = sb("bqk", [P, 4])
        cT = sb("cT", [P, 2, B, LC])
        kx = sb("kx", [P, 2, B, LC])
        vx = sb("vx", [P, 2, B, D])
        at = sb("at", [P, 2, 4, D])
        xt = sb("xt", [P, 2, 4, D])
        atT = sb("atT", [P, 2, 2, HALF])
        h = sb("h", [P, 2, 4, D])
        h1 = sb("h1", [P, 2, 4, D])
        h1T = sb("h1T", [P, 2, 2, HALF])
        qx = sb("qx", [P, 2, 2, HALF])
        nm = sb("nm", [P, 2, 4])
        e = sb("e", [P, 2, 4, LC])
        esum = sb("esum", [P, 2, 4])
        erec = sb("erec", [P, 2, 4])
        eT = sb("eT", [P, 2, 2, HALF])
        g = sb("g", [P, 2, 4, D])
        h2 = sb("h2", [P, 2, 4, D])
        wn = [sb(f"wn{j}", [P, FT * D]) for j in range(3)]
        ws = [sb(f"ws{j}", [P, FT * D // 32]) for j in range(3)]
        wi = [sb(f"wi{j}", [P, FT * D // 32]) for j in range(3)]

        c_in = sem("c_in")
        ld = [sem(f"d_ld{j}") for j in range(2)]
        d_st = [sem(f"d_st{j}") for j in range(2)]
        d_t1 = sem("d_t1")
        d_atT = sem("d_atT")
        d_y = sem("d_y")
        d_bo = sem("d_bo")
        d_h1 = sem("d_h1")
        d_t2 = sem("d_t2")
        d_h1T = sem("d_h1T")
        d_q = sem("d_q")
        d_qx = sem("d_qx")
        d_s = sem("d_s")
        d_nm = sem("d_nm")
        d_e = sem("d_e")
        d_t3 = sem("d_t3")
        d_eT = sem("d_eT")
        d_a = sem("d_a")
        d_rec = sem("d_rec")
        d_h2 = sem("d_h2")
        d_am = sem("d_am")
        c_kv = sem("c_kv")
        c_k = sem("c_k")
        c_v = sem("c_v")
        w_in = sem("w_in")
        w_top = sem("w_top")
        w_inv = sem("w_inv")
        w_s = sem("w_s")
        w_over = sem("w_over")
        w_round = sem("w_round")
        w_deq = sem("w_deq")
        w_turn = sem("w_turn")
        w_copy = sem("w_copy")

        block = ctx.enter_context(nc.Block())
        NC_IN = 10
        TAIL = LC - P

        def run_batches(eng, batch):
            batch(0, False)
            with eng.Fori(1, B) as b:
                batch(b, True)

        @block.sync
        def _(sp):
            for j, w in enumerate((w_up, w_gate)):
                sp.dma_start(wn[j][:].rearrange("p (t d) -> p t d", d=D), w.rearrange("(t p) d -> p t d", p=P)).then_inc(w_in, 16)
            sp.dma_start(wn[2][:].rearrange("p (t d) -> p t d", d=FI), w_down.rearrange("(t p) d -> p t d", p=P)).then_inc(w_in, 16)
            sp.dma_start(idf[:], ident).then_inc(c_in, 16)
            for to, w in ((wo, woT), (xq_w, xwqT), (xk_w, xwkT), (xv_w, xwvT)):
                sp.dma_start(to[:], w.rearrange("(c p) n -> p c n", p=P)).then_inc(c_in, 16)
            sp.dma_start(cT[:].rearrange("p c b t -> p c (b t)"), ctxT.rearrange("(c p) n -> p c n", p=P)).then_inc(c_in, 16)
            sp.dma_start(bot[:], bo).then_inc(c_in, 16)
            sp.dma_start(bvt[:], xbv).then_inc(c_in, 16)
            sp.dma_start(bqk[:, 0:2], xbq).then_inc(c_in, 16)
            sp.dma_start(bqk[:, 2:4], xbk).then_inc(c_in, 16)

            def batch(b, before):
                for hf in range(2):
                    n = 2 * b + hf
                    if before:
                        hold(sp, d_t1, n - 1)
                        hold(sp, l_sum, 4 * b - 3 + hf)
                    for gr in range(4):
                        sp.dma_start(at[:, hf, :, gr * G * HD:(gr + 1) * G * HD],
                                     ad[bass.ds(4 * b + gr, 1), hf * HALF:(hf + 1) * HALF, :].rearrange(
                                         "a (q p) d -> p (a q) d", p=P)).then_inc(ld[hf], 16)
                    sp.dma_start(xt[:, hf], tokens(x, n)).then_inc(ld[hf], 16)
                if before:
                    for hf in range(2):
                        hold(sp, d_h2, 2 * b + hf - 1)
                        sp.dma_start(tokens(h2d, 2 * b + hf - 2), h2[:, hf]).then_inc(d_st[hf], 16)

            run_batches(sp, batch)
            for hf in range(2):
                sp.wait_ge(d_h2, NBLK - 1 + hf)
                sp.dma_start(tokens(h2d, NBLK - 2 + hf), h2[:, hf]).then_inc(d_st[hf], 16)
            for hf in range(2):
                sp.wait_ge(d_st[hf], 16 * B)

        @block.gpsimd
        def _(pool):
            nc.gpsimd.memset(magic[:, 0:1], MAGIC)
            nc.gpsimd.memset(magic[:, 1:2], -MAGIC)
            nc.gpsimd.memset(neg_half[:], -0.5).then_inc(s_half, 1)
            pool.wait_ge(s_half, 1)
            def batch(b, before):
                for ln in range(2):
                    for hf in range(2):
                        norm_rstd(pool, 4 * b + 2 * ln + hf, hf)

            run_batches(pool, batch)

        @block.scalar
        def _(act):
            act.wait_ge(c_in, 16 * NC_IN)
            for m in range(2):
                for j in range(2):
                    act.wait_ge(c_kv, 2 * m + j + 1)
                    last = nc.scalar.activation(kx[:, m, 2 * j:2 * j + 2, :].rearrange("p b t -> p (b t)"),
                                                ps[:, 2 * m + j, 0:2 * LC], ACT.Identity, bias=bqk[:, 2 + m:3 + m])
                    last.then_inc(c_k, 1)
            for j, to in enumerate((wuT, wgT, wdT)):
                flat = to[:].rearrange("p a b -> p (a b)")
                for k in range(3):
                    act.wait_ge(w_turn, 3 * j + k + 1)
                    nc.scalar.activation(flat[:, k * HALF:(k + 1) * HALF], ps[:, (3 * j + k) % 8, :], ACT.Copy).then_inc(w_copy, 1)

            def batch(b, before):
                for hf in range(2):
                    hold(act, d_t1, 2 * b + hf + 1)
                    nc.scalar.activation(atT[:, hf], ps[:, 2 * hf:2 * hf + 2, :], ACT.Copy).then_inc(d_atT, 1)
                for hf in range(2):
                    hold(act, d_t2, 2 * b + hf + 1)
                    nc.scalar.activation(h1T[:, hf], ps[:, 2 * hf:2 * hf + 2, :], ACT.Copy).then_inc(d_h1T, 1)
                for hf in range(2):
                    hold(act, d_q, 2 * b + hf + 1)
                    for m in range(2):
                        last = nc.scalar.activation(qx[:, hf, m, :], ps[:, 4 + 2 * hf + m, :], ACT.Identity, bias=bqk[:, m:m + 1])
                    last.then_inc(d_qx, 1)
                for hf in range(2):
                    hold(act, d_nm, 2 * b + hf + 1)
                    for q in range(4):
                        o = (q % 2) * D
                        last = nc.scalar.activation(e[:, hf, q, :], ps[:, 2 * hf + q // 2, o:o + LC], ACT.Exp,
                                                    bias=nm[:, hf, q:q + 1], accum_out=esum[:, hf, q:q + 1])
                    last.then_inc(d_e, 1)
                for hf in range(2):
                    hold(act, d_t3, 2 * b + hf + 1)
                    nc.scalar.activation(eT[:, hf, 0, :], ps[:, 4 + 2 * hf, :], ACT.Copy)
                    nc.scalar.activation(eT[0:TAIL, hf, 1, :], ps[0:TAIL, 5 + 2 * hf, :], ACT.Copy).then_inc(d_eT, 1)

            run_batches(act, batch)

        @block.vector
        def _(dve):
            dve.wait_ge(w_in, 16 * 3)
            for j in range(3):
                v = wn[j][:].rearrange("p (n k) -> p n k", k=32)
                nc.vector.tensor_reduce(ws[j][:], v, AX.X, ALU.max, apply_absolute_value=True).then_inc(w_top, 1)
                dve.wait_ge(w_top, j + 1)
                nc.vector.tensor_scalar(ws[j][:], ws[j][:], 1.0 / 7.0, TINY, ALU.mult, ALU.max).then_inc(w_s, 1)
                dve.wait_ge(w_s, j + 1)
                nc.vector.reciprocal(wi[j][:], ws[j][:]).then_inc(w_inv, 1)
                dve.wait_ge(w_inv, j + 1)
                nc.vector.tensor_tensor(v, v, wi[j][:].unsqueeze(2).to_broadcast([P, FT * D // 32, 32]),
                                        ALU.mult).then_inc(w_over, 1)
            dve.wait_ge(c_in, 16 * NC_IN)
            dve.wait_ge(c_kv, 5)
            for b in range(B):
                nc.vector.tensor_tensor(vx[:, 0, b, :], ps[:, 4 + b // 2, (b % 2) * D:(b % 2 + 1) * D], bvt[:], ALU.add)
                last = nc.vector.tensor_tensor(vx[0:TAIL, 1, b, :], ps[0:TAIL, 6 + b // 2, (b % 2) * D:(b % 2 + 1) * D],
                                               bvt[0:TAIL, :], ALU.add)
            last.then_inc(c_v, 1)
            for j in range(3):
                v = wn[j][:].rearrange("p (n k) -> p n k", k=32)
                dve.wait_ge(w_over, j + 1)
                nc.vector.tensor_scalar(wn[j][:], wn[j][:], MAGIC, MAGIC, ALU.add, ALU.subtract).then_inc(w_round, 1)
                dve.wait_ge(w_round, j + 1)
                nc.vector.tensor_tensor(v, v, ws[j][:].unsqueeze(2).to_broadcast([P, FT * D // 32, 32]),
                                        ALU.mult).then_inc(w_deq, 1)

            def batch(b, before):
                for hf in range(2):
                    n = 2 * b + hf
                    hold(dve, ld[hf], 16 * 5 * (b + 1))
                    nc.vector.tensor_tensor(xt[:, hf], xt[:, hf], bot[:].unsqueeze(1).to_broadcast([P, 4, D]), ALU.add).then_inc(d_bo, 1)
                for hf in range(2):
                    n = 2 * b + hf
                    hold(dve, d_bo, n + 1)
                    hold(dve, d_y, n + 1)
                    nc.vector.tensor_tensor(h[:, hf].rearrange("p q d -> p (q d)"),
                                            ps[:, 4 + 2 * hf:6 + 2 * hf, :].rearrange("p a n -> p (a n)"),
                                            xt[:, hf].rearrange("p q d -> p (q d)"), ALU.add).then_inc(l_sum, 1)
                    norm_stats(dve, 4 * b + hf, hf, h[:, hf])
                for hf in range(2):
                    norm_apply(dve, 4 * b + hf, hf, h[:, hf], h1[:, hf]).then_inc(d_h1, 1)
                for hf in range(2):
                    hold(dve, d_s, 2 * b + hf + 1)
                    v = ps[:, 2 * hf:2 * hf + 2, :].rearrange("p a (c n) -> p (a c) n", n=D)
                    nc.vector.tensor_reduce(nm[:, hf, :], v[:, :, 0:LC], AX.X, ALU.max, negate=True).then_inc(d_nm, 1)
                for hf in range(2):
                    n = 2 * b + hf
                    hold(dve, d_e, n + 1)
                    nc.vector.reciprocal(erec[:, hf, :], esum[:, hf, :]).then_inc(d_rec, 1)
                    hold(dve, d_rec, n + 1)
                    hold(dve, d_a, n + 1)
                    for q in range(4):
                        o = (q % 2) * D
                        last = nc.vector.scalar_tensor_tensor(g[:, hf, q, :], ps[:, 2 * hf + q // 2, o:o + D],
                                                              erec[:, hf, q:q + 1], h1[:, hf, q, :], ALU.mult, ALU.add)
                    last.then_inc(l_sum, 1)
                    norm_stats(dve, 4 * b + 2 + hf, hf, g[:, hf])
                for hf in range(2):
                    n = 2 * b + hf
                    if before:
                        hold(dve, d_st[hf], 16 * b)
                    norm_apply(dve, 4 * b + 2 + hf, hf, g[:, hf], h2[:, hf]).then_inc(d_h2, 1)
                    hold(dve, d_h2, n + 1)
                    nc.vector.tensor_reduce(amax[:, 0, bass.ds(n, 1)], h2[:, hf].rearrange("p q d -> p (q d)"), AX.X, ALU.max,
                                            apply_absolute_value=True).then_inc(d_am, 1)

            run_batches(dve, batch)

        @block.tensor
        def _(pe):
            mm = nc.tensor.matmul
            tr = nc.tensor.transpose
            pe.wait_ge(c_in, 16 * NC_IN)
            for m in range(2):
                for j in range(2):
                    for c in range(2):
                        last = mm(ps[:, 2 * m + j, 0:2 * LC], xk_w[:, c, m * P:(m + 1) * P],
                                  cT[:, c, 2 * j:2 * j + 2, :].rearrange("p b t -> p (b t)"), start=(c == 0), stop=(c == 1))
                    last.then_inc(c_kv, 1)
            for b in range(B):
                for w, lo, hi in ((0, 0, P), (1, P, LC)):
                    for c in range(2):
                        last = mm(ps[0:hi - lo, 4 + 2 * w + b // 2, (b % 2) * D:(b % 2 + 1) * D], cT[:, c, b, lo:hi], xv_w[:, c, :],
                                  start=(c == 0), stop=(c == 1))
            last.then_inc(c_kv, 1)
            pe.wait_ge(c_k, 4)
            pe.wait_ge(c_v, 1)
            for j in range(3):
                pe.wait_ge(w_deq, j + 1)
                for k in range(3):
                    bank = 3 * j + k
                    if bank >= 8:
                        pe.wait_ge(w_copy, bank - 7)
                    for u in range(4):
                        v = 4 * k + u
                        if j < 2:
                            c, t = v // FT, v % FT
                            src = wn[j][:, t * D + c * P:t * D + (c + 1) * P]
                        else:
                            t, c = v // 2, v % 2
                            src = wn[j][:, c * FI + t * P:c * FI + (t + 1) * P]
                        last = tr(ps[:, bank % 8, u * P:(u + 1) * P], src, idf[:])
                    last.then_inc(w_turn, 1)
            pe.wait_ge(w_copy, 9)

            def batch(b, before):
                for hf in range(2):
                    hold(pe, ld[hf], 16 * 5 * (b + 1))
                    if before:
                        hold(pe, l_sum, 4 * b - 1 + hf)
                    for c in range(2):
                        for q in range(4):
                            last = tr(ps[:, 2 * hf + c, q * P:(q + 1) * P], at[:, hf, q, c * P:(c + 1) * P], idf[:])
                    last.then_inc(d_t1, 1)
                for hf in range(2):
                    hold(pe, d_atT, 2 * b + hf + 1)
                    for q in range(4):
                        for c in range(2):
                            last = mm(ps[:, 4 + 2 * hf + q // 2, (q % 2) * D:(q % 2 + 1) * D], atT[:, hf, c, q * P:(q + 1) * P],
                                      wo[:, c, :], start=(c == 0), stop=(c == 1))
                    last.then_inc(d_y, 1)
                for hf in range(2):
                    hold(pe, d_h1, 2 * b + hf + 1)
                    for c in range(2):
                        for q in range(4):
                            last = tr(ps[:, 2 * hf + c, q * P:(q + 1) * P], h1[:, hf, q, c * P:(c + 1) * P], idf[:])
                    last.then_inc(d_t2, 1)
                for hf in range(2):
                    hold(pe, d_h1T, 2 * b + hf + 1)
                    for m in range(2):
                        for c in range(2):
                            last = mm(ps[:, 4 + 2 * hf + m, :], xq_w[:, c, m * P:(m + 1) * P], h1T[:, hf, c, :],
                                      start=(c == 0), stop=(c == 1))
                    last.then_inc(d_q, 1)
                for hf in range(2):
                    hold(pe, d_qx, 2 * b + hf + 1)
                    for q in range(4):
                        for m in range(2):
                            o = (q % 2) * D
                            last = mm(ps[:, 2 * hf + q // 2, o:o + LC], qx[:, hf, m, q * P:(q + 1) * P],
                                      kx[:, m, bass.ds(b, 1), :].rearrange("p a t -> p (a t)"), start=(m == 0), stop=(m == 1))
                    last.then_inc(d_s, 1)
                for hf in range(2):
                    hold(pe, d_e, 2 * b + hf + 1)
                    for q in range(4):
                        tr(ps[:, 4 + 2 * hf, q * P:(q + 1) * P], e[:, hf, q, 0:P], idf[:])
                        last = tr(ps[0:TAIL, 5 + 2 * hf, q * P:(q + 1) * P], e[:, hf, q, P:LC], idf[:])
                    last.then_inc(d_t3, 1)
                for hf in range(2):
                    hold(pe, d_eT, 2 * b + hf + 1)
                    for q in range(4):
                        to = ps[:, 2 * hf + q // 2, (q % 2) * D:(q % 2 + 1) * D]
                        mm(to, eT[:, hf, 0, q * P:(q + 1) * P], vx[:, 0, bass.ds(b, 1), :].rearrange("p a d -> p (a d)"),
                           start=True, stop=False)
                        last = mm(to, eT[0:TAIL, hf, 1, q * P:(q + 1) * P],
                                  vx[0:TAIL, 1, bass.ds(b, 1), :].rearrange("p a d -> p (a d)"), start=False, stop=True)
                    last.then_inc(d_a, 1)

            run_batches(pe, batch)


def run_pairs(eng, body):
    body(0, 0, False)
    body(1, 1, False)
    with eng.Fori(1, NBLK // 2) as j:
        body(2 * j, 0, True)
        body(2 * j + 1, 1, True)


def flat(t, n):
    return t[:, bass.ds(n, 1), :].rearrange("p a n -> p (a n)")


def project_gate(nc, sem, hold, tokens, h2d, idf, wgT, magic, step, inv, t_inv, ps, xqT, raw, amax, scale_of, scale_pool):
    with ExitStack() as ctx:
        hb = ctx.enter_context(nc.sbuf_tensor("hb", [P, 2, 4, D], F32))
        f_ld = [sem(f"f_ld{j}") for j in range(2)]
        f_x = sem("f_x")
        f_xq = sem("f_xq")
        f_t = sem("f_t")
        f_xqT = sem("f_xqT")
        f_g = sem("f_g")
        f_gc = sem("f_gc")
        f_ga = sem("f_ga")
        block = ctx.enter_context(nc.Block())

        @block.sync
        def _(sp):
            def load(n, par, before):
                if before:
                    hold(sp, f_t, n - 1)
                sp.dma_start(hb[:, par], tokens(h2d, n)).then_inc(f_ld[par], 16)

            run_pairs(sp, load)

        @block.gpsimd
        def _(pool):
            scale_pool(pool, 0)
            scale_pool(pool, 1)

        @block.scalar
        def _(act):
            act.wait_ge(t_inv, 1)

            def quantise(n, par):
                hold(act, f_ld[par], 16 * (n // 2 + 1))
                nc.scalar.activation(hb[:, par], hb[:, par], ACT.Identity, bias=magic[:, 0:1], scale=inv[:, 0:1]).then_inc(f_x, 1)

            def copy(n, par):
                hold(act, f_t, n + 1)
                nc.scalar.activation(xqT[:, :, bass.ds(n, 1), :].rearrange("p c a n -> p c (a n)"),
                                     ps[:, 6:8, :], ACT.Copy).then_inc(f_xqT, 1)

            def copy_gate(n):
                for m in range(FT):
                    hold(act, f_g, FT * n + m + 1)
                    nc.scalar.activation(raw[:, bass.ds(n, 1), m * HALF:(m + 1) * HALF].rearrange("p a n -> p (a n)"),
                                         ps[:, m, :], ACT.Copy).then_inc(f_gc, 1)

            quantise(0, 0)
            copy(0, 0)
            quantise(1, 1)
            copy(1, 1)
            with act.Fori(0, NBLK // 2 - 1) as j:
                for par in range(2):
                    quantise(2 * j + 2 + par, par)
                    copy_gate(2 * j + par)
                    copy(2 * j + 2 + par, par)
            copy_gate(NBLK - 2)
            copy_gate(NBLK - 1)

        @block.vector
        def _(dve):
            scale_of(dve, 0)

            def quantise(n, par):
                hold(dve, f_x, n + 1)
                nc.vector.tensor_scalar(hb[:, par], hb[:, par], MAGIC, step[:, 0:1], ALU.subtract, ALU.mult).then_inc(f_xq, 1)

            def largest(n):
                hold(dve, f_gc, FT * n + FT)
                nc.vector.tensor_reduce(amax[:, 1, bass.ds(n, 1)], flat(raw, n), AX.X, ALU.max,
                                        apply_absolute_value=True).then_inc(f_ga, 1)

            quantise(0, 0)
            quantise(1, 1)
            with dve.Fori(0, NBLK // 2 - 1) as j:
                for par in range(2):
                    quantise(2 * j + 2 + par, par)
                    largest(2 * j + par)
            largest(NBLK - 2)
            largest(NBLK - 1)
            dve.wait_ge(f_ga, NBLK)
            scale_of(dve, 1)

        @block.tensor
        def _(pe):
            mm = nc.tensor.matmul

            def turn(n, par, before):
                hold(pe, f_xq, n + 1)
                if before:
                    hold(pe, f_xqT, n)
                for c in range(2):
                    for q in range(4):
                        last = nc.tensor.transpose(ps[:, 6 + c, q * P:(q + 1) * P], hb[:, par, q, c * P:(c + 1) * P], idf[:])
                last.then_inc(f_t, 1)

            def products(n, before):
                hold(pe, f_xqT, n + 1)
                for m in range(FT):
                    if before:
                        hold(pe, f_gc, FT * (n - 1) + m + 1)
                    for c in range(2):
                        last = mm(ps[:, m, :], wgT[:, c, m * P:(m + 1) * P],
                                  xqT[:, c, bass.ds(n, 1), :].rearrange("p a n -> p (a n)"), start=(c == 0), stop=(c == 1))
                    last.then_inc(f_g, 1)

            turn(0, 0, False)
            turn(1, 1, True)
            products(0, False)
            turn(2, 0, True)
            products(1, True)
            turn(3, 1, True)
            with pe.Fori(1, NBLK // 2 - 1) as j:
                for par in range(2):
                    products(2 * j + par, True)
                    turn(2 * j + 2 + par, par, True)
            products(NBLK - 2, True)
            products(NBLK - 1, True)


def project_up(nc, sem, hold, wuT, ud, magic, step, inv, t_inv, ps, xqT, raw, amax, scale_of, scale_pool):
    with ExitStack() as ctx:
        ub = ctx.enter_context(nc.sbuf_tensor("ub", [P, 2, FT * HALF], F32))
        sg = ctx.enter_context(nc.sbuf_tensor("sg", [P, 2, FT * HALF], F32))
        u_full = sem("u_full")
        u_copied = sem("u_copied")
        u_max = sem("u_max")
        u_st = [sem(f"u_st{j}") for j in range(2)]
        g_r = sem("g_r")
        g_q = sem("g_q")
        g_sig = sem("g_sig")
        g_clip = sem("g_clip")
        g_sr = sem("g_sr")
        g_g2 = sem("g_g2")
        g_a2 = sem("g_a2")
        block = ctx.enter_context(nc.Block())

        @block.sync
        def _(sp):
            def store(n, par, before):
                hold(sp, u_copied, FT * n + FT)
                sp.dma_start(ud[bass.ds(n, 1)].rearrange("a p n -> (a p) n"), ub[:, par]).then_inc(u_st[par], 16)

            run_pairs(sp, store)
            for par in range(2):
                sp.wait_ge(u_st[par], 8 * NBLK)

        @block.gpsimd
        def _(pool):
            scale_pool(pool, 2)
            scale_pool(pool, 3)

        @block.scalar
        def _(act):
            def round_gate(n):
                nc.scalar.activation(flat(raw, n), flat(raw, n), ACT.Identity, bias=magic[:, 0:1], scale=inv[:, 1:2]).then_inc(g_r, 1)

            def step_of(n, par, before, more=True):
                if more:
                    round_gate(n + 1)
                if before:
                    hold(act, u_st[par], 16 * (n // 2))
                    hold(act, u_max, n - 1)
                for m in range(FT):
                    if m == 0:
                        hold(act, g_q, n + 1)
                        if before:
                            hold(act, g_g2, n - 1)
                        nc.scalar.activation(sg[:, par], flat(raw, n), ACT.Sigmoid).then_inc(g_sig, 1)
                    if m == 3:
                        hold(act, g_clip, n + 1)
                        nc.scalar.activation(sg[:, par], sg[:, par], ACT.Identity, bias=magic[:, 0:1]).then_inc(g_sr, 1)
                    hold(act, u_full, FT * n + m + 1)
                    nc.scalar.activation(ub[:, par, m * HALF:(m + 1) * HALF], ps[:, m, :], ACT.Copy).then_inc(u_copied, 1)

            round_gate(0)
            step_of(0, 0, False)
            step_of(1, 1, False)
            with act.Fori(1, NBLK // 2 - 1) as j:
                step_of(2 * j, 0, True)
                step_of(2 * j + 1, 1, True)
            step_of(NBLK - 2, 0, True)
            step_of(NBLK - 1, 1, True, False)

        @block.vector
        def _(dve):
            def dequantise(n):
                hold(dve, g_r, n + 1)
                nc.vector.tensor_scalar(flat(raw, n), flat(raw, n), MAGIC, step[:, 1:2], ALU.subtract, ALU.mult).then_inc(g_q, 1)

            def step_of(n, par, more=True):
                hold(dve, g_sig, n + 1)
                w = sg[:, par]
                nc.vector.tensor_scalar(w, w, U16, U16 - 1.0, ALU.mult, ALU.min).then_inc(g_clip, 1)
                if more:
                    dequantise(n + 1)
                hold(dve, g_sr, n + 1)
                nc.vector.scalar_tensor_tensor(flat(raw, n), w, MAGIC, flat(raw, n), ALU.subtract, ALU.mult).then_inc(g_g2, 1)
                hold(dve, g_g2, n + 1)
                nc.vector.tensor_reduce(amax[:, 2, bass.ds(n, 1)], flat(raw, n), AX.X, ALU.max, apply_absolute_value=True).then_inc(g_a2, 1)
                hold(dve, u_copied, FT * n + FT)
                nc.vector.tensor_reduce(amax[:, 3, bass.ds(n, 1)], ub[:, par], AX.X, ALU.max, apply_absolute_value=True).then_inc(u_max, 1)

            dequantise(0)
            with dve.Fori(0, NBLK // 2 - 1) as j:
                step_of(2 * j, 0)
                step_of(2 * j + 1, 1)
            step_of(NBLK - 2, 0)
            step_of(NBLK - 1, 1, False)
            dve.wait_ge(g_a2, NBLK)
            scale_of(dve, 2, U16)
            dve.wait_ge(u_max, NBLK)
            scale_of(dve, 3)

        @block.tensor
        def _(pe):
            def products(n, before):
                for m in range(FT):
                    if before:
                        hold(pe, u_copied, FT * (n - 1) + m + 1)
                    for c in range(2):
                        last = nc.tensor.matmul(ps[:, m, :], wuT[:, c, m * P:(m + 1) * P],
                                                xqT[:, c, bass.ds(n, 1), :].rearrange("p a n -> p (a n)"), start=(c == 0), stop=(c == 1))
                    last.then_inc(u_full, 1)

            products(0, False)
            with pe.Fori(1, NBLK) as n:
                products(n, True)


def down(nc, sem, hold, tokens, h2d, ud, wdT, magic, coarse, t_coarse, step, inv, t_inv, ps, raw, amax,
         scale_of, scale_pool, l_sum, norm_stats, norm_rstd, norm_apply, out):
    with ExitStack() as ctx:
        ub = ctx.enter_context(nc.sbuf_tensor("ub_in", [P, 2, FT * HALF], F32))
        work = ctx.enter_context(nc.sbuf_tensor("work", [P, 2, FT * HALF], F32))
        res = ctx.enter_context(nc.sbuf_tensor("res", [P, 2, 4, D], F32))
        p_ld = [sem(f"p_ld{j}") for j in range(2)]
        p_g = sem("p_g")
        p_gi = sem("p_gi")
        p_u = sem("p_u")
        p_o = sem("p_o")
        p_a = sem("p_a")
        o_r = sem("o_r")
        o_q = sem("o_q")
        o_ps = sem("o_ps")
        o_fin = sem("o_fin")
        o_ld = [sem(f"o_ld{j}") for j in range(2)]
        o_st = [sem(f"o_st{j}") for j in range(2)]
        block = ctx.enter_context(nc.Block())

        @block.sync
        def _(sp):
            def load_up(n, par, before):
                if before:
                    hold(sp, p_o, n - 1)
                sp.dma_start(ub[:, par], ud[bass.ds(n, 1)].rearrange("a p n -> (a p) n")).then_inc(p_ld[par], 16)

            run_pairs(sp, load_up)

            def load(n, par, before):
                if before:
                    hold(sp, o_fin, n - 1)
                    sp.dma_start(tokens(out, n - 2), res[:, par]).then_inc(o_st[par], 16)
                    hold(sp, o_st[par], 16 * (n // 2))
                sp.dma_start(res[:, par], tokens(h2d, n)).then_inc(o_ld[par], 16)

            run_pairs(sp, load)
            for par in range(2):
                sp.wait_ge(o_fin, NBLK - 1 + par)
                sp.dma_start(tokens(out, NBLK - 2 + par), res[:, par]).then_inc(o_st[par], 16)
            for par in range(2):
                sp.wait_ge(o_st[par], 8 * NBLK)

        @block.gpsimd
        def _(pool):
            scale_pool(pool, 4)
            run_pairs(pool, lambda n, par, before: norm_rstd(pool, 2 * NBLK + n, par))

        @block.scalar
        def _(act):
            def multiply(n, par, before):
                nc.scalar.activation(flat(raw, n), flat(raw, n), ACT.Identity, bias=magic[:, 0:1], scale=inv[:, 2:3]).then_inc(p_g, 1)
                hold(act, p_ld[par], 16 * (n // 2 + 1))
                nc.scalar.activation(ub[:, par], ub[:, par], ACT.Identity, bias=magic[:, 0:1], scale=inv[:, 3:4]).then_inc(p_u, 1)
                hold(act, p_g, n + 1)
                nc.scalar.activation(flat(raw, n), flat(raw, n), ACT.Identity, bias=magic[:, 1:2]).then_inc(p_gi, 1)

            run_pairs(act, multiply)
            act.wait_ge(t_inv, NSC + 1)
            with act.Fori(0, NBLK) as n:
                nc.scalar.activation(flat(raw, n), flat(raw, n), ACT.Identity, bias=magic[:, 0:1], scale=inv[:, 4:5]).then_inc(o_r, 1)

        @block.vector
        def _(dve):
            nc.vector.tensor_scalar(coarse[:], step[:, 2:3], step[:, 3:4], 1.0 / U16, ALU.mult, ALU.mult).then_inc(t_coarse, 1)

            def multiply(n, par, before):
                hold(dve, p_gi, n + 1)
                hold(dve, p_u, n + 1)
                nc.vector.scalar_tensor_tensor(flat(raw, n), ub[:, par], MAGIC, flat(raw, n), ALU.subtract, ALU.mult).then_inc(p_o, 1)
                hold(dve, p_o, n + 1)
                nc.vector.tensor_reduce(amax[:, 4, bass.ds(n, 1)], flat(raw, n), AX.X, ALU.max, apply_absolute_value=True).then_inc(p_a, 1)

            run_pairs(dve, multiply)
            dve.wait_ge(p_a, NBLK)
            dve.wait_ge(t_coarse, 1)
            scale_of(dve, 4, 1.0, coarse[:])

            def down_in(n, par, before):
                hold(dve, o_r, n + 1)
                if before:
                    hold(dve, o_ps, n - 1)
                nc.vector.tensor_scalar(work[:, par], flat(raw, n), MAGIC, step[:, 4:5], ALU.subtract, ALU.mult).then_inc(o_q, 1)

            def finish(n, par):
                hold(dve, o_ps, n + 1)
                hold(dve, o_ld[par], 16 * (n // 2 + 1))
                r = res[:, par]
                nc.vector.tensor_tensor(r.rearrange("p q d -> p (q d)"), ps[:, 2 * par:2 * par + 2, :].rearrange("p a n -> p (a n)"),
                                        r.rearrange("p q d -> p (q d)"), ALU.add).then_inc(l_sum, 1)
                norm_stats(dve, 2 * NBLK + n, par, r)
                norm_apply(dve, 2 * NBLK + n, par, r, r).then_inc(o_fin, 1)

            down_in(0, 0, False)
            down_in(1, 1, False)
            finish(0, 0)
            with dve.Fori(1, NBLK // 2) as j:
                down_in(2 * j, 0, True)
                finish(2 * j - 1, 1)
                down_in(2 * j + 1, 1, True)
                finish(2 * j, 0)
            finish(NBLK - 1, 1)

        @block.tensor
        def _(pe):
            def products(n, par, before):
                hold(pe, o_q, n + 1)
                if before:
                    hold(pe, l_sum, 2 * NBLK + n - 1)
                for q in range(4):
                    for m in range(FT):
                        last = nc.tensor.matmul(ps[:, 2 * par + q // 2, (q % 2) * D:(q % 2 + 1) * D],
                                                work[:, par, m * HALF + q * P:m * HALF + (q + 1) * P], wdT[:, m, :],
                                                start=(m == 0), stop=(m == FT - 1))
                last.then_inc(o_ps, 1)

            run_pairs(pe, products)


def build(nc, xT, wqT, wkT, wvT, bq, bk, bv, emb, part_of_row, e_lo, e_hi, ident,
          x, woT, bo, ctxT, xwqT, xwkT, xwvT, xbq, xbk, xbv, w_up, w_gate, w_down, out):
    with ExitStack() as sems:
        def sem(name):
            return sems.enter_context(nc.semaphore(name))

        ad = nc.dram_tensor("attn_all", [NIT, L, G * HD], F32, kind="Internal").ap()
        self_attention(nc, sem, ad, xT, wqT, wkT, wvT, bq, bk, bv, emb, part_of_row, e_lo, e_hi, ident)
        decoder_rest(nc, sem, ad, x, ident, woT, bo, ctxT, xwqT, xwkT, xwvT, xbq, xbk, xbv, w_up, w_gate, w_down, out)


def kernel(**inputs):
    import numpy as np
    import concourse.bacc as bacc
    from concourse.bass_utils import run_bass_kernel_spmd

    a = {k: np.asarray(v) for k, v in inputs.items()}
    e = a["L0_attn_dist_emb"]
    part_of_row = np.zeros((KR, 3), np.float32)
    for slot, p in enumerate((0, 0, 0, 1, 1, 2)):
        part_of_row[HD * slot:HD * (slot + 1), p] = 1.0
    ident = np.eye(P, dtype=np.float32)

    def by_dim(w):
        return w.reshape(-1, 2, 2, G, HD).transpose(0, 1, 2, 4, 3).reshape(-1, D)

    arrays = {
        "xT": a["x"].reshape(N, D).T, "wqT": by_dim(a["L0_attn_Wq"].T), "wkT": by_dim(a["L0_attn_Wk"].T), "wvT": a["L0_attn_Wv"].T,
        "bq": by_dim(a["L0_attn_bq"]).reshape(2, P).T, "bk": by_dim(a["L0_attn_bk"]).reshape(2, P).T,
        "bv": np.broadcast_to(a["L0_attn_bv"], (P, D)), "emb": np.tile(e.T, (6, 1)), "part_of_row": part_of_row,
        "e_lo": np.tile(np.repeat(e[0], G), 2).reshape(P, 1), "e_hi": np.tile(np.repeat(e[NJ], G), 2).reshape(P, 1),
        "ident": ident,
        "x": a["x"].reshape(NBLK, HALF, D), "woT": a["L0_attn_Wo"].T, "bo": np.broadcast_to(a["L0_attn_bo"], (P, D)),
        "ctxT": a["ctx_1024"].reshape(B * LC, D).T, "xwqT": a["L0_xattn_Wq"].T, "xwkT": a["L0_xattn_Wk"].T,
        "xwvT": a["L0_xattn_Wv"].T, "xbq": a["L0_xattn_bq"].reshape(2, P).T, "xbk": a["L0_xattn_bk"].reshape(2, P).T,
        "xbv": np.broadcast_to(a["L0_xattn_bv"], (P, D)),
        "w_up": a["L0_ffn_w_up"], "w_gate": a["L0_ffn_w_gate"], "w_down": a["L0_ffn_w_down"],
    }
    nc = bacc.Bacc("TRN2", target_bir_lowering=False, num_devices=1)
    args = []
    for name in arrays:
        arrays[name] = np.ascontiguousarray(arrays[name])
        args.append(nc.dram_tensor(name, arrays[name].shape, mybir.dt.from_np(arrays[name].dtype), kind="ExternalInput").ap())
    args.append(nc.dram_tensor("result", [NBLK, HALF, D], F32, kind="ExternalOutput").ap())
    build(nc, *args)
    r = run_bass_kernel_spmd(nc, [arrays], core_ids=[0])
    return r.results[0]["result"].reshape(B, L, D)
```

```python
import concourse.bass as bass
from concourse import mybir
from contextlib import ExitStack

F32 = mybir.dt.float32
BF16 = mybir.dt.bfloat16
ALU = mybir.AluOpType
ACT = mybir.ActivationFunctionType
AX = mybir.AxisListType

P = 128
B, L, D = 4, 1024, 256
N = B * L
NH, HD = 16, 16
LEFT, RIGHT = 64, 8
NJ = LEFT + RIGHT
G = 4
NIT = B * NH // G
HALF = 512
TL = L // P
PADL = P
TW = PADL + NJ + P
WIN = LEFT + P + RIGHT
ZL = LEFT
STEPS = 32
KR = 6 * HD
NP_BUF = 4
LC = 154
FI = 768
FT = FI // P
NBLK = N // HALF
NSC = 5
EPS = 1e-5
QMAX = 32767.0
U16 = 65536.0
TINY = 1e-12
MAGIC = 1.5 * 2.0 ** 23
RMAX = bass.bass_isa.ReduceOp.max
NR = 4



def self_attention(nc, sem, ad, xT, wqT, wkT, wvT, bq, bk, bv, emb, part_of_row, e_lo, e_hi, ident):
    ctx = ExitStack()
    with ctx:
        def sb(name, shape, dt=F32):
            return ctx.enter_context(nc.sbuf_tensor(name, shape, dt))

        def dram(name, shape, dt=F32):
            return nc.dram_tensor(name, shape, dt, kind="Internal").ap()

        td = [dram(n, [NIT // 2, 3, 2, G * HD, L], BF16) for n in ("q_parts", "k_lo_parts", "k_hi_parts", "k_mixed_parts")]
        vd = dram("v_all", [NIT, L, P])
        tab = dram("rel_table", [2, G, L, TW])

        psT = ctx.enter_context(nc.psum_tensor("scoresT", [P, 4, HALF], F32))
        psX = ctx.enter_context(nc.psum_tensor("scores_for_max", [P, 2, HALF], F32))
        psO = ctx.enter_context(nc.psum_tensor("attn_out", [P, HALF], F32))
        psM = ctx.enter_context(nc.psum_tensor("misc", [P, HALF], F32))

        idf = sb("idf", [P, P])
        idb = sb("idb", [P, P], BF16)
        embr = sb("embr", [KR, NJ + 1])
        prow = sb("prow", [KR, 3])
        embd = sb("embd", [KR, NJ])
        embt = sb("embt", [KR, 3, NJ])
        embp = sb("embp", [KR, 3, NJ], BF16)
        embS = sb("embS", [KR, NJ], BF16)
        colb = sb("colb", [P, 6])
        colc = sb("colc", [P, 6])

        s_const = sem("s_const")
        s_w = sem("s_w")
        s_pads = sem("s_pads")
        s_zero = sem("s_zero")
        s_prep = sem("s_prep")
        s_ones = sem("s_ones")
        s_bufs = sem("s_bufs")
        a_x = [sem(f"a_x{j}") for j in range(2)]
        a_full = sem("a_full")
        a_val = sem("a_val")
        a_hi_val = sem("a_hi_val")
        a_high = sem("a_high")
        a_rem = sem("a_rem")
        a_mid = sem("a_mid")
        a_low = sem("a_low")
        a_v = sem("a_v")
        a_mix = sem("a_mix")
        a_out = [sem(f"a_out{j}") for j in range(2)]
        ld_q = [sem(f"ld_q{i}") for i in range(2)]
        ld_k = [sem(f"ld_k{i}") for i in range(2)]
        ld_lo = [sem(f"ld_lo{i}") for i in range(2)]
        ld_hi = [sem(f"ld_hi{i}") for i in range(2)]
        ld_r = [sem(f"ld_r{i}") for i in range(2)]
        t_wr = [sem(f"t_wr{i}") for i in range(NR)]
        st_done = sem("st_done")
        exp_done = sem("exp_done")
        pv_done = sem("pv_done")
        mx_full = sem("mx_full")
        mx_free = sem("mx_free")
        m_ready = sem("m_ready")
        m_turned = sem("m_turned")
        qm_ready = sem("qm_ready")
        r_full = sem("r_full")
        r_rows = sem("r_rows")
        r_padded = sem("r_padded")
        wb_ready = sem("wb_ready")
        o_copied = sem("o_copied")
        o_turned = sem("o_turned")
        o_rec = sem("o_rec")
        m_small = sem("m_small")
        an_ready = sem("an_ready")
        an_out = sem("an_out")
        s_held = sem("s_held")
        s_dve = sem("s_dve")

        with ExitStack() as early:
            def sbe(name, shape, dt=F32):
                return early.enter_context(nc.sbuf_tensor(name, shape, dt))
            zero = sbe("zero", [P, TL * P])
            wq = sbe("wq", [P, 2, D])
            wk = sbe("wk", [P, 2, D])
            wv = sbe("wv", [P, 2, D])
            bvt = sbe("bvt", [P, D])
            xs = sbe("xs", [P, 2, 2, HALF])
            val = sbe("val", [P, 2, 6, HALF])
            rem = sbe("rem", [P, 2, 6, HALF])
            part = sbe("part", [P, 2, 8, 3, HALF], BF16)
            vs = sbe("vs", [P, 2, 4, NH, 32])

        qT = sb("qT", [P, 2, G, L], BF16)
        qR = sb("qR", [P, 2, G, L], BF16)
        kT = sb("kT", [P, 2, 3, G, L], BF16)
        vS = sb("vS", [P, 2, TL, P])
        win = sb("win", [P, 2, TL, G, ZL + WIN])
        winb = sb("winb", [P, 2, TL // 2, G, WIN], BF16)
        rows = sb("rows", [P, NR, G, PADL + NJ])
        pr = sb("pr", [P, NP_BUF, 2 * HALF])
        nmax = sb("nmax", [P, 2, 4, 2, G])
        mval = sb("mval", [P, G])
        mcol = sb("mcol", [P, G, 32], BF16)
        ot = sb("ot", [P, HALF])
        orec = sb("orec", [P, 16])
        an = sb("an", [P, 4, G * HD])

        block = ctx.enter_context(nc.Block())
        NCONST = 8
        NPADS = 2 * G
        A_DMAS = 8 + 4
        LQ, LK, LW = 3, 10, 4

        def row(t, i):
            return t[bass.ds(i, 1)].rearrange("a p n -> (a p) n")

        def pieces(cuts, hf):
            lo, hi = hf * HALF, (hf + 1) * HALF
            return [(max(a, lo), min(b, hi), v) for a, b, v in cuts if max(a, lo) < min(b, hi)]

        def by_query(kt, hf):
            return pieces([(0, (kt + 1) * P, 1), ((kt + 1) * P, (kt + 2) * P, 2), ((kt + 2) * P, L, 0)], hf)

        def by_key(qt, hf):
            return pieces([(0, (qt - 1) * P, 0), ((qt - 1) * P, qt * P, 2), (qt * P, L, 1)], hf)

        R_STEPS = {0: 0, 4: 1, 8: 2, 12: 3}
        M_STEPS = {2: 0, 6: 1, 10: 2, 14: 3}
        N_STEP = 5
        LEAD = 6
        T_CH = 32

        def chunks_at(t):
            return [((LEAD + 2 * t + e) // T_CH, (LEAD + 2 * t + e) % T_CH) for e in range(2)]

        def run_blocks(eng, block_of):
            block_of(0, 0, False, False)
            block_of(0, 1, True, False)
            with eng.Fori(1, B) as b:
                block_of(b, 0, True, True)
                block_of(b, 1, True, True)

        def hold(eng, s, value):
            eng.wait_ge(s, value)
            eng.sem_inc(s_held, 1)

        def run_groups(eng, group):
            group(0, 0, 0, first=True)
            with eng.Fori(0, 6) as j:
                group(1 + 2 * j, 1, j)
                group(2 + 2 * j, 0, j + 1)
            group(13, 1, 6, ahead=False)
            group(14, 0, 7, rel=False, ahead=False)
            group(15, 1, 7, rel=False, last=True, ahead=False)

        @block.sync
        def _(sp):
            def load_x(b, hf, again=True):
                k = 2 * b + hf
                if again:
                    hold(sp, a_full, 6 * (k - 1))
                sp.dma_start(xs[:, hf], xT[:, bass.ds(k * HALF, HALF)].rearrange("(c p) n -> p c n", p=P)).then_inc(a_x[hf], 16)

            load_x(0, 0, False)
            for dst, src in ((wq, wqT.rearrange("(c p) n -> p c n", p=P)),
                             (wk, wkT.rearrange("(c p) n -> p c n", p=P)),
                             (wv, wvT.rearrange("(c p) n -> p c n", p=P))):
                sp.dma_start(dst[:], src).then_inc(s_w, 16)
            for dst, src in ((idf, ident), (prow, part_of_row), (embr, emb), (colb[:, 0:2], bq), (colb[:, 2:4], bk),
                             (colb[:, 4:5], e_lo), (colb[:, 5:6], e_hi), (bvt, bv)):
                sp.dma_start(dst[:], src).then_inc(s_const, 16)
            sp.wait_ge(s_zero, 1)
            for p in range(2):
                for h in range(G):
                    sp.dma_start(tab[p, h].rearrange("(t p) n -> p t n", p=P)[:, :, PADL + NJ:TW],
                                 zero[:, :].rearrange("p (t n) -> p t n", n=P)).then_inc(s_pads, 16)

            def store_values(b, hf):
                k = 2 * b + hf
                hold(sp, a_v, 2 * k + 2)
                for g in range(4):
                    dst = vd[bass.ds(4 * b + g, 1), hf * HALF:(hf + 1) * HALF, :].rearrange("i (t p) n -> (i p) t n", p=P)
                    sp.dma_start(dst, vs[:, hf, :, 4 * g:4 * g + 4, :].rearrange("p t h r -> p t (h r)")).then_inc(a_out[hf], 16)

            def store_parts(b, hf):
                k = 2 * b + hf
                for n in range(8):
                    if n == 6:
                        store_values(b, hf)
                    if n < 6:
                        hold(sp, a_low, 6 * k + n + 1)
                    else:
                        hold(sp, a_mix, 4 * k + 2 * (n - 6) + 2)
                    dst = td[n // 2][bass.ds(2 * b + n % 2, 1)].rearrange("a t g r n -> (a g r) t n")[:, :, hf * HALF:(hf + 1) * HALF]
                    sp.dma_start(dst, part[:, hf, n, :, :]).then_inc(a_out[hf], 16)

            load_x(0, 1, False)
            store_parts(0, 0)
            with sp.Fori(1, B) as b:
                load_x(b, 0)
                store_parts(b - 1, 1)
                load_x(b, 1)
                store_parts(b, 0)
            store_parts(B - 1, 1)
            for hf in range(2):
                sp.wait_ge(a_out[hf], 16 * A_DMAS * B)
            sp.wait_ge(s_pads, 16 * NPADS)

            def parts(t, i, par):
                return t[bass.ds((i - par) // 2, 1), :, par].rearrange("a t (r h) n -> (a t) r (h n)", h=G)

            def load_q(dst, i, par, s):
                t = parts(td[0], i, par)
                for r0, n in ((0, 3), (3, 2), (5, 1)):
                    sp.dma_start(dst[HD * r0:HD * (r0 + n)].rearrange("p h n -> p (h n)"), t[0:n]).then_inc(s, 16)

            def load_k(dst, t, i, par, s):
                t = parts(t, i, par)
                for p, r0, n in ((0, 0, 3), (1, 3, 2), (2, 5, 1)):
                    sp.dma_start(dst[HD * r0:HD * (r0 + n)].rearrange("p h n -> p (h n)"),
                                 t[p:p + 1].to_broadcast([n, HD, G * L])).then_inc(s, 16)

            def load_rel_q(i, par):
                load_q(qR[:, par], i, par, ld_r[par])

            def load_qk(i, par):
                load_q(qT[:, par], i, par, ld_q[par])
                for v in range(3):
                    load_k(kT[:, par, v], td[1 + v], i, par, ld_k[par])

            def load_v(i, par):
                sp.dma_start(vS[:, par, :, :], row(vd, i).rearrange("(t p) n -> p t n", p=P)).then_inc(ld_k[par], 16)

            def load_windows(par, part):
                for h in range(G):
                    first = ((par * G + h) * L + part * HALF) * TW + P
                    src = bass.AP(tab.tensor, first, [[TW - 1, P], [P * TW, 4], [1, WIN]])
                    sp.dma_start(win[:, par, 4 * part:4 * part + 4, h, ZL:], src).then_inc((ld_lo, ld_hi)[part][par], 16)

            def store_rows(n, par, qt):
                hold(sp, r_padded, n + 1)
                dst = tab[par].rearrange("h (t p) n -> t p h n", p=P)[qt, :, :, 0:PADL + NJ]
                sp.dma_start(dst, rows[:, qt % NR, :, :]).then_inc(t_wr[qt % NR], 16)

            def store_attn(i, hf, m):
                hold(sp, an_ready, m + 1)
                dst = row(ad, i)[hf * HALF:(hf + 1) * HALF, :].rearrange("(t p) n -> p t n", p=P)
                sp.dma_start(dst, an[:]).then_inc(an_out, 16)

            load_rel_q(0, 0)
            load_rel_q(1, 1)
            load_q(qT[:, 0], 0, 0, ld_q[0])
            for qt in range(TL):
                sp.wait_ge(r_rows, qt + 1)
                store_rows(qt, 0, qt)
                if qt in (1, 3, 5):
                    load_k(kT[:, 0, qt // 2], td[1 + qt // 2], 0, 0, ld_k[0])
            for p in range(NR):
                sp.wait_ge(t_wr[p], 16 * (TL // NR))
            load_windows(0, 0)
            load_v(0, 0)
            load_windows(0, 1)
            for qt in range(TL):
                store_rows(TL + qt, 1, qt)
            load_rel_q(2, 0)

            def group(i, par, k, first=False, rel=True, last=False, ahead=True):
                if not last:
                    if not first:
                        hold(sp, pv_done, STEPS * i)
                    for p in range(NR):
                        hold(sp, t_wr[p], 16 * (TL // NR) * (i + 2))
                    load_windows(1 - par, 0)
                    load_qk(i + 1, 1 - par)
                    load_v(i + 1, 1 - par)
                if rel:
                    hold(sp, ld_lo[par], 16 * LW * (k + 1))
                    hold(sp, ld_hi[par], 16 * LW * (k + 1))
                for hf in range(2):
                    for t in range(16):
                        if t == N_STEP + 1 and not (first and hf == 0):
                            store_attn(i if hf else i - 1, 1 - hf, 2 * i + hf - 1)
                        if t in R_STEPS and rel:
                            qt = 4 * hf + R_STEPS[t]
                            store_rows(TL * (i + 2) + qt, par, qt)
                        if hf == 0 and not last:
                            if t == 6:
                                load_windows(1 - par, 1)
                        if hf == 0 and t == 12 and ahead:
                            hold(sp, r_full, TL * (i + 2))
                            load_rel_q(i + 3, 1 - par)

            run_groups(sp, group)
            store_attn(NIT - 1, 1, 2 * NIT - 1)
            sp.wait_ge(an_out, 16 * 2 * NIT)

        @block.gpsimd
        def _(pool):
            nc.gpsimd.memset(zero[:], 0.0).then_inc(s_zero, 1)
            nc.gpsimd.memset(vs[:], 0.0).then_inc(s_ones, 1)
            pool.wait_ge(s_ones, 1)
            nc.gpsimd.memset(vs[:, :, :, :, HD:HD + 1], 1.0).then_inc(s_ones, 1)

            def pad_rows(n, qt):
                hold(pool, r_rows, n + 1)
                nc.gpsimd.tensor_copy(rows[:, qt % NR, :, 0:PADL],
                                      rows[:, qt % NR, :, PADL:PADL + 1].to_broadcast([P, G, PADL])).then_inc(r_padded, 1)

            def cast_window(T, par, k, part, q4, wait_use=True):
                hold(pool, (ld_lo, ld_hi)[part][par], 16 * LW * (k + 1))
                if wait_use:
                    hold(pool, mx_full, T_CH * (T - 2) + 8 * (q4 + 1))
                nc.gpsimd.tensor_copy(winb[:, part, q4, :, :], win[:, par, 4 * part + q4, :, ZL:]).then_inc(wb_ready, 1)

            cast_window(0, 0, 0, 0, 0, False)
            cast_window(0, 0, 0, 0, 1, False)
            for q4 in range(2, 4):
                for qt in (2 * q4 - 4, 2 * q4 - 3):
                    pad_rows(TL + qt, qt)
                cast_window(0, 0, 0, 0, q4, False)
            cast_window(1, 0, 0, 1, 0, False)
            for qt in range(4, TL):
                pad_rows(TL + qt, qt)

            def group(i, par, k, first=False, rel=True, last=False, ahead=True):
                for hf in range(2):
                    T = 2 * i + hf
                    for t in range(16):
                        if t in (0, 3, 6) and not (last and hf):
                            tp, tk = (par, k) if hf == 0 else (1 - par, k + par)
                            cast_window(T + 1, tp, tk, 1 - hf, 1 + t // 3, not first or hf == 1)
                        if t == 10 and not last:
                            cast_window(T + 2, 1 - par, k + par, hf, 0)
                        if t in R_STEPS and rel:
                            qt = 4 * hf + R_STEPS[t]
                            pad_rows(TL * (i + 2) + qt, qt)

            run_groups(pool, group)

        @block.scalar
        def _(act):
            act.wait_ge(s_prep, 3)

            def project(b, hf, before, again):
                k = 2 * b + hf
                if again:
                    act.wait_ge(a_out[hf], 16 * A_DMAS * b)
                    act.wait_ge(a_low, 6 * (k - 1))

                def value(n):
                    act.wait_ge(a_full, 6 * k + 1 + n)
                    nc.scalar.activation(val[:, hf, n, :], psT[:, n, :], ACT.Identity, bias=colc[:, n:n + 1],
                                         scale=0.25 if n < 2 else 1.0).then_inc(a_val, 1)

                def high(n):
                    if n < 4:
                        act.wait_ge(a_val, 4 * k + 1 + n)
                    else:
                        act.wait_ge(a_hi_val, 2 * k + n - 3)
                    nc.scalar.activation(part[:, hf, n, 0, :], val[:, hf, n, :], ACT.Copy).then_inc(a_high, 1)

                def middle(n):
                    act.wait_ge(a_rem, 6 * k + 1 + n)
                    nc.scalar.activation(part[:, hf, n, 1, :], rem[:, hf, n, :], ACT.Copy).then_inc(a_mid, 1)

                value(0)
                value(1)
                high(0)
                high(1)
                value(2)
                value(3)
                for n in range(2, 6):
                    middle(n - 2)
                    high(n)
                middle(4)
                middle(5)

            run_blocks(act, project)
            for hf in range(2):
                act.wait_ge(a_out[hf], 16 * A_DMAS * B)
            act.wait_ge(s_pads, 16 * NPADS)

            def copy_rows(n, qt, tw, pad=False):
                act.wait_ge(r_full, n + 1)
                if not (isinstance(tw, int) and tw == 0):
                    act.wait_ge(t_wr[qt % NR], 16 * tw)
                if pad:
                    first = psM[:, 0:G * NJ].rearrange("p (h n) -> p h n", h=G)[:, :, 0:1]
                    nc.scalar.activation(rows[:, qt % NR, :, 0:PADL], first.to_broadcast([P, G, PADL]), ACT.Copy).then_inc(r_padded, 1)
                nc.scalar.activation(rows[:, qt % NR, :, PADL:PADL + NJ],
                                     psM[:, 0:G * NJ].rearrange("p (h n) -> p h n", h=G), ACT.Copy).then_inc(r_rows, 1)

            def exps(i, s, first):
                act.wait_ge(st_done, STEPS * i + s + 1)
                if not (first and s < NP_BUF):
                    act.wait_ge(pv_done, STEPS * i + s + 1 - NP_BUF)
                hp = s % 2
                nc.scalar.activation(pr[:, s % NP_BUF, :], psT[:, 2 * hp:2 * hp + 2, :].rearrange("p a n -> p (a n)"),
                                     ACT.Exp).then_inc(exp_done, 1)

            def place_max(T, par, part, q4, i):
                act.wait_ge(m_turned, 4 * T + q4 + 1)
                if i is not None:
                    act.wait_ge(st_done, 16 * (T - 1))
                to = qT[96:98, par, :, part * HALF + q4 * P:part * HALF + (q4 + 1) * P]
                nc.scalar.activation(to, psM[96:98, :].rearrange("p (h n) -> p h n", h=G), ACT.Copy).then_inc(qm_ready, 1)

            def copy_out(T):
                act.wait_ge(pv_done, 16 * (T + 1))
                if not (isinstance(T, int) and T == 0):
                    act.wait_ge(o_turned, T)
                nc.scalar.activation(ot[:], psO[:], ACT.Copy).then_inc(o_copied, 1)

            for qt in range(TL):
                copy_rows(qt, qt, qt // NR, True)
            for q4 in range(4):
                for qt in (2 * q4, 2 * q4 + 1):
                    copy_rows(TL + qt, qt, TL // NR + qt // NR)
                place_max(0, 0, 0, q4, None)

            def group(i, par, k, first=False, rel=True, last=False, ahead=True):
                for hf in range(2):
                    for t in range(16):
                        exps(i, 16 * hf + t, first)
                        if t in M_STEPS and not (last and hf):
                            place_max(2 * i + hf + 1, par if hf == 0 else 1 - par, 1 - hf, M_STEPS[t],
                                      None if first and hf == 0 else i)
                        if t == 0 and not (first and hf == 0):
                            copy_out(2 * i + hf - 1)
                        if t in R_STEPS and rel:
                            qt = 4 * hf + R_STEPS[t]
                            copy_rows(TL * (i + 2) + qt, qt, TL // NR * (i + 2) + qt // NR)

            run_groups(act, group)
            copy_out(2 * NIT - 1)

        @block.vector
        def _(dve):
            small = [0]

            def link(ins):
                small[0] += 1
                ins.then_inc(s_dve, 1)
                dve.wait_ge(s_dve, small[0])

            dve.wait_ge(s_const, 16 * NCONST)
            nc.vector.tensor_scalar(colc[:, 0:2], colb[:, 0:2], 0.25, None, ALU.mult).then_inc(s_prep, 1)
            nc.vector.tensor_scalar(colc[:, 2:4], colb[:, 2:4], colb[:, 4:5], None, ALU.add).then_inc(s_prep, 1)
            nc.vector.tensor_scalar(colc[:, 4:6], colb[:, 2:4], colb[:, 5:6], None, ALU.add).then_inc(s_prep, 1)
            link(nc.vector.tensor_tensor(embd[:], embr[:, 0:NJ], embr[:, NJ:NJ + 1].to_broadcast([KR, NJ]), ALU.subtract))
            left = embd[:]
            for p in range(3):
                link(nc.vector.tensor_copy(embp[:, p, :], left))
                if p < 2:
                    link(nc.vector.tensor_tensor(embt[:, p, :], left, embp[:, p, :], ALU.subtract))
                    left = embt[:, p, :]
            link(nc.vector.tensor_scalar(embt[:, 2, :], embp[:, 0, :], prow[:, 0:1], None, ALU.mult))
            link(nc.vector.scalar_tensor_tensor(embt[:, 0, :], embp[:, 1, :], prow[:, 1:2], embt[:, 2, :], ALU.mult, ALU.add))
            link(nc.vector.scalar_tensor_tensor(embS[:], embp[:, 2, :], prow[:, 2:3], embt[:, 0, :], ALU.mult, ALU.add))
            nc.vector.tensor_copy(idb[:], idf[:]).then_inc(s_prep, 1)
            dve.wait_ge(s_ones, 2)

            def project(b, hf, before, again):
                k = 2 * b + hf
                if again:
                    dve.wait_ge(a_out[hf], 16 * A_DMAS * b)
                    dve.wait_ge(a_mid, 6 * (k - 1))

                def k_hi(m):
                    dve.wait_ge(a_val, 4 * k + 3 + m)
                    nc.vector.tensor_scalar(val[:, hf, 4 + m, :], psT[:, 2 + m, :], colc[:, 4 + m:5 + m], None,
                                            ALU.add).then_inc(a_hi_val, 1)

                def remainder(n):
                    dve.wait_ge(a_high, 6 * k + 1 + n)
                    nc.vector.tensor_tensor(rem[:, hf, n, :], val[:, hf, n, :], part[:, hf, n, 0, :], ALU.subtract).then_inc(a_rem, 1)

                def low(n):
                    dve.wait_ge(a_mid, 6 * k + 1 + n)
                    nc.vector.tensor_tensor(part[:, hf, n, 2, :], rem[:, hf, n, :], part[:, hf, n, 1, :], ALU.subtract).then_inc(a_low, 1)

                remainder(0)
                remainder(1)
                k_hi(0)
                k_hi(1)
                for v in range(2):
                    dve.wait_ge(a_full, 6 * k + 5 + v)
                    for e in range(2):
                        last = nc.vector.tensor_tensor(
                            vs[:, hf, 2 * v + e, :, 0:HD],
                            psX[:, v, e * D:(e + 1) * D].rearrange("p (h d) -> p h d", d=HD),
                            bvt[:].rearrange("p (h d) -> p h d", d=HD), ALU.add)
                    last.then_inc(a_v, 1)
                for n in range(2, 6):
                    low(n - 2)
                    remainder(n)
                low(4)
                low(5)
                dve.wait_ge(a_low, 6 * k + 6)
                for m in range(2):
                    for v in range(2):
                        halves = [part[:, hf, n, :, :].rearrange("p t (q n) -> p (t q) n", n=P)[:, :, v * ZL:(v + 1) * ZL]
                                  for n in (6 + m, 2 + 2 * v + m)]
                        nc.vector.tensor_copy(halves[0], halves[1]).then_inc(a_mix, 1)

            run_blocks(dve, project)
            for hf in range(2):
                dve.wait_ge(a_out[hf], 16 * A_DMAS * B)
            dve.wait_ge(s_pads, 16 * NPADS)
            for par in range(2):
                nc.vector.memset(win[:, par, :, :, 0:ZL], 0.0).then_inc(s_bufs, 1)
            nc.vector.memset(mcol[:], 0.0).then_inc(s_bufs, 1)
            for par in range(2):
                nc.vector.memset(kT[KR:KR + 2, par], 1.0).then_inc(s_bufs, 1)

            def reduce(T, part, c, q4, kh, h):
                n = T_CH * T + c
                dve.wait_ge(mx_full, n + 1)
                nc.vector.tensor_reduce(nmax[:, part, q4, kh, h:h + 1], psX[:, c % 2, :], AX.X, ALU.max,
                                        negate=True).then_inc(mx_free, 1)
                if c % 8 == 7:
                    m = 4 * T + q4
                    dve.wait_ge(mx_free, n + 1)
                    nc.vector.tensor_tensor(mval[:], nmax[:, part, q4, 0, :], nmax[:, part, q4, 1, :],
                                            ALU.min).then_inc(m_small, 1)
                    if not (isinstance(T, int) and m == 0):
                        dve.wait_ge(m_turned, m)
                    dve.wait_ge(m_small, 2 * m + 1)
                    nc.vector.tensor_copy(mcol[:, :, 0], mval[:]).then_inc(m_small, 1)
                    dve.wait_ge(m_small, 2 * m + 2)
                    nc.vector.tensor_tensor(mcol[:, :, 1], mval[:], mcol[:, :, 0], ALU.subtract).then_inc(m_ready, 1)

            def chunk(T, part, c):
                reduce(T, part, c, c // 8, c // 4 % 2, c % 4)

            def normalise(T):
                dve.wait_ge(o_turned, T + 1)
                o = psM[:].rearrange("p (g r) -> p g r", r=32)
                nc.vector.reciprocal(orec[:], o[:, :, HD]).then_inc(o_rec, 1)
                dve.wait_ge(o_rec, T + 1)
                if not (isinstance(T, int) and T == 0):
                    dve.wait_ge(an_out, 16 * T)
                nc.vector.tensor_tensor(an[:].rearrange("p q (h d) -> p (q h) d", d=HD), o[:, :, 0:HD],
                                        orec[:].unsqueeze(2).to_broadcast([P, 16, HD]), ALU.mult).then_inc(an_ready, 1)

            for c in range(T_CH):
                chunk(0, 0, c)
            for c in range(LEAD):
                chunk(1, 1, c)

            def group(i, par, k, first=False, rel=True, last=False, ahead=True):
                for hf in range(2):
                    T = 2 * i + hf
                    for t in range(16):
                        if t == N_STEP + 1 and not (first and hf == 0):
                            normalise(T - 1)
                        for ahead, c in chunks_at(t):
                            if not (last and hf + ahead >= 1):
                                chunk(T + 1 + ahead, (hf + 1 + ahead) % 2, c)

            run_groups(dve, group)
            normalise(2 * NIT - 1)

        @block.tensor
        def _(pe):
            mm = nc.tensor.matmul
            pe.wait_ge(s_w, 16 * 3)

            def project(b, hf, before, again):
                k = 2 * b + hf
                pe.wait_ge(a_x[hf], 16 * (b + 1))
                if before:
                    pe.wait_ge(a_val, 4 * k)
                for w, bank in ((wq, 0), (wk, 2)):
                    if bank and before:
                        pe.wait_ge(a_hi_val, 2 * k)
                    for m in range(2):
                        for c in range(2):
                            last = mm(psT[:, bank + m, :], w[:, c, m * P:(m + 1) * P], xs[:, hf, c, :],
                                      start=(c == 0), stop=(c == 1))
                        last.then_inc(a_full, 1)
                if before:
                    pe.wait_ge(a_v, 2 * k)
                for v in range(2):
                    for e in range(2):
                        t = 2 * v + e
                        for c in range(2):
                            last = mm(psX[:, v, e * D:(e + 1) * D], xs[:, hf, c, t * P:(t + 1) * P], wv[:, c, :],
                                      start=(c == 0), stop=(c == 1))
                    last.then_inc(a_full, 1)

            run_blocks(pe, project)
            pe.wait_ge(a_val, 8 * B)
            pe.wait_ge(a_hi_val, 4 * B)
            pe.wait_ge(a_v, 4 * B)

            def misc_bank(R, M, O):
                pe.wait_ge(r_rows, R)
                if M is not None:
                    pe.wait_ge(qm_ready, M)
                if O is not None:
                    pe.wait_ge(an_ready, O)

            def make_rows(n, par, k, qt, M, O=None):
                if qt == 0:
                    pe.wait_ge(ld_r[par], 16 * LQ * (k + 1))
                misc_bank(n, M, O)
                for h in range(G):
                    last = mm(psM[:, h * NJ:(h + 1) * NJ], qR[0:KR, par, h, qt * P:(qt + 1) * P], embS[:],
                              start=True, stop=True)
                last.then_inc(r_full, 1)

            def max_chunk(T, part, par, k, c, begun=True):
                q4, kh, h = c // 8, c // 4 % 2, c % 4
                qt = 4 * part + q4
                if c == 0:
                    pe.wait_ge(ld_q[par], 16 * LQ * (k + 1))
                    pe.wait_ge(ld_k[par], 16 * LK * (k + 1))
                if c % 8 == 0:
                    pe.wait_ge(wb_ready, 4 * T + q4 + 1)
                if begun:
                    pe.wait_ge(mx_free, T_CH * T + c - 1)
                lo = kh * HALF
                bank = psX[:, c % 2, :]
                ps = by_key(qt, kh)
                w0, w1 = max(qt * P - LEFT, lo), min(qt * P + P + RIGHT, lo + HALF)
                near = w0 < w1
                for n, (a, e, v) in enumerate(ps):
                    last = mm(bank[:, a - lo:e - lo], qT[0:KR, par, h, qt * P:(qt + 1) * P], kT[0:KR, par, v, h, a:e],
                              start=(n == 0), stop=not near and n == len(ps) - 1, skip_group_check=True)
                if near:
                    u = w0 - (qt * P - LEFT)
                    last = mm(bank[:, w0 - lo:w1 - lo], idb[:], winb[:, part, q4, h, u:u + w1 - w0],
                              start=False, stop=True, skip_group_check=True)
                last.then_inc(mx_full, 1)

            def turn_max(m, R, O=None):
                pe.wait_ge(m_ready, m + 1)
                misc_bank(R, m, O)
                for h in range(G):
                    last = mm(psM[96:P, h * P:(h + 1) * P], mcol[:, h, :], idb[:], start=True, stop=True)
                last.then_inc(m_turned, 1)

            def scores(i, par, s, first):
                hf, kt, hp = s // 16, s % 16 // 2, s % 2
                if s % 16 == 0:
                    pe.wait_ge(qm_ready, 4 * (2 * i + hf + 1))
                if not (first and s < 2):
                    pe.wait_ge(exp_done, STEPS * i + s - 1)
                lo = hf * HALF
                ps = by_query(kt, hf)
                near = [(qt, c0, w) for qt, c0, w in ((kt + 1, 0, P), (kt, P, P), (kt - 1, 2 * P, RIGHT))
                        if 4 * hf <= qt < 4 * hf + 4]
                for n, (a, e, v) in enumerate(ps):
                    for h in (2 * hp, 2 * hp + 1):
                        last = mm(psT[:, h, a - lo:e - lo], kT[0:KR + 2, par, v, h, kt * P:(kt + 1) * P], qT[0:KR + 2, par, h, a:e],
                                  start=(n == 0), stop=not near and n == len(ps) - 1, skip_group_check=True)
                for n, (qt, c0, w) in enumerate(near):
                    for h in (2 * hp, 2 * hp + 1):
                        if w == P:
                            last = mm(psT[:, h, qt * P - lo:(qt + 1) * P - lo], win[:, par, qt, h, c0:c0 + w], idf[:],
                                      is_transpose=True, start=False, stop=n == len(near) - 1, skip_group_check=True)
                        else:
                            last = mm(psT[0:w, h, (qt + 1) * P - w - lo:(qt + 1) * P - lo], win[:, par, qt, h, c0:c0 + w],
                                      idf[:, P - w:P], start=False, stop=n == len(near) - 1, skip_group_check=True)
                last.then_inc(st_done, 1)

            def weigh(i, par, s, first):
                hf, kt = s // 16, s % 16 // 2
                pe.wait_ge(exp_done, STEPS * i + s + 2)
                if s % 16 == 0 and not (first and hf == 0):
                    pe.wait_ge(o_copied, 2 * i + hf)
                for h in range(G):
                    last = mm(psO[32 * h:32 * h + 32, :], vS[:, par, kt, 32 * h:32 * h + 32],
                              pr[:, (s + h // 2) % NP_BUF, h % 2 * HALF:(h % 2 + 1) * HALF], start=(kt == 0), stop=(kt == TL - 1))
                last.then_inc(pv_done, 2)

            def turn_out(T, R, M, O=None):
                pe.wait_ge(o_copied, T + 1)
                misc_bank(R, M, O)
                for q in range(4):
                    last = nc.tensor.transpose(psM[:, q * P:(q + 1) * P], ot[:, q * P:(q + 1) * P], idf[:])
                last.then_inc(o_turned, 1)

            pe.wait_ge(s_prep, 4)
            for qt in range(TL):
                make_rows(qt, 0, 0, qt, None)
            pe.wait_ge(s_bufs, 3)
            for c in range(T_CH):
                max_chunk(0, 0, 0, 0, c, c >= 2)
                if c % 4 == 1:
                    make_rows(TL + c // 4, 1, 0, c // 4, c // 8 if c >= 8 else None)
                if c % 8 == 7:
                    turn_max(c // 8, TL + 2 * (c // 8) + 2)
            for c in range(LEAD):
                max_chunk(1, 1, 0, 0, c)
            pe.wait_ge(s_bufs, 5)

            def group(i, par, k, first=False, rel=True, last=False, ahead=True):
                for hf in range(2):
                    T = 2 * i + hf
                    for t in range(16):
                        s = 16 * hf + t
                        scores(i, par, s, first)
                        for e, (ahead, c) in enumerate(chunks_at(t)):
                            if e == 1 and s % 2 == 0:
                                if s >= 2:
                                    weigh(i, par, s - 2, first)
                                elif not first:
                                    weigh(i - 1, 1 - par, STEPS + s - 2, False)
                            if not (last and hf + ahead >= 1):
                                same = hf + 1 + ahead < 2
                                max_chunk(T + 1 + ahead, (hf + 1 + ahead) % 2, par if same else 1 - par,
                                          k if same else k + par, c)
                        outs = None if first and hf == 0 or first and t <= N_STEP else T if t > N_STEP else T - 1
                        tabs = TL * (i + 2) + 4 * hf + sum(u < t for u in R_STEPS) if rel else TL * NIT
                        turns = 4 * (T + 1) + sum(u < t for u in M_STEPS) if not (last and hf) else 8 * NIT
                        if t in R_STEPS and rel:
                            qt = 4 * hf + R_STEPS[t]
                            make_rows(tabs, par, k + 1, qt, turns, outs)
                        if t in M_STEPS and not (last and hf):
                            turn_max(turns, tabs, outs)
                        if t == N_STEP and not (first and hf == 0):
                            turn_out(T - 1, tabs, turns, outs)

            run_groups(pe, group)
            weigh(NIT - 1, 1, STEPS - 2, False)
            turn_out(2 * NIT - 1, TL * NIT, 8 * NIT, 2 * NIT - 1)



def decoder_rest(nc, sem, ad, x, ident, woT, bo, ctxT, xwq, xwkT, xwvT, xbq, xbk, xbv, w_up, w_gate, w_down, out):
    h2d = nc.dram_tensor("second_norm", [NBLK, HALF, D], F32, kind="Internal").ap()
    ud = nc.dram_tensor("up_raw", [NBLK, P, FT * HALF], F32, kind="Internal").ap()
    s_held = sem("f_held")

    def hold(eng, s, value):
        eng.wait_ge(s, value)
        eng.sem_inc(s_held, 1)

    def tokens(t, n):
        return t[bass.ds(n, 1)].rearrange("a (q p) d -> p (a q) d", p=P)

    with ExitStack() as ctx:
        def sb(name, shape, dt=F32):
            return ctx.enter_context(nc.sbuf_tensor(name, shape, dt))

        idf = sb("ident_f", [P, P])
        wuT = sb("w_upT", [P, 2, FI])
        wgT = sb("w_gateT", [P, 2, FI])
        wdT = sb("w_downT", [P, FT, D])
        neg_half = sb("neg_half", [P, 1])
        amax = sb("amax", [P, NSC, NBLK])
        top = sb("top", [P, NSC])
        top_all = sb("top_all", [P, NSC])
        step = sb("step", [P, NSC])
        inv = sb("inv", [P, NSC])
        stats = sb("stats", [P, 4, 4, 6])
        mv = sb("mean_var", [P, 4, 4, 2])
        rstd = sb("rstd", [P, 4, 4])
        shift = sb("shift", [P, 4, 4])
        magic = sb("magic", [P, 2])
        coarse = sb("coarse", [P, 1])
        ps = ctx.enter_context(nc.psum_tensor("banks", [P, 8, HALF], F32))

        l_sum = sem("l_sum")
        l_stat = sem("l_stat")
        l_aggr = sem("l_aggr")
        l_eps = sem("l_eps")
        l_rstd = sem("l_rstd")
        s_half = sem("s_half")
        t_top = sem("t_top")
        t_all = sem("t_all")
        t_step = sem("t_step")
        t_coarse = sem("t_coarse")
        t_inv = sem("t_inv")

        def norm_stats(dve, i, hf, h):
            hold(dve, l_sum, i + 1)
            for q in range(4):
                last = nc.vector.bn_stats(stats[:, hf, q, :], h[:, q, :])
            last.then_inc(l_stat, 1)
            hold(dve, l_stat, i + 1)
            for q in range(4):
                last = nc.vector.bn_aggr(mv[:, hf, q, :], stats[:, hf, q, :])
            last.then_inc(l_aggr, 1)

        def norm_rstd(pool, i, hf):
            hold(pool, l_aggr, i + 1)
            nc.gpsimd.tensor_scalar(rstd[:, hf, :], mv[:, hf, :, 1], EPS, None, ALU.add).then_inc(l_eps, 1)
            nc.gpsimd.tensor_scalar(shift[:, hf, :], mv[:, hf, :, 0], -1.0, None, ALU.mult).then_inc(l_eps, 1)
            hold(pool, l_eps, 3 * i + 2)
            nc.gpsimd.tensor_tensor(rstd[:, hf, :], rstd[:, hf, :], neg_half[:].to_broadcast([P, 4]), ALU.pow).then_inc(l_eps, 1)
            hold(pool, l_eps, 3 * i + 3)
            nc.gpsimd.tensor_tensor(shift[:, hf, :], shift[:, hf, :], rstd[:, hf, :], ALU.mult).then_inc(l_rstd, 1)

        def norm_scalar(act, i, hf, h, to):
            hold(act, l_rstd, i + 1)
            for q in range(4):
                last = nc.scalar.activation(to[:, q, :], h[:, q, :], ACT.Identity, bias=shift[:, hf, q:q + 1],
                                            scale=rstd[:, hf, q:q + 1])
            return last

        def norm_apply(dve, i, hf, h, to):
            hold(dve, l_rstd, i + 1)
            for q in range(4):
                last = nc.vector.tensor_scalar(to[:, q, :], h[:, q, :], mv[:, hf, q, 0:1], rstd[:, hf, q:q + 1],
                                               ALU.subtract, ALU.mult)
            return last

        def largest_of(dve, k):
            nc.vector.tensor_reduce(top[:, k:k + 1], amax[:, k, :], AX.X, ALU.max).then_inc(t_top, 1)

        def scale_of(dve, k, unit=1.0, coarse=None):
            dve.wait_ge(t_all, k + 1)
            largest = top_all[:, k:k + 1]
            if coarse is not None:
                nc.vector.tensor_tensor(largest, largest, coarse, ALU.mult).then_inc(t_coarse, 1)
                dve.wait_ge(t_coarse, 2)
            nc.vector.tensor_scalar(step[:, k:k + 1], largest, 1.0 / QMAX, TINY * unit, ALU.mult, ALU.max).then_inc(t_step, 1)
            dve.wait_ge(t_step, k + 1)
            nc.vector.reciprocal(inv[:, k:k + 1], step[:, k:k + 1]).then_inc(t_inv, 1)
            if coarse is not None:
                dve.wait_ge(t_inv, k + 1)
                nc.vector.tensor_tensor(inv[:, k:k + 1], inv[:, k:k + 1], coarse, ALU.mult).then_inc(t_inv, 1)

        def scale_pool(pool, k):
            pool.wait_ge(t_top, k + 1)
            nc.gpsimd.partition_all_reduce(top_all[:, k:k + 1], top[:, k:k + 1], P, RMAX).then_inc(t_all, 1)

        cross_attention(nc, sem, hold, tokens, ad, x, ident, woT, bo, ctxT, xwq, xwkT, xwvT, xbq, xbk, xbv,
                        w_up, w_gate, w_down, h2d, idf, wuT, wgT, wdT, neg_half, magic, s_half, amax, ps,
                        l_sum, norm_stats, norm_rstd, norm_scalar)

        with ExitStack() as feed:
            raw = feed.enter_context(nc.sbuf_tensor("raw", [P, NBLK, FT * HALF], F32))
            ub = feed.enter_context(nc.sbuf_tensor("ub", [P, 2, FT * HALF], F32))
            with ExitStack() as first:
                xqT = first.enter_context(nc.sbuf_tensor("xqT", [P, 2, NBLK, HALF], F32))
                project_gate(nc, sem, hold, tokens, h2d, idf, wgT, magic, step, inv, t_inv, ps, xqT, raw, amax, largest_of, scale_of, scale_pool)
                project_up(nc, sem, hold, wuT, ud, magic, step, inv, t_inv, ps, xqT, raw, ub, amax, largest_of, scale_of, scale_pool)
            down(nc, sem, hold, tokens, h2d, ud, wdT, magic, coarse, t_coarse, step, inv, t_inv, ps, raw, ub, amax,
                 largest_of, scale_of, scale_pool, l_sum, norm_stats, norm_rstd, norm_apply, out)


def cross_attention(nc, sem, hold, tokens, ad, x, ident, woT, bo, ctxT, xwq, xwkT, xwvT, xbq, xbk, xbv,
                    w_up, w_gate, w_down, h2d, idf, wuT, wgT, wdT, neg_half, magic, s_half, amax, ps,
                    l_sum, norm_stats, norm_rstd, norm_scalar):
    with ExitStack() as ctx:
        def sb(name, shape, dt=F32):
            return ctx.enter_context(nc.sbuf_tensor(name, shape, dt))

        wo = sb("wo", [P, 2, D])
        xq_w = sb("xq_w", [P, 2, D])
        xk_w = sb("xk_w", [P, 2, D])
        xv_w = sb("xv_w", [P, 2, D])
        bot = sb("bot", [P, D])
        bvt = sb("xbvt", [P, D])
        bqk = sb("bqk", [P, 4])
        cT = sb("cT", [P, 2, B, LC])
        kx = sb("kx", [P, 2, B, LC])
        kq = sb("kq", [P, 2, B, LC])
        kb = sb("kb", [1, B, LC])
        ones = sb("ones", [1, P])
        vx = sb("vx", [P, 2, B, D])
        at = sb("at", [P, 2, 4, D])
        xt = sb("xt", [P, 2, 4, D])
        atT = sb("atT", [P, 2, 2, HALF])
        h = sb("h", [P, 2, 4, D])
        h1 = sb("h1", [P, 2, 4, D])
        h1T = sb("h1T", [P, 2, 2, HALF])
        hr = sb("hr", [P, 2, 4, D])
        nm = sb("nm", [P, 2, 4])
        e = sb("e", [P, 2, 4, LC])
        esum = sb("esum", [P, 2, 4])
        erec = sb("erec", [P, 2, 4])
        eT = sb("eT", [P, 2, 2, HALF])
        g = sb("g", [P, 2, 4, D])
        h2 = sb("h2", [P, 2, 4, D])
        wn = [sb(f"wn{j}", [P, FT * D]) for j in range(3)]
        ws = [sb(f"ws{j}", [P, FT * D // 32]) for j in range(3)]
        wi = [sb(f"wi{j}", [P, FT * D // 32]) for j in range(3)]

        c_key = sem("c_key")
        c_in = sem("c_in")
        ld = [sem(f"d_ld{j}") for j in range(2)]
        d_st = [sem(f"d_st{j}") for j in range(2)]
        d_t1 = sem("d_t1")
        d_atT = sem("d_atT")
        d_y = sem("d_y")
        d_bo = sem("d_bo")
        d_h1 = sem("d_h1")
        d_t2 = sem("d_t2")
        d_h1T = sem("d_h1T")
        d_hr = sem("d_hr")
        c_q = sem("c_q")
        c_m = sem("c_m")
        d_s = sem("d_s")
        d_nm = sem("d_nm")
        d_e = sem("d_e")
        d_t3 = sem("d_t3")
        d_eT = sem("d_eT")
        d_a = sem("d_a")
        d_rec = sem("d_rec")
        d_h2 = sem("d_h2")
        d_am = sem("d_am")
        c_kv = sem("c_kv")
        c_k = sem("c_k")
        c_v = sem("c_v")
        w_in = [sem(f"w_in{j}") for j in range(3)]
        w_top = sem("w_top")
        w_inv = sem("w_inv")
        w_s = sem("w_s")
        w_over = sem("w_over")
        w_round = sem("w_round")
        w_deq = sem("w_deq")
        w_turn = sem("w_turn")
        w_copy = sem("w_copy")

        block = ctx.enter_context(nc.Block())
        NC_IN = 6
        TAIL = LC - P

        def front_norm(b, hf):
            return hf if isinstance(b, int) and b == 0 else 4 * b - 2 + hf

        def back_norm(b, hf, more):
            return 4 * b + 4 + hf if more else 4 * b + 2 + hf

        def run_steps(eng, step_of):
            step_of(0, False, True)
            step_of(1, True, True)
            with eng.Fori(2, B - 1) as b:
                step_of(b, True, True)
            step_of(B - 1, True, False)

        @block.sync
        def _(sp):
            sp.dma_start(cT[:].rearrange("p c b t -> p c (b t)"), ctxT.rearrange("(c p) n -> p c n", p=P)).then_inc(c_key, 16)
            sp.dma_start(xk_w[:], xwkT.rearrange("(c p) n -> p c n", p=P)).then_inc(c_key, 16)
            sp.dma_start(bqk[:, 0:2], xbq).then_inc(c_key, 16)
            sp.dma_start(bqk[:, 2:4], xbk).then_inc(c_key, 16)
            for to, w in ((xv_w, xwvT), (xq_w, xwq), (wo, woT)):
                sp.dma_start(to[:], w.rearrange("(c p) n -> p c n", p=P)).then_inc(c_in, 16)
            sp.dma_start(bvt[:], xbv).then_inc(c_in, 16)
            sp.dma_start(bot[:], bo).then_inc(c_in, 16)
            sp.dma_start(idf[:], ident).then_inc(c_in, 16)

            def load(b, before=True):
                for hf in range(2):
                    n = 2 * b + hf
                    if before:
                        hold(sp, d_t1, n - 1)
                        hold(sp, d_h1, n - 1)
                    for gr in range(4):
                        sp.dma_start(at[:, hf, :, gr * G * HD:(gr + 1) * G * HD],
                                     ad[bass.ds(4 * b + gr, 1), hf * HALF:(hf + 1) * HALF, :].rearrange(
                                         "a (q p) d -> p (a q) d", p=P)).then_inc(ld[hf], 16)
                    sp.dma_start(xt[:, hf], tokens(x, n)).then_inc(ld[hf], 16)

            def store(b):
                for hf in range(2):
                    hold(sp, d_h2, 2 * b + hf + 1)
                    sp.dma_start(tokens(h2d, 2 * b + hf), h2[:, hf]).then_inc(d_st[hf], 16)

            load(0, False)
            for j, w in enumerate((w_up, w_gate)):
                sp.dma_start(wn[j][:].rearrange("p (t d) -> p t d", d=D), w.rearrange("(t p) d -> p t d", p=P)).then_inc(w_in[j], 16)
            sp.dma_start(wn[2][:].rearrange("p (t d) -> p t d", d=FI), w_down.rearrange("(t p) d -> p t d", p=P)).then_inc(w_in[2], 16)
            load(1)
            with sp.Fori(2, B) as b:
                load(b)
                store(b - 2)
            store(B - 2)
            store(B - 1)
            for hf in range(2):
                sp.wait_ge(d_st[hf], 16 * B)

        @block.gpsimd
        def _(pool):
            nc.gpsimd.memset(magic[:, 0:1], MAGIC)
            nc.gpsimd.memset(magic[:, 1:2], -MAGIC)
            nc.gpsimd.memset(ones[:], 1.0)
            nc.gpsimd.memset(neg_half[:], -0.5).then_inc(s_half, 1)
            pool.wait_ge(s_half, 1)
            def front(b):
                for hf in range(2):
                    hold(pool, ld[hf], 16 * 5 * (b + 1))
                    nc.gpsimd.tensor_tensor(xt[:, hf], xt[:, hf], bot[:].unsqueeze(1).to_broadcast([P, 4, D]), ALU.add).then_inc(d_bo, 1)
                for hf in range(2):
                    norm_rstd(pool, front_norm(b, hf), hf)

            pool.wait_ge(c_in, 16 * NC_IN)
            front(0)
            with pool.Fori(0, B - 1) as b:
                front(b + 1)
                for hf in range(2):
                    norm_rstd(pool, back_norm(b, hf, True), 2 + hf)
            for hf in range(2):
                norm_rstd(pool, back_norm(B - 1, hf, False), 2 + hf)

        @block.scalar
        def _(act):
            act.wait_ge(c_key, 16 * 4)
            for m in range(2):
                for j in range(2):
                    act.wait_ge(c_kv, 2 * m + j + 1)
                    last = nc.scalar.activation(kx[:, m, 2 * j:2 * j + 2, :].rearrange("p b t -> p (b t)"),
                                                ps[:, 2 * m + j, 0:2 * LC], ACT.Identity, bias=bqk[:, 2 + m:3 + m])
                    last.then_inc(c_k, 1)
            for m in range(2):
                for j in range(2):
                    act.wait_ge(c_q, 2 * m + j + 1)
                    nc.scalar.activation(kq[:, m, 2 * j:2 * j + 2, :].rearrange("p b t -> p (b t)"),
                                         ps[:, 2 * m + j, 0:2 * LC], ACT.Copy)
            for j in range(2):
                last = nc.scalar.activation(kb[:, 2 * j:2 * j + 2, :].rearrange("p b t -> p (b t)"), ps[0:1, 4 + j, 0:2 * LC], ACT.Copy)
            last.then_inc(c_m, 1)

            def copy_front(b, hf):
                hold(act, d_t1, 2 * b + hf + 1)
                nc.scalar.activation(atT[:, hf], ps[:, 2 * hf:2 * hf + 2, :], ACT.Copy).then_inc(d_atT, 1)

            def norm_back(b, again, more):
                for hf in range(2):
                    if again:
                        hold(act, d_st[hf], 16 * b)
                        hold(act, d_am, 2 * b + hf - 1)
                    norm_scalar(act, back_norm(b, hf, more), 2 + hf, g[:, hf], h2[:, hf]).then_inc(d_h2, 1)

            def step_of(b, before, more):
                for hf in range(2):
                    hold(act, d_t2, 2 * b + hf + 1)
                    nc.scalar.activation(h1T[:, hf], ps[:, 2 * hf:2 * hf + 2, :], ACT.Copy).then_inc(d_h1T, 1)
                for hf in range(2):
                    if before:
                        hold(act, l_sum, back_norm(b - 1, hf, True) + 1)
                    nc.scalar.activation(hr[:, hf], h1[:, hf], ACT.Copy).then_inc(d_hr, 1)
                if before:
                    norm_back(b - 1, not (isinstance(b, int) and b == 1), True)
                for hf in range(2):
                    hold(act, d_nm, 2 * b + hf + 1)
                    for q in range(4):
                        o = (q % 2) * D
                        last = nc.scalar.activation(e[:, hf, q, :], ps[:, 4 + 2 * hf + q // 2, o:o + LC], ACT.Exp,
                                                    bias=nm[:, hf, q:q + 1], accum_out=esum[:, hf, q:q + 1])
                    last.then_inc(d_e, 1)
                    if more:
                        copy_front(b + 1, hf)
                for hf in range(2):
                    hold(act, d_t3, 2 * b + hf + 1)
                    nc.scalar.activation(eT[:, hf, 0, :], ps[:, 2 * hf, :], ACT.Copy)
                    nc.scalar.activation(eT[0:TAIL, hf, 1, :], ps[0:TAIL, 2 * hf + 1, :], ACT.Copy).then_inc(d_eT, 1)
                if more:
                    for hf in range(2):
                        norm_scalar(act, front_norm(b + 1, hf), hf, h[:, hf], h1[:, hf]).then_inc(d_h1, 1)

            for hf in range(2):
                copy_front(0, hf)
            for hf in range(2):
                norm_scalar(act, hf, hf, h[:, hf], h1[:, hf]).then_inc(d_h1, 1)
            run_steps(act, step_of)
            for j, to in enumerate((wuT, wgT, wdT)):
                w = to[:].rearrange("p a b -> p (a b)")
                for k in range(3):
                    act.wait_ge(w_turn, 3 * j + k + 1)
                    nc.scalar.activation(w[:, k * HALF:(k + 1) * HALF], ps[:, (3 * j + k) % 4, :], ACT.Copy).then_inc(w_copy, 1)
            norm_back(B - 1, True, False)

        @block.vector
        def _(dve):
            dve.wait_ge(c_in, 16 * NC_IN)
            dve.wait_ge(c_kv, 5)
            for b in range(B):
                nc.vector.tensor_tensor(vx[:, 0, b, :], ps[:, 4 + b // 2, (b % 2) * D:(b % 2 + 1) * D], bvt[:], ALU.add)
                last = nc.vector.tensor_tensor(vx[0:TAIL, 1, b, :], ps[0:TAIL, 6 + b // 2, (b % 2) * D:(b % 2 + 1) * D],
                                               bvt[0:TAIL, :], ALU.add)
            last.then_inc(c_v, 1)
            def dequantise(j):
                v = wn[j][:].rearrange("p (n k) -> p n k", k=32)
                dve.wait_ge(w_in[j], 16)
                nc.vector.tensor_reduce(ws[j][:], v, AX.X, ALU.max, apply_absolute_value=True).then_inc(w_top, 1)
                dve.wait_ge(w_top, j + 1)
                nc.vector.tensor_scalar(ws[j][:], ws[j][:], 1.0 / 7.0, TINY, ALU.mult, ALU.max).then_inc(w_s, 1)
                dve.wait_ge(w_s, j + 1)
                nc.vector.reciprocal(wi[j][:], ws[j][:]).then_inc(w_inv, 1)
                dve.wait_ge(w_inv, j + 1)
                nc.vector.tensor_tensor(v, v, wi[j][:].unsqueeze(2).to_broadcast([P, FT * D // 32, 32]),
                                        ALU.mult).then_inc(w_over, 1)
                dve.wait_ge(w_over, j + 1)
                nc.vector.tensor_scalar(wn[j][:], wn[j][:], MAGIC, MAGIC, ALU.add, ALU.subtract).then_inc(w_round, 1)
                dve.wait_ge(w_round, j + 1)
                nc.vector.tensor_tensor(v, v, ws[j][:].unsqueeze(2).to_broadcast([P, FT * D // 32, 32]),
                                        ALU.mult).then_inc(w_deq, 1)

            def largest(b):
                for hf in range(2):
                    n = 2 * b + hf
                    hold(dve, d_h2, n + 1)
                    nc.vector.tensor_reduce(amax[:, 0, bass.ds(n, 1)], h2[:, hf].rearrange("p q d -> p (q d)"), AX.X, ALU.max,
                                            apply_absolute_value=True).then_inc(d_am, 1)

            def sum_front(b, hf):
                n = 2 * b + hf
                hold(dve, d_bo, n + 1)
                hold(dve, d_y, n + 1)
                nc.vector.tensor_tensor(h[:, hf].rearrange("p q d -> p (q d)"),
                                        ps[:, 4 + 2 * hf:6 + 2 * hf, :].rearrange("p a n -> p (a n)"),
                                        xt[:, hf].rearrange("p q d -> p (q d)"), ALU.add).then_inc(l_sum, 1)
                norm_stats(dve, front_norm(b, hf), hf, h[:, hf])

            def step_of(b, before, more):
                for hf in range(2):
                    hold(dve, d_s, 2 * b + hf + 1)
                    v = ps[:, 4 + 2 * hf:6 + 2 * hf, :].rearrange("p a (c n) -> p (a c) n", n=D)
                    nc.vector.tensor_reduce(nm[:, hf, :], v[:, :, 0:LC], AX.X, ALU.max, negate=True).then_inc(d_nm, 1)
                if not before:
                    dequantise(0)
                else:
                    largest(b - 1)
                if more:
                    for hf in range(2):
                        sum_front(b + 1, hf)
                if not before:
                    dequantise(1)
                for hf in range(2):
                    n = 2 * b + hf
                    hold(dve, d_e, n + 1)
                    nc.vector.reciprocal(erec[:, hf, :], esum[:, hf, :]).then_inc(d_rec, 1)
                    hold(dve, d_rec, n + 1)
                    hold(dve, d_hr, n + 1)
                    hold(dve, d_a, n + 1)
                    for q in range(4):
                        o = (q % 2) * D
                        last = nc.vector.scalar_tensor_tensor(g[:, hf, q, :], ps[:, 4 + 2 * hf + q // 2, o:o + D],
                                                              erec[:, hf, q:q + 1], hr[:, hf, q, :], ALU.mult, ALU.add)
                    last.then_inc(l_sum, 1)
                    norm_stats(dve, back_norm(b, hf, more), 2 + hf, g[:, hf])
                if not before:
                    dequantise(2)

            for hf in range(2):
                sum_front(0, hf)
            run_steps(dve, step_of)
            largest(B - 1)

        @block.tensor
        def _(pe):
            mm = nc.tensor.matmul
            tr = nc.tensor.transpose
            pe.wait_ge(c_key, 16 * 4)
            for m in range(2):
                for j in range(2):
                    for c in range(2):
                        last = mm(ps[:, 2 * m + j, 0:2 * LC], xk_w[:, c, m * P:(m + 1) * P],
                                  cT[:, c, 2 * j:2 * j + 2, :].rearrange("p b t -> p (b t)"), start=(c == 0), stop=(c == 1))
                    last.then_inc(c_kv, 1)
            pe.wait_ge(c_in, 16 * NC_IN)
            for b in range(B):
                for w, lo, hi in ((0, 0, P), (1, P, LC)):
                    for c in range(2):
                        last = mm(ps[0:hi - lo, 4 + 2 * w + b // 2, (b % 2) * D:(b % 2 + 1) * D], cT[:, c, b, lo:hi], xv_w[:, c, :],
                                  start=(c == 0), stop=(c == 1))
            last.then_inc(c_kv, 1)
            pe.wait_ge(c_k, 4)
            pe.wait_ge(c_v, 1)
            for m in range(2):
                for j in range(2):
                    for c in range(2):
                        last = mm(ps[:, 2 * m + j, 0:2 * LC], xq_w[:, c, m * P:(m + 1) * P],
                                  kx[:, c, 2 * j:2 * j + 2, :].rearrange("p b t -> p (b t)"), start=(c == 0), stop=(c == 1))
                    if m == 1:
                        for c in range(2):
                            last = mm(ps[0:1, 4 + j, 0:2 * LC], bqk[:, c:c + 1],
                                      kx[:, c, 2 * j:2 * j + 2, :].rearrange("p b t -> p (b t)"), start=(c == 0), stop=(c == 1))
                    last.then_inc(c_q, 1)
            pe.wait_ge(c_m, 1)
            pe.wait_ge(s_half, 1)

            def turn_front(b, hf):
                hold(pe, ld[hf], 16 * 5 * (b + 1))
                for c in range(2):
                    for q in range(4):
                        last = tr(ps[:, 2 * hf + c, q * P:(q + 1) * P], at[:, hf, q, c * P:(c + 1) * P], idf[:])
                last.then_inc(d_t1, 1)

            def project_out(b, hf, before=True):
                hold(pe, d_atT, 2 * b + hf + 1)
                if before:
                    hold(pe, d_e, 2 * b + hf - 1)
                for q in range(4):
                    for c in range(2):
                        last = mm(ps[:, 4 + 2 * hf + q // 2, (q % 2) * D:(q % 2 + 1) * D], atT[:, hf, c, q * P:(q + 1) * P],
                                  wo[:, c, :], start=(c == 0), stop=(c == 1))
                last.then_inc(d_y, 1)

            def step_of(b, before, more):
                for hf in range(2):
                    hold(pe, d_h1, 2 * b + hf + 1)
                    for c in range(2):
                        for q in range(4):
                            last = tr(ps[:, 2 * hf + c, q * P:(q + 1) * P], h1[:, hf, q, c * P:(c + 1) * P], idf[:])
                    last.then_inc(d_t2, 1)
                for hf in range(2):
                    hold(pe, d_h1T, 2 * b + hf + 1)
                    if before:
                        hold(pe, l_sum, back_norm(b - 1, hf, True) + 1)
                    for q in range(4):
                        o = (q % 2) * D
                        to = ps[:, 4 + 2 * hf + q // 2, o:o + LC]
                        for c in range(2):
                            mm(to, h1T[:, hf, c, q * P:(q + 1) * P], kq[:, c, bass.ds(b, 1), :].rearrange("p a t -> p (a t)"),
                               start=(c == 0), stop=False)
                        last = mm(to, ones[:], kb[:, bass.ds(b, 1), :].rearrange("p a t -> p (a t)"), start=False, stop=True)
                    last.then_inc(d_s, 1)
                if more:
                    for hf in range(2):
                        turn_front(b + 1, hf)
                    for hf in range(2):
                        project_out(b + 1, hf)
                for hf in range(2):
                    hold(pe, d_e, 2 * b + hf + 1)
                    for q in range(4):
                        tr(ps[:, 2 * hf, q * P:(q + 1) * P], e[:, hf, q, 0:P], idf[:])
                        last = tr(ps[0:TAIL, 2 * hf + 1, q * P:(q + 1) * P], e[:, hf, q, P:LC], idf[:])
                    last.then_inc(d_t3, 1)
                for hf in range(2):
                    hold(pe, d_eT, 2 * b + hf + 1)
                    if more:
                        hold(pe, l_sum, front_norm(b + 1, hf) + 1)
                    for q in range(4):
                        to = ps[:, 4 + 2 * hf + q // 2, (q % 2) * D:(q % 2 + 1) * D]
                        mm(to, eT[:, hf, 0, q * P:(q + 1) * P], vx[:, 0, bass.ds(b, 1), :].rearrange("p a d -> p (a d)"),
                           start=True, stop=False)
                        last = mm(to, eT[0:TAIL, hf, 1, q * P:(q + 1) * P],
                                  vx[0:TAIL, 1, bass.ds(b, 1), :].rearrange("p a d -> p (a d)"), start=False, stop=True)
                    last.then_inc(d_a, 1)

            for hf in range(2):
                turn_front(0, hf)
            for hf in range(2):
                project_out(0, hf, False)
            run_steps(pe, step_of)
            for j in range(3):
                pe.wait_ge(w_deq, j + 1)
                for k in range(3):
                    bank = 3 * j + k
                    if bank >= 4:
                        pe.wait_ge(w_copy, bank - 3)
                    for u in range(4):
                        v = 4 * k + u
                        if j < 2:
                            c, t = v // FT, v % FT
                            src = wn[j][:, t * D + c * P:t * D + (c + 1) * P]
                        else:
                            t, c = v // 2, v % 2
                            src = wn[j][:, c * FI + t * P:c * FI + (t + 1) * P]
                        last = tr(ps[:, bank % 4, u * P:(u + 1) * P], src, idf[:])
                    last.then_inc(w_turn, 1)

def run_pairs(eng, body):
    body(0, 0, False)
    body(1, 1, False)
    with eng.Fori(1, NBLK // 2) as j:
        body(2 * j, 0, True)
        body(2 * j + 1, 1, True)


def run_kept_first(eng, body):
    body(0, NBLK - 2, 0, True)
    body(1, NBLK - 1, 1, True)
    with eng.Fori(0, NBLK // 2 - 1) as j:
        for par in range(2):
            body(2 * j + 2 + par, 2 * j + par, par)


def flat(t, n):
    return t[:, bass.ds(n, 1), :].rearrange("p a n -> p (a n)")


def project_gate(nc, sem, hold, tokens, h2d, idf, wgT, magic, step, inv, t_inv, ps, xqT, raw, amax, largest_of, scale_of, scale_pool):
    with ExitStack() as ctx:
        hb = ctx.enter_context(nc.sbuf_tensor("hb", [P, 2, 4, D], F32))
        f_ld = [sem(f"f_ld{j}") for j in range(2)]
        f_x = sem("f_x")
        f_xq = sem("f_xq")
        f_t = sem("f_t")
        f_xqT = sem("f_xqT")
        f_g = sem("f_g")
        f_gc = sem("f_gc")
        f_ga = sem("f_ga")
        block = ctx.enter_context(nc.Block())

        @block.sync
        def _(sp):
            def load(n, par, before):
                if before:
                    hold(sp, f_t, n - 1)
                sp.dma_start(hb[:, par], tokens(h2d, n)).then_inc(f_ld[par], 16)

            run_pairs(sp, load)

        @block.gpsimd
        def _(pool):
            scale_pool(pool, 0)
            scale_pool(pool, 1)

        @block.scalar
        def _(act):
            act.wait_ge(t_inv, 1)

            def quantise(n, par):
                hold(act, f_ld[par], 16 * (n // 2 + 1))
                nc.scalar.activation(hb[:, par], hb[:, par], ACT.Identity, bias=magic[:, 0:1], scale=inv[:, 0:1]).then_inc(f_x, 1)

            def copy(n, par):
                hold(act, f_t, n + 1)
                nc.scalar.activation(xqT[:, :, bass.ds(n, 1), :].rearrange("p c a n -> p c (a n)"),
                                     ps[:, 6:8, :], ACT.Copy).then_inc(f_xqT, 1)

            def copy_gate(n):
                for m in range(FT):
                    hold(act, f_g, FT * n + m + 1)
                    nc.scalar.activation(raw[:, bass.ds(n, 1), m * HALF:(m + 1) * HALF].rearrange("p a n -> p (a n)"),
                                         ps[:, m, :], ACT.Copy).then_inc(f_gc, 1)

            quantise(0, 0)
            copy(0, 0)
            quantise(1, 1)
            copy(1, 1)
            with act.Fori(0, NBLK // 2 - 1) as j:
                for par in range(2):
                    quantise(2 * j + 2 + par, par)
                    copy_gate(2 * j + par)
                    copy(2 * j + 2 + par, par)
            copy_gate(NBLK - 2)
            copy_gate(NBLK - 1)

        @block.vector
        def _(dve):
            largest_of(dve, 0)
            scale_of(dve, 0)

            def quantise(n, par):
                hold(dve, f_x, n + 1)
                nc.vector.tensor_scalar(hb[:, par], hb[:, par], MAGIC, step[:, 0:1], ALU.subtract, ALU.mult).then_inc(f_xq, 1)

            def largest(n):
                hold(dve, f_gc, FT * n + FT)
                nc.vector.tensor_reduce(amax[:, 1, bass.ds(n, 1)], flat(raw, n), AX.X, ALU.max,
                                        apply_absolute_value=True).then_inc(f_ga, 1)

            quantise(0, 0)
            quantise(1, 1)
            with dve.Fori(0, NBLK // 2 - 1) as j:
                for par in range(2):
                    quantise(2 * j + 2 + par, par)
                    largest(2 * j + par)
            largest(NBLK - 2)
            largest(NBLK - 1)
            dve.wait_ge(f_ga, NBLK)
            largest_of(dve, 1)
            scale_of(dve, 1)

        @block.tensor
        def _(pe):
            mm = nc.tensor.matmul

            def turn(n, par, before):
                hold(pe, f_xq, n + 1)
                if before:
                    hold(pe, f_xqT, n)
                for c in range(2):
                    for q in range(4):
                        last = nc.tensor.transpose(ps[:, 6 + c, q * P:(q + 1) * P], hb[:, par, q, c * P:(c + 1) * P], idf[:])
                last.then_inc(f_t, 1)

            def products(n, before):
                hold(pe, f_xqT, n + 1)
                for m in range(FT):
                    if before:
                        hold(pe, f_gc, FT * (n - 1) + m + 1)
                    for c in range(2):
                        last = mm(ps[:, m, :], wgT[:, c, m * P:(m + 1) * P],
                                  xqT[:, c, bass.ds(n, 1), :].rearrange("p a n -> p (a n)"), start=(c == 0), stop=(c == 1))
                    last.then_inc(f_g, 1)

            turn(0, 0, False)
            turn(1, 1, True)
            products(0, False)
            turn(2, 0, True)
            products(1, True)
            turn(3, 1, True)
            with pe.Fori(1, NBLK // 2 - 1) as j:
                for par in range(2):
                    products(2 * j + par, True)
                    turn(2 * j + 2 + par, par, True)
            products(NBLK - 2, True)
            products(NBLK - 1, True)


def project_up(nc, sem, hold, wuT, ud, magic, step, inv, t_inv, ps, xqT, raw, ub, amax, largest_of, scale_of, scale_pool):
    with ExitStack() as ctx:
        sg = ctx.enter_context(nc.sbuf_tensor("sg", [P, 2, FT * HALF], F32))
        u_full = sem("u_full")
        u_copied = sem("u_copied")
        u_max = sem("u_max")
        u_st = [sem(f"u_st{j}") for j in range(2)]
        g_r = sem("g_r")
        g_q = sem("g_q")
        g_sig = sem("g_sig")
        g_clip = sem("g_clip")
        g_sr = sem("g_sr")
        g_g2 = sem("g_g2")
        g_a2 = sem("g_a2")
        block = ctx.enter_context(nc.Block())

        @block.sync
        def _(sp):
            def store(n, par):
                hold(sp, u_copied, FT * n + FT)
                sp.dma_start(ud[bass.ds(n, 1)].rearrange("a p n -> (a p) n"), ub[:, par]).then_inc(u_st[par], 16)

            with sp.Fori(0, NBLK // 2 - 1) as j:
                for par in range(2):
                    store(2 * j + par, par)
            for par in range(2):
                sp.wait_ge(u_st[par], 16 * (NBLK // 2 - 1))

        @block.gpsimd
        def _(pool):
            scale_pool(pool, 2)
            scale_pool(pool, 3)

        @block.scalar
        def _(act):
            def round_gate(n):
                nc.scalar.activation(flat(raw, n), flat(raw, n), ACT.Identity, bias=magic[:, 0:1], scale=inv[:, 1:2]).then_inc(g_r, 1)

            def step_of(n, par, before, more=True):
                if more:
                    round_gate(n + 1)
                if before:
                    hold(act, u_st[par], 16 * (n // 2))
                    hold(act, u_max, n - 1)
                for m in range(FT):
                    if m == 0:
                        hold(act, g_q, n + 1)
                        if before:
                            hold(act, g_g2, n - 1)
                        nc.scalar.activation(sg[:, par], flat(raw, n), ACT.Sigmoid).then_inc(g_sig, 1)
                    if m == 3:
                        hold(act, g_clip, n + 1)
                        nc.scalar.activation(sg[:, par], sg[:, par], ACT.Identity, bias=magic[:, 0:1]).then_inc(g_sr, 1)
                    hold(act, u_full, FT * n + m + 1)
                    nc.scalar.activation(ub[:, par, m * HALF:(m + 1) * HALF], ps[:, m, :], ACT.Copy).then_inc(u_copied, 1)

            round_gate(0)
            step_of(0, 0, False)
            step_of(1, 1, False)
            with act.Fori(1, NBLK // 2 - 1) as j:
                step_of(2 * j, 0, True)
                step_of(2 * j + 1, 1, True)
            step_of(NBLK - 2, 0, True)
            step_of(NBLK - 1, 1, True, False)

        @block.vector
        def _(dve):
            def dequantise(n):
                hold(dve, g_r, n + 1)
                nc.vector.tensor_scalar(flat(raw, n), flat(raw, n), MAGIC, step[:, 1:2], ALU.subtract, ALU.mult).then_inc(g_q, 1)

            def largest_up(n, par):
                hold(dve, u_copied, FT * n + FT)
                nc.vector.tensor_reduce(amax[:, 3, bass.ds(n, 1)], ub[:, par], AX.X, ALU.max, apply_absolute_value=True).then_inc(u_max, 1)

            def step_of(n, par, before=True, more=True):
                hold(dve, g_sig, n + 1)
                w = sg[:, par]
                nc.vector.tensor_scalar(w, w, U16, U16 - 1.0, ALU.mult, ALU.min).then_inc(g_clip, 1)
                if more:
                    dequantise(n + 1)
                if before:
                    largest_up(n - 1, 1 - par)
                hold(dve, g_sr, n + 1)
                nc.vector.scalar_tensor_tensor(flat(raw, n), w, MAGIC, flat(raw, n), ALU.subtract, ALU.mult).then_inc(g_g2, 1)
                hold(dve, g_g2, n + 1)
                nc.vector.tensor_reduce(amax[:, 2, bass.ds(n, 1)], flat(raw, n), AX.X, ALU.max, apply_absolute_value=True).then_inc(g_a2, 1)

            dequantise(0)
            step_of(0, 0, False)
            step_of(1, 1)
            with dve.Fori(1, NBLK // 2 - 1) as j:
                step_of(2 * j, 0)
                step_of(2 * j + 1, 1)
            step_of(NBLK - 2, 0)
            step_of(NBLK - 1, 1, True, False)
            dve.wait_ge(g_a2, NBLK)
            largest_of(dve, 2)
            largest_up(NBLK - 1, 1)
            dve.wait_ge(u_max, NBLK)
            largest_of(dve, 3)
            scale_of(dve, 2, U16)
            scale_of(dve, 3)

        @block.tensor
        def _(pe):
            def products(n, before):
                for m in range(FT):
                    if before:
                        hold(pe, u_copied, FT * (n - 1) + m + 1)
                    for c in range(2):
                        last = nc.tensor.matmul(ps[:, m, :], wuT[:, c, m * P:(m + 1) * P],
                                                xqT[:, c, bass.ds(n, 1), :].rearrange("p a n -> p (a n)"), start=(c == 0), stop=(c == 1))
                    last.then_inc(u_full, 1)

            products(0, False)
            with pe.Fori(1, NBLK) as n:
                products(n, True)


def down(nc, sem, hold, tokens, h2d, ud, wdT, magic, coarse, t_coarse, step, inv, t_inv, ps, raw, ub, amax,
         largest_of, scale_of, scale_pool, l_sum, norm_stats, norm_rstd, norm_apply, out):
    with ExitStack() as ctx:
        work = ctx.enter_context(nc.sbuf_tensor("work", [P, 2, FT * HALF], F32))
        res = ctx.enter_context(nc.sbuf_tensor("res", [P, 2, 4, D], F32))
        p_ld = [sem(f"p_ld{j}") for j in range(2)]
        p_g = sem("p_g")
        p_gi = sem("p_gi")
        p_odd = sem("p_odd")
        p_u = sem("p_u")
        p_o = sem("p_o")
        p_a = sem("p_a")
        o_r = sem("o_r")
        o_q = sem("o_q")
        o_ps = sem("o_ps")
        o_fin = sem("o_fin")
        o_ld = [sem(f"o_ld{j}") for j in range(2)]
        o_st = [sem(f"o_st{j}") for j in range(2)]
        block = ctx.enter_context(nc.Block())

        @block.sync
        def _(sp):
            def load_up(n, par):
                hold(sp, p_o, n + 1)
                sp.dma_start(ub[:, par], ud[bass.ds(n, 1)].rearrange("a p n -> (a p) n")).then_inc(p_ld[par], 16)

            with sp.Fori(0, NBLK // 2 - 1) as j:
                for par in range(2):
                    load_up(2 * j + par, par)

            def load(n, par, before):
                if before:
                    hold(sp, o_fin, n - 1)
                    sp.dma_start(tokens(out, n - 2), res[:, par]).then_inc(o_st[par], 16)
                    hold(sp, o_st[par], 16 * (n // 2))
                sp.dma_start(res[:, par], tokens(h2d, n)).then_inc(o_ld[par], 16)

            run_pairs(sp, load)
            for par in range(2):
                sp.wait_ge(o_fin, NBLK - 1 + par)
                sp.dma_start(tokens(out, NBLK - 2 + par), res[:, par]).then_inc(o_st[par], 16)
            for par in range(2):
                sp.wait_ge(o_st[par], 8 * NBLK)

        @block.gpsimd
        def _(pool):
            scale_pool(pool, 4)
            run_pairs(pool, lambda n, par, before: norm_rstd(pool, 2 * NBLK + n, par))

        @block.scalar
        def _(act):
            def multiply(k, n, par, kept=False):
                nc.scalar.activation(flat(raw, n), flat(raw, n), ACT.Identity, bias=magic[:, 0:1], scale=inv[:, 2:3]).then_inc(p_g, 1)
                if not kept:
                    hold(act, p_ld[par], 16 * (n // 2 + 1))
                nc.scalar.activation(ub[:, par], ub[:, par], ACT.Identity, bias=magic[:, 0:1], scale=inv[:, 3:4]).then_inc(p_u, 1)
                if par == 0:
                    hold(act, p_g, k + 1)
                    nc.scalar.activation(flat(raw, n), flat(raw, n), ACT.Identity, bias=magic[:, 1:2]).then_inc(p_gi, 1)

            run_kept_first(act, multiply)
            act.wait_ge(t_inv, NSC + 1)
            with act.Fori(0, NBLK) as n:
                nc.scalar.activation(flat(raw, n), flat(raw, n), ACT.Identity, bias=magic[:, 0:1], scale=inv[:, 4:5]).then_inc(o_r, 1)

        @block.vector
        def _(dve):
            nc.vector.tensor_scalar(coarse[:], step[:, 2:3], step[:, 3:4], 1.0 / U16, ALU.mult, ALU.mult).then_inc(t_coarse, 1)

            def multiply(k, n, par, kept=False):
                if par == 0:
                    hold(dve, p_gi, k // 2 + 1)
                else:
                    hold(dve, p_g, k + 1)
                    nc.vector.tensor_scalar(flat(raw, n), flat(raw, n), MAGIC, None, ALU.subtract).then_inc(p_odd, 1)
                    hold(dve, p_odd, k // 2 + 1)
                hold(dve, p_u, k + 1)
                nc.vector.scalar_tensor_tensor(flat(raw, n), ub[:, par], MAGIC, flat(raw, n), ALU.subtract, ALU.mult).then_inc(p_o, 1)
                hold(dve, p_o, k + 1)
                nc.vector.tensor_reduce(amax[:, 4, bass.ds(n, 1)], flat(raw, n), AX.X, ALU.max, apply_absolute_value=True).then_inc(p_a, 1)

            run_kept_first(dve, multiply)
            dve.wait_ge(p_a, NBLK)
            dve.wait_ge(t_coarse, 1)
            largest_of(dve, 4)
            scale_of(dve, 4, 1.0, coarse[:])

            def down_in(n, par, before):
                hold(dve, o_r, n + 1)
                if before:
                    hold(dve, o_ps, n - 1)
                nc.vector.tensor_scalar(work[:, par], flat(raw, n), MAGIC, step[:, 4:5], ALU.subtract, ALU.mult).then_inc(o_q, 1)

            def finish(n, par):
                hold(dve, o_ps, n + 1)
                hold(dve, o_ld[par], 16 * (n // 2 + 1))
                r = res[:, par]
                nc.vector.tensor_tensor(r.rearrange("p q d -> p (q d)"), ps[:, 2 * par:2 * par + 2, :].rearrange("p a n -> p (a n)"),
                                        r.rearrange("p q d -> p (q d)"), ALU.add).then_inc(l_sum, 1)
                norm_stats(dve, 2 * NBLK + n, par, r)
                norm_apply(dve, 2 * NBLK + n, par, r, r).then_inc(o_fin, 1)

            down_in(0, 0, False)
            down_in(1, 1, False)
            finish(0, 0)
            with dve.Fori(1, NBLK // 2) as j:
                down_in(2 * j, 0, True)
                finish(2 * j - 1, 1)
                down_in(2 * j + 1, 1, True)
                finish(2 * j, 0)
            finish(NBLK - 1, 1)

        @block.tensor
        def _(pe):
            def products(n, par, before):
                hold(pe, o_q, n + 1)
                if before:
                    hold(pe, l_sum, 2 * NBLK + n - 1)
                for q in range(4):
                    for m in range(FT):
                        last = nc.tensor.matmul(ps[:, 2 * par + q // 2, (q % 2) * D:(q % 2 + 1) * D],
                                                work[:, par, m * HALF + q * P:m * HALF + (q + 1) * P], wdT[:, m, :],
                                                start=(m == 0), stop=(m == FT - 1))
                last.then_inc(o_ps, 1)

            run_pairs(pe, products)


def build(nc, xT, wqT, wkT, wvT, bq, bk, bv, emb, part_of_row, e_lo, e_hi, ident,
          x, woT, bo, ctxT, xwq, xwkT, xwvT, xbq, xbk, xbv, w_up, w_gate, w_down, out):
    with ExitStack() as sems:
        def sem(name):
            return sems.enter_context(nc.semaphore(name))

        ad = nc.dram_tensor("attn_all", [NIT, L, G * HD], F32, kind="Internal").ap()
        self_attention(nc, sem, ad, xT, wqT, wkT, wvT, bq, bk, bv, emb, part_of_row, e_lo, e_hi, ident)
        decoder_rest(nc, sem, ad, x, ident, woT, bo, ctxT, xwq, xwkT, xwvT, xbq, xbk, xbv, w_up, w_gate, w_down, out)


def kernel(**inputs):
    import numpy as np
    import concourse.bacc as bacc
    from concourse.bass_utils import run_bass_kernel_spmd

    a = {k: np.asarray(v) for k, v in inputs.items()}
    e = a["L0_attn_dist_emb"]
    part_of_row = np.zeros((KR, 3), np.float32)
    for slot, p in enumerate((0, 0, 0, 1, 1, 2)):
        part_of_row[HD * slot:HD * (slot + 1), p] = 1.0
    ident = np.eye(P, dtype=np.float32)

    def by_dim(w):
        return w.reshape(-1, 2, 2, G, HD).transpose(0, 1, 2, 4, 3).reshape(-1, D)

    arrays = {
        "xT": a["x"].reshape(N, D).T, "wqT": by_dim(a["L0_attn_Wq"].T), "wkT": by_dim(a["L0_attn_Wk"].T), "wvT": a["L0_attn_Wv"].T,
        "bq": by_dim(a["L0_attn_bq"]).reshape(2, P).T, "bk": by_dim(a["L0_attn_bk"]).reshape(2, P).T,
        "bv": np.broadcast_to(a["L0_attn_bv"], (P, D)), "emb": np.tile(e.T, (6, 1)), "part_of_row": part_of_row,
        "e_lo": np.tile(np.repeat(e[0], G), 2).reshape(P, 1), "e_hi": np.tile(np.repeat(e[NJ], G), 2).reshape(P, 1),
        "ident": ident,
        "x": a["x"].reshape(NBLK, HALF, D), "woT": a["L0_attn_Wo"].T, "bo": np.broadcast_to(a["L0_attn_bo"], (P, D)),
        "ctxT": a["ctx_1024"].reshape(B * LC, D).T, "xwq": a["L0_xattn_Wq"], "xwkT": a["L0_xattn_Wk"].T,
        "xwvT": a["L0_xattn_Wv"].T, "xbq": a["L0_xattn_bq"].reshape(2, P).T, "xbk": a["L0_xattn_bk"].reshape(2, P).T,
        "xbv": np.broadcast_to(a["L0_xattn_bv"], (P, D)),
        "w_up": a["L0_ffn_w_up"], "w_gate": a["L0_ffn_w_gate"], "w_down": a["L0_ffn_w_down"],
    }
    nc = bacc.Bacc("TRN2", target_bir_lowering=False, num_devices=1)
    args = []
    for name in arrays:
        arrays[name] = np.ascontiguousarray(arrays[name])
        args.append(nc.dram_tensor(name, arrays[name].shape, mybir.dt.from_np(arrays[name].dtype), kind="ExternalInput").ap())
    args.append(nc.dram_tensor("result", [NBLK, HALF, D], F32, kind="ExternalOutput").ap())
    build(nc, *args)
    r = run_bass_kernel_spmd(nc, [arrays], core_ids=[0])
    return r.results[0]["result"].reshape(B, L, D)
```
